# Optimizing a Trainium2 kernel written in Bass

```python
import numpy as np
import jax
import jax.numpy as jnp

def _softmax(x, axis=-1):
    return jax.nn.softmax(x, axis=axis)

def _gelu(x):
    return jax.nn.gelu(x, approximate=True)

def _silu(x):
    return jax.nn.silu(x)

def _sigmoid(x):
    return jax.nn.sigmoid(x)

def _layernorm(x, axis=-1, eps=1e-05):
    m = jnp.mean(x, axis=axis, keepdims=True)
    v = jnp.var(x, axis=axis, keepdims=True)
    return (x - m) / jnp.sqrt(v + eps)

def _scatter_add(tgt, idx, src, axis=0):
    return tgt.at[idx].add(src)

def _segment_sum(src, seg, n):
    return jax.ops.segment_sum(src, seg, n)
kernel_name = 'mk_perceiver_d1_seqx_r2_57d936'

def setup_inputs(seed: int=0):
    np.random.seed(seed)
    _w = jnp.asarray

    def _rec_inputs():
        import jax
        import jax.numpy as jnp
        _rk = jax.random.key(seed)
        x = -0.0005207 + 1.001 * jax.random.normal(jax.random.fold_in(_rk, 1), (1, 512, 1024), jnp.float32)
        _lenS = 512 - jax.random.randint(jax.random.fold_in(_rk, 7), (1,), 0, max(1, 512 // 4) + 1, jnp.int32)
        _lenS2 = 8192 - jax.random.randint(jax.random.fold_in(_rk, 8), (1,), 0, max(1, 8192 // 4) + 1, jnp.int32)
        _ctx_2048P = jax.random.normal(jax.random.fold_in(_rk, 12), (1, 16, 1024), jnp.float32)
        _ctx_2048c = jax.random.dirichlet(jax.random.fold_in(_rk, 512), 0.3 * jnp.ones((16,), jnp.float32), (1, 8192))
        _ctx_2048t = jnp.einsum('bsk,bkd->bsd', _ctx_2048c, _ctx_2048P)
        _ctx_2048t = _ctx_2048t * jax.lax.rsqrt(jnp.mean(jnp.square(_ctx_2048t)) + 1e-12) * 0.953939
        ctx_2048 = -5.72187e-05 + 0.999849 * (_ctx_2048t + 0.3 * jax.random.normal(jax.random.fold_in(_rk, 612), (1, 8192, 1024), jnp.float32))
        _validS = jnp.arange(512)[None, :] < _lenS[:, None]
        _validS2 = jnp.arange(8192)[None, :] < _lenS2[:, None]
        _causal = jnp.tril(jnp.ones((512, 512), dtype=bool))
        mask_BxSx4224_bf0 = jnp.logical_not(jnp.ones((1, 512, 2112), dtype=bool))
        return (x, ctx_2048, mask_BxSx4224_bf0)
    x, ctx_2048, mask_BxSx4224_bf0 = _rec_inputs()

    def _L0_xattn_setup():
        import jax, jax.numpy as jnp
        import numpy as np
        import math
        DIM = 1024
        B, Q_LEN, KV_LEN = (8, 128, 2048)
        key = jax.random.key(seed)
        ks = jax.random.split(key, 8)
        x = jax.random.normal(ks[0], (B, Q_LEN, DIM), dtype=jnp.float32)
        mask = jnp.zeros((B, Q_LEN, KV_LEN + Q_LEN), dtype=bool)
        k_cache = jax.random.normal(ks[1], (B, KV_LEN, DIM), dtype=jnp.float32)
        v_cache = jax.random.normal(ks[2], (B, KV_LEN, DIM), dtype=jnp.float32)
        scale = 1.0 / math.sqrt(DIM)
        wq = jax.random.normal(ks[3], (DIM, DIM), dtype=jnp.float32) * scale
        wk = jax.random.normal(ks[4], (DIM, DIM), dtype=jnp.float32) * scale
        wv = jax.random.normal(ks[5], (DIM, DIM), dtype=jnp.float32) * scale
        wo = jax.random.normal(ks[6], (DIM, DIM), dtype=jnp.float32) * scale
        return {'x': x, 'mask': mask, 'k_cache': k_cache, 'v_cache': v_cache, 'wq': wq, 'wk': wk, 'wv': wv, 'wo': wo}
    _L0_xattn_all = _L0_xattn_setup()
    _L0_xattn_in = {k: v for k, v in _L0_xattn_all.items() if k in ('wq', 'wk', 'wv', 'wo')}
    del _L0_xattn_all

    def _L0_attn_setup():
        import jax, jax.numpy as jnp
        import numpy as np
        import math
        HIDDEN = 1024
        NUM_HEADS = 16
        HEAD_DIM = HIDDEN // NUM_HEADS
        BATCH = 2
        SEQ = 2048
        BLOCK = 128
        TOPK = 64
        NEG = -1000000000.0

        def _split_heads(x):
            n, t, _ = x.shape
            return x.reshape(n, t, NUM_HEADS, HEAD_DIM).transpose(0, 2, 1, 3)

        def _local_attention(q, k, v):
            n, h, t, d = q.shape
            nb = t // BLOCK
            half = BLOCK // 2
            qb = q.reshape(n, h, nb, BLOCK, d)
            win = jnp.arange(nb)[:, None] * BLOCK - half + jnp.arange(2 * BLOCK)[None, :]
            valid = (win >= 0) & (win < t)
            winc = jnp.clip(win, 0, t - 1)
            kb = k[:, :, winc, :]
            vb = v[:, :, winc, :]
            scores = jnp.einsum('nhbqd,nhbkd->nhbqk', qb, kb) / math.sqrt(d)
            scores = jnp.where(valid[None, None, :, None, :], scores, NEG)
            probs = jax.nn.softmax(scores, axis=-1)
            ctx = jnp.einsum('nhbqk,nhbkd->nhbqd', probs, vb)
            return ctx.reshape(n, h, t, d)

        def _global_index(q):
            n, h, t, d = q.shape
            norm = jnp.linalg.norm(q, axis=-1)
            _, top_idx = jax.lax.top_k(norm, TOPK - 2)
            bos = jnp.zeros((n, h, 1), jnp.int32)
            eos = jnp.full((n, h, 1), t - 1, jnp.int32)
            return jnp.concatenate([bos, top_idx.astype(jnp.int32), eos], axis=-1)
        key = jax.random.key(seed)
        ks = jax.random.split(key, 7)
        s = 1.0 / math.sqrt(HIDDEN)
        return {'hidden_states': jax.random.normal(ks[0], (BATCH, SEQ, HIDDEN), jnp.float32), 'Wq': jax.random.normal(ks[1], (HIDDEN, HIDDEN), jnp.float32) * s, 'bq': jnp.zeros((HIDDEN,), jnp.float32), 'Wk': jax.random.normal(ks[2], (HIDDEN, HIDDEN), jnp.float32) * s, 'bk': jnp.zeros((HIDDEN,), jnp.float32), 'Wv': jax.random.normal(ks[3], (HIDDEN, HIDDEN), jnp.float32) * s, 'bv': jnp.zeros((HIDDEN,), jnp.float32)}
    _L0_attn_all = _L0_attn_setup()
    _L0_attn_in = {k: v for k, v in _L0_attn_all.items() if k in ('Wq', 'bq', 'Wk', 'bk', 'Wv', 'bv')}
    del _L0_attn_all

    def _L0_ffn_setup():
        import jax, jax.numpy as jnp
        import numpy as np
        D_MODEL = 1024
        NUM_TILES = 64
        D_SLICE = D_MODEL // NUM_TILES
        TILES_PER_CLUSTER = 8
        NUM_CLUSTERS = NUM_TILES // TILES_PER_CLUSTER
        GRID = 16
        LN_EPS = 1e-05
        DIMS = (np.arange(NUM_TILES)[:, None] * D_SLICE + np.arange(D_SLICE)[None, :]) % D_MODEL
        DIMS = jnp.asarray(DIMS, dtype=jnp.int32)

        def _forward(x, ln_gamma, ln_beta, spline_bases, spline_slopes, output_scale):
            B, S, D = x.shape
            N = B * S
            mu = jnp.mean(x, axis=-1, keepdims=True)
            var = jnp.mean(jnp.square(x - mu), axis=-1, keepdims=True)
            xn = (x - mu) * jax.lax.rsqrt(var + LN_EPS) * ln_gamma + ln_beta
            xf = xn.reshape(N, D)
            slope_sign = jnp.sign(jnp.mean(spline_slopes, axis=-1))
            tile_sigs = jnp.zeros((NUM_TILES, D), dtype=x.dtype)
            tile_sigs = tile_sigs.at[jnp.arange(NUM_TILES)[:, None], DIMS].set(slope_sign)
            cluster_sigs = jnp.sign(tile_sigs.reshape(NUM_CLUSTERS, TILES_PER_CLUSTER, D).mean(axis=1))
            cluster_assign = jnp.arange(NUM_TILES, dtype=jnp.int32) // TILES_PER_CLUSTER
            input_sigs = jnp.sign(xf)
            cluster_scores = input_sigs @ cluster_sigs.T
            best_cluster = jnp.argmax(cluster_scores, axis=-1)
            tile_scores = input_sigs @ tile_sigs.T
            in_cluster = cluster_assign[None, :] == best_cluster[:, None]
            tile_idx = jnp.argmax(jnp.where(in_cluster, tile_scores, -jnp.inf), axis=-1)
            tok_dims = DIMS[tile_idx]
            x_slice = jnp.take_along_axis(xf, tok_dims, axis=1)
            tok_min = x_slice.min(axis=1)
            tok_max = x_slice.max(axis=1)
            onehot = tile_idx[None, :] == jnp.arange(NUM_TILES)[:, None]
            tile_min = jnp.where(onehot, tok_min[None, :], jnp.inf).min(axis=1)
            tile_max = jnp.where(onehot, tok_max[None, :], -jnp.inf).max(axis=1)
            mn = tile_min[tile_idx][:, None]
            mx = tile_max[tile_idx][:, None]
            u = jnp.clip((x_slice - mn) / (mx - mn + 1e-08), 0.0, 1.0 - 1e-06)
            gi = jnp.clip((u * GRID).astype(jnp.int32), 0, GRID - 1)
            j = jnp.arange(D_SLICE)[None, :]
            b = spline_bases[tile_idx[:, None], j, gi]
            s = spline_slopes[tile_idx[:, None], j, gi]
            x_local = (u - gi.astype(u.dtype) / GRID) * GRID
            delta = (b + s * x_local) * output_scale[tile_idx][:, None]
            out = jnp.zeros_like(xf).at[jnp.arange(N)[:, None], tok_dims].set(delta)
            return x + out.reshape(B, S, D)
        key = jax.random.key(seed)
        k1, k2, k3, k4, k5, k6 = jax.random.split(key, 6)
        x = jax.random.normal(k1, (4, 2048, D_MODEL), dtype=jnp.float32)
        ln_gamma = 1.0 + 0.1 * jax.random.normal(k2, (D_MODEL,), dtype=jnp.float32)
        ln_beta = 0.1 * jax.random.normal(k3, (D_MODEL,), dtype=jnp.float32)
        spline_bases = 0.1 * jax.random.normal(k4, (NUM_TILES, D_SLICE, GRID), dtype=jnp.float32)
        spline_slopes = 0.1 + 0.1 * jax.random.normal(k5, (NUM_TILES, D_SLICE, GRID), dtype=jnp.float32)
        output_scale = 1.0 + 0.1 * jax.random.normal(k6, (NUM_TILES,), dtype=jnp.float32)
        return {'x': x, 'ln_gamma': ln_gamma, 'ln_beta': ln_beta, 'spline_bases': spline_bases, 'spline_slopes': spline_slopes, 'output_scale': output_scale}
    _L0_ffn_all = _L0_ffn_setup()
    _L0_ffn_in = {k: v for k, v in _L0_ffn_all.items() if k in ('ln_gamma', 'ln_beta', 'spline_bases', 'spline_slopes', 'output_scale')}
    del _L0_ffn_all
    return {'x': x, 'ctx_2048': ctx_2048, 'mask_BxSx4224_bf0': mask_BxSx4224_bf0, 'L0_xattn_wq': _L0_xattn_in['wq'], 'L0_xattn_wk': _L0_xattn_in['wk'], 'L0_xattn_wv': _L0_xattn_in['wv'], 'L0_xattn_wo': _L0_xattn_in['wo'], 'L0_attn_Wq': _L0_attn_in['Wq'], 'L0_attn_bq': _L0_attn_in['bq'], 'L0_attn_Wk': _L0_attn_in['Wk'], 'L0_attn_bk': _L0_attn_in['bk'], 'L0_attn_Wv': _L0_attn_in['Wv'], 'L0_attn_bv': _L0_attn_in['bv'], 'L0_ffn_ln_gamma': _L0_ffn_in['ln_gamma'], 'L0_ffn_ln_beta': _L0_ffn_in['ln_beta'], 'L0_ffn_spline_bases': _L0_ffn_in['spline_bases'], 'L0_ffn_spline_slopes': _L0_ffn_in['spline_slopes'], 'L0_ffn_output_scale': _L0_ffn_in['output_scale']}

def reference(x, ctx_2048, mask_BxSx4224_bf0, L0_xattn_wq, L0_xattn_wk, L0_xattn_wv, L0_xattn_wo, L0_attn_Wq, L0_attn_bq, L0_attn_Wk, L0_attn_bk, L0_attn_Wv, L0_attn_bv, L0_ffn_ln_gamma, L0_ffn_ln_beta, L0_ffn_spline_bases, L0_ffn_spline_slopes, L0_ffn_output_scale):
    import jax
    import jax.numpy as jnp

    def _L0_xattn_ref(x, mask, k_cache, v_cache, wq, wk, wv, wo):
        import jax, jax.numpy as jnp
        import numpy as np
        import math
        DIM = 1024
        B, Q_LEN, KV_LEN = (8, 128, 2048)
        q = jnp.einsum('bsd,ed->bse', x, wq)
        k_new = jnp.einsum('bsd,ed->bse', x, wk)
        v_new = jnp.einsum('bsd,ed->bse', x, wv)
        k = jnp.concatenate([k_cache, k_new], axis=1)
        v = jnp.concatenate([v_cache, v_new], axis=1)
        scale = 1.0 / math.sqrt(q.shape[-1])
        scores = jnp.einsum('bqd,bkd->bqk', q, k) * scale
        attn = jax.nn.softmax(scores, axis=-1)
        out = jnp.einsum('bqk,bkd->bqd', attn, v)
        return jnp.einsum('bqd,ed->bqe', out, wo)

    def _L0_attn_ref(hidden_states, Wq, bq, Wk, bk, Wv, bv):
        import jax, jax.numpy as jnp
        import numpy as np
        import math
        HIDDEN = 1024
        NUM_HEADS = 16
        HEAD_DIM = HIDDEN // NUM_HEADS
        BATCH = 2
        SEQ = 2048
        BLOCK = 128
        TOPK = 64
        NEG = -1000000000.0

        def _split_heads(x):
            n, t, _ = x.shape
            return x.reshape(n, t, NUM_HEADS, HEAD_DIM).transpose(0, 2, 1, 3)

        def _local_attention(q, k, v):
            n, h, t, d = q.shape
            nb = t // BLOCK
            half = BLOCK // 2
            qb = q.reshape(n, h, nb, BLOCK, d)
            win = jnp.arange(nb)[:, None] * BLOCK - half + jnp.arange(2 * BLOCK)[None, :]
            valid = (win >= 0) & (win < t)
            winc = jnp.clip(win, 0, t - 1)
            kb = k[:, :, winc, :]
            vb = v[:, :, winc, :]
            scores = jnp.einsum('nhbqd,nhbkd->nhbqk', qb, kb) / math.sqrt(d)
            scores = jnp.where(valid[None, None, :, None, :], scores, NEG)
            probs = jax.nn.softmax(scores, axis=-1)
            ctx = jnp.einsum('nhbqk,nhbkd->nhbqd', probs, vb)
            return ctx.reshape(n, h, t, d)

        def _global_index(q):
            n, h, t, d = q.shape
            norm = jnp.linalg.norm(q, axis=-1)
            _, top_idx = jax.lax.top_k(norm, TOPK - 2)
            bos = jnp.zeros((n, h, 1), jnp.int32)
            eos = jnp.full((n, h, 1), t - 1, jnp.int32)
            return jnp.concatenate([bos, top_idx.astype(jnp.int32), eos], axis=-1)
        q = _split_heads(hidden_states @ Wq + bq)
        k = _split_heads(hidden_states @ Wk + bk)
        v = _split_heads(hidden_states @ Wv + bv)
        n, h, t, d = q.shape
        ctx = _local_attention(q, k, v)
        idx = _global_index(q)
        qg = jnp.take_along_axis(q, idx[..., None], axis=-2)
        g_scores = jnp.einsum('nhqd,nhkd->nhqk', qg, k) / math.sqrt(d)
        g_probs = jax.nn.softmax(g_scores, axis=-1)
        g_ctx = jnp.einsum('nhqk,nhkd->nhqd', g_probs, v)
        bn = jnp.arange(n)[:, None, None]
        bh = jnp.arange(h)[None, :, None]
        ctx = ctx.at[bn, bh, idx].set(g_ctx)
        out = ctx.transpose(0, 2, 1, 3).reshape(n, t, h * d)
        return out

    def _L0_ffn_ref(x, ln_gamma, ln_beta, spline_bases, spline_slopes, output_scale):
        import jax, jax.numpy as jnp
        import numpy as np
        D_MODEL = 1024
        NUM_TILES = 64
        D_SLICE = D_MODEL // NUM_TILES
        TILES_PER_CLUSTER = 8
        NUM_CLUSTERS = NUM_TILES // TILES_PER_CLUSTER
        GRID = 16
        LN_EPS = 1e-05
        DIMS = (np.arange(NUM_TILES)[:, None] * D_SLICE + np.arange(D_SLICE)[None, :]) % D_MODEL
        DIMS = jnp.asarray(DIMS, dtype=jnp.int32)

        def _forward(x, ln_gamma, ln_beta, spline_bases, spline_slopes, output_scale):
            B, S, D = x.shape
            N = B * S
            mu = jnp.mean(x, axis=-1, keepdims=True)
            var = jnp.mean(jnp.square(x - mu), axis=-1, keepdims=True)
            xn = (x - mu) * jax.lax.rsqrt(var + LN_EPS) * ln_gamma + ln_beta
            xf = xn.reshape(N, D)
            slope_sign = jnp.sign(jnp.mean(spline_slopes, axis=-1))
            tile_sigs = jnp.zeros((NUM_TILES, D), dtype=x.dtype)
            tile_sigs = tile_sigs.at[jnp.arange(NUM_TILES)[:, None], DIMS].set(slope_sign)
            cluster_sigs = jnp.sign(tile_sigs.reshape(NUM_CLUSTERS, TILES_PER_CLUSTER, D).mean(axis=1))
            cluster_assign = jnp.arange(NUM_TILES, dtype=jnp.int32) // TILES_PER_CLUSTER
            input_sigs = jnp.sign(xf)
            cluster_scores = input_sigs @ cluster_sigs.T
            best_cluster = jnp.argmax(cluster_scores, axis=-1)
            tile_scores = input_sigs @ tile_sigs.T
            in_cluster = cluster_assign[None, :] == best_cluster[:, None]
            tile_idx = jnp.argmax(jnp.where(in_cluster, tile_scores, -jnp.inf), axis=-1)
            tok_dims = DIMS[tile_idx]
            x_slice = jnp.take_along_axis(xf, tok_dims, axis=1)
            tok_min = x_slice.min(axis=1)
            tok_max = x_slice.max(axis=1)
            onehot = tile_idx[None, :] == jnp.arange(NUM_TILES)[:, None]
            tile_min = jnp.where(onehot, tok_min[None, :], jnp.inf).min(axis=1)
            tile_max = jnp.where(onehot, tok_max[None, :], -jnp.inf).max(axis=1)
            mn = tile_min[tile_idx][:, None]
            mx = tile_max[tile_idx][:, None]
            u = jnp.clip((x_slice - mn) / (mx - mn + 1e-08), 0.0, 1.0 - 1e-06)
            gi = jnp.clip((u * GRID).astype(jnp.int32), 0, GRID - 1)
            j = jnp.arange(D_SLICE)[None, :]
            b = spline_bases[tile_idx[:, None], j, gi]
            s = spline_slopes[tile_idx[:, None], j, gi]
            x_local = (u - gi.astype(u.dtype) / GRID) * GRID
            delta = (b + s * x_local) * output_scale[tile_idx][:, None]
            out = jnp.zeros_like(xf).at[jnp.arange(N)[:, None], tok_dims].set(delta)
            return x + out.reshape(B, S, D)
        return _forward(x, ln_gamma, ln_beta, spline_bases, spline_slopes, output_scale)
    x = x + _L0_xattn_ref(_layernorm(x, axis=-1), mask_BxSx4224_bf0, ctx_2048, ctx_2048, L0_xattn_wq, L0_xattn_wk, L0_xattn_wv, L0_xattn_wo)
    x = x + _L0_attn_ref(_layernorm(x, axis=-1), L0_attn_Wq, L0_attn_bq, L0_attn_Wk, L0_attn_bk, L0_attn_Wv, L0_attn_bv)
    x = x + _L0_ffn_ref(_layernorm(x, axis=-1), L0_ffn_ln_gamma, L0_ffn_ln_beta, L0_ffn_spline_bases, L0_ffn_spline_slopes, L0_ffn_output_scale)
    return x

_drawn_inputs = setup_inputs


def setup_inputs(seed=0):
    import zlib

    import numpy as np

    out = dict(_drawn_inputs(seed))
    spreads = {'L0_attn_bq': (0.0, 0.689), 'L0_attn_bk': (0.0, 2.0), 'L0_attn_bv': (0.0, 0.1)}
    factors = {'L0_xattn_wk': 8.0,
     'L0_xattn_wv': 8.0,
     'L0_ffn_ln_gamma': 8.0,
     'L0_ffn_ln_beta': 8.0,
     'L0_ffn_spline_bases': 8.0,
     'L0_ffn_spline_slopes': 8.0,
     'L0_ffn_output_scale': 30.844,
     'ctx_2048': 8.0}
    for name, (base, spread) in spreads.items():
        noise = np.random.default_rng([zlib.crc32(name.encode()), seed]).standard_normal(out[name].shape)
        drawn = base * np.exp(spread * noise) if base else spread * noise
        out[name] = jnp.asarray(drawn.astype(out[name].dtype))
    for name, factor in factors.items():
        out[name] = (out[name] * factor).astype(out[name].dtype)
    return out
```

```python
from contextlib import ExitStack

import concourse.bass as bass
from concourse import mybir

F32 = mybir.dt.float32
F32R = mybir.dt.float32r
ALU = mybir.AluOpType
ACT = mybir.ActivationFunctionType
X = mybir.AxisListType.X

P = 128
T = 512
D = 1024
NT = T // P
NC = D // P
KV = 8192
NB = KV // T
HALF = 512
HEADS = 16
HD = D // HEADS
TOPK = 62
TILES = 64
CLUSTERS = 8
SLICE = D // TILES
GRID = 16
EPS = 1e-5
X_SCALE = 1.0 / 32.0
S_SCALE = 1.0 / 8.0
FAR = float(-(2.0 ** 100))
BIG = 1e30
BOOST = 1024.0

WQ, WK, WV = 0, 4, 8
K0 = 12
LOOP0 = 16
V14 = LOOP0 + 4 * (NB - 2)
V15 = V14 + 2
WO = V15 + 2
SV, SQ, SK = WO + 4, WO + 8, WO + 12
T_X = 0
T_P = 8
T_O = T_P + 4 * (NB + 1)
T_Y = T_O + 8
A_Q, A_K, A_V, A_O, A_SV, A_SQ, A_SK = (8 * n for n in range(7))
NU = NT * HEADS


class Tally:

    def __init__(self, eng, sem):
        self.eng, self.sem, self.n = eng, sem, 0

    def link(self, ins):
        self.n += 1
        ins.then_inc(self.sem, 1)
        self.eng.wait_ge(self.sem, self.n)


def program(nc, x_in, k_in, v_in, wq, wk, wv, wo, sv, sq, sk, bq, bk, bv, gamma, beta, bases, slopes, scale, out):
    with ExitStack() as ctx:
        def sb(name, shape, dt=F32):
            return ctx.enter_context(nc.sbuf_tensor(name, shape, dt))

        def sem(name):
            return ctx.enter_context(nc.semaphore(name))

        psum = ctx.enter_context(nc.psum_tensor("psum", [P, 8, 512], F32))
        xT = sb("xT", [P, 2, NC, T], F32R)
        qT = sb("qT", [P, 2, NC, T], F32R)
        slot = sb("slot", [P, 4, 2, 2048], F32R)
        klo = sb("klo", [P, NC, T], F32R)
        xres = sb("xres", [P, NT, D])
        oacc = sb("oacc", [P, NT, D])
        raw = sb("raw", [P, 2, 2048])
        prob = sb("prob", [P, 4, T])
        ident = sb("ident", [P, P])
        heads = sb("heads", [P, NC, HEADS])
        tables = sb("tables", [TILES, 2, SLICE * GRID])
        gath = sb("gath", [TILES, 4])
        norms = sb("norms", [HEADS, T])
        top8 = sb("top8", [HEADS, 8])
        bqc = sb("bqc", [P, NC])
        bkc = sb("bkc", [P, NC])
        steps = sb("steps", [P, GRID + 1])
        stat = sb("stat", [P, 2, 6])
        mv = sb("mv", [P, NT, 2])
        var = sb("var", [P, NT])
        rs0 = sb("rs0", [P, NT])
        rsq = sb("rsq", [P, 4])
        power = sb("power", [P, 1])
        rmax = sb("rmax", [P, NT])
        nbias = sb("nbias", [P, NT])
        nprev = sb("nprev", [P, NT])
        rsum = sb("rsum", [P, NT])
        alpha = sb("alpha", [P, NT])
        alpha_o = sb("alpha_o", [P, NT])
        lsum = sb("lsum", [P, NT])
        linv = sb("linv", [P, NT])
        hmax = sb("hmax", [P, 2])
        hbias = sb("hbias", [P, 4])
        hsum = sb("hsum", [P, 2, HEADS])
        hinv = sb("hinv", [P, 8])
        tsc = sb("tsc", [P, TILES])
        csc = sb("csc", [P, 4 * CLUSTERS])
        small = sb("small", [P, 8])
        xs = sb("xs", [P, NT, SLICE])
        tmm = sb("tmm", [TILES, 2, NT])
        slo = sb("slo", [TILES, 3, SLICE])

        pT = xT[:, 0].rearrange("p c (k t) -> p (c k t)", k=1).rearrange("p (s k t) -> p s k t", s=2, k=4)
        oT = qT
        qa = slot[:, 2:4].rearrange("p s h n -> p (s h n)").rearrange("p (h t) -> p h t", h=HEADS)
        qstack = qT[:].rearrange("p s c t -> p (s c) t")
        kstack = qa
        val = oacc
        qf = prob[:, 0:2]
        sqr = prob[:, 2:4]
        bvb = prob[:].rearrange("p a t -> p (a t)")[:, 0:D]
        hprob = prob[:, 0:2]
        hpT = prob[:, 2:4]
        outside = slot[0:HEADS, 0, 0, 0:896]
        flag = slot[:, 0, 0, 1024:1536].rearrange("p (r q) -> p r q", r=4)
        local = slot[0:HEADS, 0, 0, 1536:2048]
        spread = slot[0:TILES, 0, 1, 0:D]
        ssign = slot[:, 0, 1, D:2 * D]
        signs = slot[:, 1, 0, 0:D]
        ones = slot[0:TILES, 1, 0, D:D + P]
        onehot = slot[:, 1, 1, 0:NT * TILES].rearrange("p (i t) -> p i t", i=NT)
        gam = raw[:, 0, 0:D]
        bet = raw[:, 0, D:2 * D]
        xln = raw[:, 1, 0:D]
        xff = raw[:, 1, D:2 * D]
        wide = val[:, 1, :]
        bins = val[:, 2, 0:SLICE * (GRID + 1)].rearrange("p (j g) -> p j g", j=SLICE)
        pick = val[:, 2, 512:1024]
        pick_f = val[:, 3, 0:512]
        ubuf = val[:, 3, 512:1024]
        mmx = sb("mmx", [P, 2, TILES])
        ohT = slot[0:TILES, 1, 1, 512:512 + NT * P].rearrange("p (i t) -> p i t", i=NT)

        x_full = [sem(f"x_full{t}") for t in range(NT)]
        raw_full = [sem(f"raw_full{s}") for s in range(2)]
        consts_full = sem("consts_full")
        tables_full = sem("tables_full")
        bv_full = sem("bv_full")
        affine_full = sem("affine_full")
        piece_hi, piece_lo = sem("piece_hi"), sem("piece_lo")
        half_used = sem("half_used")
        ln_var, ln_pow, xn_ready = sem("ln_var"), sem("ln_pow"), sem("xn_ready")
        t_full, t_hi, t_lo = sem("t_full"), sem("t_hi"), sem("t_lo")
        proj_ready, proj_hi, proj_out = sem("proj_ready"), sem("proj_hi"), sem("proj_out")
        s_ready, row_max, bias_ready = sem("s_ready"), sem("row_max"), sem("bias_ready")
        prev_kept, p_ready, alpha_ready = sem("prev_kept"), sem("p_ready"), sem("alpha_ready")
        alpha_taken, l_scaled, l_done = sem("alpha_taken"), sem("l_scaled"), sem("l_done")
        pv_ready, o_done = sem("pv_ready"), sem("o_done")
        state_zero = sem("state_zero")
        consts_ready = sem("consts_ready")
        pool_step = sem("pool_step")
        dve_step = sem("dve_step")
        f_ready, fh_ready, f_lo = sem("f_ready"), sem("fh_ready"), sem("f_lo")
        sq_ready, norm_part = sem("sq_ready"), sem("norm_part")
        local_ready, outside_ready = sem("local_ready"), sem("outside_ready")
        flag_ready = sem("flag_ready")
        hs_ready, hbias_ready, hp_ready = sem("hs_ready"), sem("hbias_ready"), sem("hp_ready")
        ht_full, ht_out, ho_ready, ho_taken = sem("ht_full"), sem("ht_out"), sem("ho_ready"), sem("ho_taken")
        spread_ready, ssign_full, ssign_ready = sem("spread_ready"), sem("ssign_full"), sem("ssign_ready")
        xln_ready, base_ready = sem("xln_ready"), sem("base_ready")
        xf_ready, sign_ready = sem("xf_ready"), sem("sign_ready")
        mm_ready, mm_full, mm_taken = sem("mm_ready"), sem("mm_full"), sem("mm_taken")
        gath_ready, picked, tile_done, stored = sem("gath_ready"), sem("picked"), sem("tile_done"), sem("stored")

        block = ctx.enter_context(nc.Block())

        def wcols(s):
            return slot[:, s].rearrange("p h (c e) -> p h c e", c=NC)

        def wrows(s):
            return slot[:, s].rearrange("p h (c e) -> p h c e", c=4)

        def kchunk(s0, c, h):
            return slot[:, s0 + c // 4, h, (c % 4) * T:(c % 4 + 1) * T]

        def vrows(s0, kt, h, dh):
            at = (kt % 2) * D + dh * HALF
            return slot[:, s0 + kt // 2, h, at:at + HALF]

        def consumed(eng, m):
            kind, i = divmod(m, 4)
            if kind in (0, 1, 5, 6):
                eng.wait_ge(proj_ready, 8 * kind + 2 * (i + 1))
            elif i % 2:
                eng.wait_ge(proj_ready, 8 * kind + 2 * (i + 1))
            else:
                eng.wait_ge(half_used, 2 * (kind - 2) + i // 2 + 1)

        @block.sync
        def _(sp):
            def piece(par, src):
                sp.dma_start(raw[:, par, :], src).then_inc(raw_full[par], 16)

            def weight(n, w, i):
                if n >= 2:
                    sp.wait_ge(piece_lo, n - 1)
                piece(n % 2, w[i])

            for t in range(NT):
                sp.dma_start(xres[:, t, :], x_in[t * P:(t + 1) * P, :]).then_inc(x_full[t], 16)
                if t < 2:
                    weight(WQ + t, wq, t)
            sp.dma_start(bqc[:], bq).then_inc(consts_full, 16)
            sp.dma_start(bkc[:], bk).then_inc(consts_full, 16)
            sp.dma_start(tables[:, 0, :], bases).then_inc(tables_full, 16)
            sp.dma_start(tables[:, 1, :], slopes).then_inc(tables_full, 16)
            sp.dma_start(gath[:, 0:1], scale).then_inc(tables_full, 16)
            for i in range(2, 4):
                weight(WQ + i, wq, i)
            for i in range(4):
                weight(WK + i, wk, i)
            for i in range(4):
                weight(WV + i, wv, i)

            def keys(n_lo, b):
                for i in range(2):
                    sp.wait_ge(piece_lo, n_lo + i)
                    piece(i, k_in[b, i] if isinstance(b, int) else k_in[bass.ds(b, 1), i].rearrange("b p n -> (b p) n"))

            def values(n_lo, b):
                for i in range(2):
                    sp.wait_ge(piece_lo, n_lo + i)
                    piece(i, v_in[b, i] if isinstance(b, int) else v_in[bass.ds(b, 1), i].rearrange("b p n -> (b p) n"))

            keys(K0 - 1, 0)
            keys(K0 + 1, 1)
            with sp.Fori(1, NB - 1) as b:
                values(LOOP0 - 1 + 4 * (b - 1), b - 1)
                keys(LOOP0 + 1 + 4 * (b - 1), b + 1)
            values(V14 - 1, NB - 2)
            values(V15 - 1, NB - 1)
            for i in range(4):
                weight(WO + i, wo, i)
            for i in range(4):
                weight(SV + i, sv, i)
                if i == 0:
                    sp.wait_ge(t_full, T_O)
                    sp.dma_start(bvb, bv.partition_broadcast(P)).then_inc(bv_full, 16)
            for i in range(4):
                weight(SQ + i, sq, i)
            for i in range(4):
                weight(SK + i, sk, i)
            sp.wait_ge(piece_lo, SK + 4)
            sp.dma_start(gam, gamma.partition_broadcast(P)).then_inc(affine_full, 16)
            sp.dma_start(bet, beta.partition_broadcast(P)).then_inc(affine_full, 16)
            for i in range(NT):
                sp.wait_ge(tile_done, i + 1)
                sp.dma_start(out[i * P:(i + 1) * P, :], xres[:, i, :]).then_inc(stored, 16)
            sp.wait_ge(stored, 16 * NT)

        @block.gpsimd
        def _(pool):
            chain = Tally(pool, pool_step)
            chain.link(nc.gpsimd.memset(ident[:], 0.0))
            nc.gpsimd.affine_select(out=ident[:], in_=ident[:], compare_op=ALU.not_equal, fill=1.0, base=0,
                                    pattern=[[-1, P]], channel_multiplier=1).then_inc(consts_ready, 1)
            nc.gpsimd.memset(power[:], -0.5).then_inc(consts_ready, 1)

            def rsqrt(k, n):
                pool.wait_ge(ln_var, k + 1)
                nc.gpsimd.tensor_tensor(rs0[:, n:n + 1], var[:, n:n + 1], power[:], ALU.pow).then_inc(ln_pow, 1)
                pool.wait_ge(ln_pow, k + 1)

            pool.wait_ge(consts_ready, 2)
            for t in range(NT):
                rsqrt(t, t)
            chain.link(nc.gpsimd.memset(heads[:], 0.0))
            for j in range(NC):
                nc.gpsimd.memset(heads[0:HD, j, 2 * j:2 * j + 1], 1.0)
                ins = nc.gpsimd.memset(heads[HD:P, j, 2 * j + 1:2 * j + 2], 1.0)
            ins.then_inc(consts_ready, 1)
            pool.wait_ge(consts_ready, 3)
            for t in range(NT):
                rsqrt(NT + t, t)
            for j in range(NC):
                pool.wait_ge(f_ready, j + 1)
                if j >= 2:
                    pool.wait_ge(norm_part, j - 1)
                nc.gpsimd.tensor_tensor(sqr[:, j % 2], qf[:, j % 2], qf[:, j % 2], ALU.mult).then_inc(sq_ready, 1)
                pool.wait_ge(sq_ready, j + 1)
            consumed(pool, 26)
            o32 = outside.bitcast(F32)
            nc.gpsimd.memset(o32[:, 0:320], FAR)
            nc.gpsimd.memset(o32[:, 320:576], 0.0)
            nc.gpsimd.memset(o32[:, 576:896], FAR).then_inc(outside_ready, 1)
            pool.wait_ge(outside_ready, 1)

            def flags(u):
                i, h = divmod(u, HEADS)
                if u == 0:
                    pool.wait_ge(local_ready, 1)
                if u >= 4:
                    pool.wait_ge(hs_ready, u - 3)
                nc.gpsimd.tensor_scalar(flag[0:HEADS, u % 4, :], local[:, i * P:(i + 1) * P].bitcast(F32),
                                        ident[0:HEADS, h:h + 1], None, ALU.mult).then_inc(flag_ready, 1)
                pool.wait_ge(flag_ready, u + 1)

            def base(i):
                pool.wait_ge(xln_ready, i + 1)
                nc.gpsimd.tensor_tensor(xres[:, i, :], xres[:, i, :], xln, ALU.add).then_inc(base_ready, 1)
                pool.wait_ge(base_ready, i + 1)

            for i in range(NT + 1):
                for h in range(HEADS):
                    if i < NT:
                        flags(HEADS * i + h)
                    if i >= 1:
                        if h == 4:
                            rsqrt(2 * NT + 2 * (i - 1), 0)
                        if h == 6:
                            rsqrt(2 * NT + 2 * (i - 1) + 1, 1)
                        if h == 7:
                            base(i - 1)

        @block.scalar
        def _(act):
            def split(par, full, dst):
                act.wait_ge(raw_full[par], full)
                nc.scalar.copy(dst, raw[:, par, :]).then_inc(piece_hi, 1)

            def weight(n, s, used=None):
                if used is not None:
                    consumed(act, used - 1)
                split(n % 2, 16 * (n // 2 + 1), slot[:, s, 0, :])

            def natural(e, dst, t, hf, bank0=4):
                act.wait_ge(t_full, e + 1)
                nc.scalar.copy(dst[:, 0, 4 * hf:4 * hf + 4, t * P:(t + 1) * P],
                               psum[:, bank0 + e % 2, :].rearrange("p (c t) -> p c t", c=4)).then_inc(t_hi, 1)

            for t in range(NT):
                for hf in range(2):
                    natural(T_X + 2 * t + hf, xT, t, hf)
                if t < 2:
                    weight(WQ + t, t)

            def hi_of(a, dst):
                act.wait_ge(proj_ready, a + 1)
                nc.scalar.copy(dst, psum[:, bank_of(a), :]).then_inc(proj_hi, 1)

            for j in range(4):
                hi_of(A_Q + 2 * j, qT[:, 0, 2 * j, :])
                n = WQ + j + 2
                weight(n, n % 2, n - 1)
                hi_of(A_Q + 2 * j + 1, qT[:, 0, 2 * j + 1, :])
            for j in range(4):
                hi_of(A_K + 2 * j, kchunk(2, 2 * j, 0))
                n = WK + j + 2
                weight(n, n % 2, n - 1)
                hi_of(A_K + 2 * j + 1, kchunk(2, 2 * j + 1, 0))

            def softmax(u, q, j, first=False):
                act.wait_ge(bias_ready, u + 1)
                if not first:
                    if q == 0:
                        act.wait_ge(t_full, T_P + 4 * j)
                        act.wait_ge(l_done, j)
                nc.scalar.activation(prob[:, q, :], psum[:, q, :], ACT.Exp, bias=nbias[:, q:q + 1], scale=X_SCALE,
                                     accum_out=rsum[:, q:q + 1]).then_inc(p_ready, 1)
                if not first and q == 0:
                    act.wait_ge(alpha_taken, j)
                nc.scalar.activation(alpha[:, q:q + 1], nprev[:, q:q + 1], ACT.Exp, bias=nbias[:, q:q + 1],
                                     scale=-1.0).then_inc(alpha_ready, 1)

            def v_self(eh, t):
                act.wait_ge(proj_ready, A_V + 4 * eh + t + 1)
                nc.scalar.copy(vrows(2, t, 0, eh), psum[:, 4 * (1 - eh) + t, :]).then_inc(proj_hi, 1)

            weight(WV + 2, 0, WV + 1)
            for q in range(NT):
                softmax(q, q, 0, first=True)
            for t in range(NT):
                v_self(0, t)
                if t == 0:
                    weight(WV + 3, 1, WV + 2)
            weight(K0, 0, WV + 3)
            for t in range(NT):
                v_self(1, t)
            weight(K0 + 1, 1, WV + 4)

            def block_step(b, v_pieces, v_slot, k_next, pair):
                if v_pieces:
                    act.wait_ge(pv_ready, 8 * b)
                    for i in range(2):
                        split(i, 16 * (pair + 1), slot[:, 2 + i, 0, :])
                for kt in range(4):
                    act.wait_ge(t_full, T_P + 4 * b + kt + 1)
                    nc.scalar.copy(pT[:, 0, kt, :], psum[:, 4 + kt % 2, :]).then_inc(t_hi, 1)
                for q in range(NT):
                    softmax(4 * (b + 1) + q, q, b + 1)
                if k_next:
                    act.wait_ge(s_ready, 4 * (b + 2))
                    for i in range(2):
                        split(i, 16 * (pair + (2 if v_pieces else 1)), slot[:, i, 0, :])

            block_step(0, False, 2, True, LOOP0 // 2 - 1)
            with act.Fori(1, NB - 1) as b:
                block_step(b, True, 2, True, LOOP0 // 2 + 2 * (b - 1))
            block_step(NB - 1, True, 2, False, V14 // 2)
            for i in range(2):
                split(i, 16 * (V15 // 2 + 1), slot[:, i, 0, :])
            for kt in range(4):
                act.wait_ge(t_full, T_P + 4 * NB + kt + 1)
                nc.scalar.copy(pT[:, 0, kt, :], psum[:, 4 + kt % 2, :]).then_inc(t_hi, 1)
            for i in range(4):
                if i == 0:
                    act.wait_ge(pv_ready, 8 * NB)
                if i == 2:
                    for e in range(4):
                        natural(T_O + e, oT, e, 0)
                    act.wait_ge(pv_ready, 8 * (NB + 1))
                weight(WO + i, (2 + i) % 4)
            for e in range(4):
                natural(T_O + 4 + e, oT, e, 1)
            for i in range(4):
                weight(SV + i, (2 + i) % 4, 12 + i + 1)
                natural(T_Y + 2 * i, xT, i, 0, 0)
                natural(T_Y + 2 * i + 1, xT, i, 1, 0)

            def q_hi(j):
                act.wait_ge(f_ready, j + 1)
                nc.scalar.copy(qstack[0:HD, 2 * j, :], qf[0:HD, j % 2, :])
                nc.scalar.copy(qstack[HD:P, 2 * j + 1, :], qf[HD:P, j % 2, :]).then_inc(fh_ready, 1)

            def k_hi(j):
                act.wait_ge(f_ready, NC + j + 1)
                nc.scalar.copy(kstack[0:HD, 2 * j, :], qf[0:HD, j % 2, :])
                nc.scalar.copy(kstack[HD:P, 2 * j + 1, :], qf[HD:P, j % 2, :]).then_inc(fh_ready, 1)
                nc.scalar.copy(kstack[HD:P, 2 * j, :], qf[0:HD, j % 2, :])
                nc.scalar.copy(kstack[0:HD, 2 * j + 1, :], qf[HD:P, j % 2, :]).then_inc(f_lo, 1)

            for i in range(3):
                weight(SQ + i, (2 + i) % 4, 16 + i + 1)
            for j in range(4):
                q_hi(2 * j)
                if j == 0:
                    weight(SQ + 3, 1, 20)
                elif j >= 3:
                    weight(SK, 0, 23)
                q_hi(2 * j + 1)
            for j in range(4):
                if j == 0:
                    weight(SK + 1, 1, 24)
                k_hi(2 * j)
                if j < 2:
                    weight(SK + 2 + j, j, 25 + j)
                k_hi(2 * j + 1)

            def head_exp(u):
                act.wait_ge(hbias_ready, u + 1)
                if u >= 2:
                    act.wait_ge(ht_full, u - 1)
                if u % HEADS == 0 and u >= 2 * HEADS:
                    act.wait_ge(ho_taken, 2 * (u // HEADS - 1))
                nc.scalar.activation(hprob[:, u % 2, :], psum[:, u % 3, :], ACT.Exp, bias=hbias[:, u % 4:u % 4 + 1],
                                     scale=S_SCALE, accum_out=hsum[:, (u // HEADS) % 2, u % HEADS:u % HEADS + 1]
                                     ).then_inc(hp_ready, 1)

            def head_turn(u):
                act.wait_ge(ht_full, u + 1)
                if u >= 2:
                    act.wait_ge(ho_ready, u - 1)
                nc.scalar.copy(hpT[:, u % 2, :], psum[:, 3, :]).then_inc(ht_out, 1)

            def sign(i):
                act.wait_ge(xf_ready, i + 1)
                nc.scalar.activation(signs, xff, ACT.Sign).then_inc(sign_ready, 1)

            for u in range(NU + 1):
                if u < NU:
                    head_exp(u)
                if u == 3:
                    act.wait_ge(ssign_full, 1)
                    nc.scalar.copy(ssign, psum[:, 6:8, :].rearrange("p a t -> p (a t)")).then_inc(ssign_ready, 1)
                if u >= 1:
                    head_turn(u - 1)
                if u >= HEADS and u < NU and u % HEADS == 10:
                    sign(u // HEADS - 1)
            sign(NT - 1)

        @block.vector
        def _(dve):
            chain = Tally(dve, dve_step)
            V = nc.vector

            def split_lo(n, par, dst, hi):
                dve.wait_ge(piece_hi, n + 1)
                V.tensor_tensor(dst, raw[:, par, :], hi.bitcast(F32), ALU.subtract).then_inc(piece_lo, 1)

            def weight(n, s):
                split_lo(n, n % 2, slot[:, s, 1, :], slot[:, s, 0, :])

            def stats(src, k, n):
                for g in range(2):
                    ins = V.bn_stats(stat[:, g, :], src[:, g * HALF:(g + 1) * HALF])
                chain.link(ins)
                chain.link(V.bn_aggr(mv[:, n, :], stat[:].rearrange("p g s -> p (g s)")))
                V.tensor_scalar(var[:, n:n + 1], mv[:, n, 1:2], EPS, None, ALU.add).then_inc(ln_var, 1)

            def normalise(src, dst, k, n, done):
                dve.wait_ge(ln_pow, k + 1)
                chain.link(V.scalar_tensor_tensor(out=rsq[:, 0:1], in0=rs0[:, n:n + 1], scalar=var[:, n:n + 1],
                                                  in1=rs0[:, n:n + 1], op0=ALU.mult, op1=ALU.mult))
                chain.link(V.tensor_scalar(rsq[:, 1:2], rsq[:, 0:1], -0.5, 1.5, ALU.mult, ALU.add))
                chain.link(V.tensor_tensor(rsq[:, 2:3], rsq[:, 1:2], rs0[:, n:n + 1], ALU.mult))
                V.tensor_scalar(dst, src, mv[:, n, 0:1], rsq[:, 2:3], ALU.subtract, ALU.mult).then_inc(done, 1)

            def natural(e, dst, t, hf, bank0=4):
                dve.wait_ge(t_hi, e + 1)
                at = (4 * hf, 4 * hf + 4)
                V.tensor_tensor(dst[:, 1, at[0]:at[1], t * P:(t + 1) * P],
                                psum[:, bank0 + e % 2, :].rearrange("p (c t) -> p c t", c=4),
                                dst[:, 0, at[0]:at[1], t * P:(t + 1) * P].bitcast(F32),
                                ALU.subtract).then_inc(t_lo, 1)

            V.memset(nbias[:], BIG)
            V.memset(lsum[:], 0.0)
            for g in range(GRID + 1):
                V.memset(steps[:, g:g + 1], float(g))
            V.memset(oacc[:, :, :].rearrange("p a b -> p (a b)")[:, 0:1], 0.0).then_inc(state_zero, 1)
            dve.wait_ge(state_zero, 1)
            for t in range(NT):
                dve.wait_ge(x_full[t], 16)
                stats(xres[:, t, :], t, t)
                normalise(xres[:, t, :], oacc[:, t, :], t, t, xn_ready)
                for hf in range(2):
                    natural(T_X + 2 * t + hf, xT, t, hf)
                if t < 2:
                    weight(WQ + t, t)

            def lo_of(a, dst, hi):
                dve.wait_ge(proj_hi, a + 1)
                V.tensor_tensor(dst, psum[:, bank_of(a), :], hi.bitcast(F32), ALU.subtract).then_inc(proj_out, 1)

            for j in range(4):
                lo_of(A_Q + 2 * j, qT[:, 1, 2 * j, :], qT[:, 0, 2 * j, :])
                weight(WQ + j + 2, j % 2)
                lo_of(A_Q + 2 * j + 1, qT[:, 1, 2 * j + 1, :], qT[:, 0, 2 * j + 1, :])
            dve.wait_ge(t_full, T_X + 8)
            V.memset(oacc[:], 0.0).then_inc(state_zero, 1)
            for j in range(4):
                lo_of(A_K + 2 * j, kchunk(2, 2 * j, 1), kchunk(2, 2 * j, 0))
                weight(WK + j + 2, j % 2)
                lo_of(A_K + 2 * j + 1, kchunk(2, 2 * j + 1, 1), kchunk(2, 2 * j + 1, 0))

            def row_bias(u, q, j, first=False):
                dve.wait_ge(s_ready, u + 1)
                V.tensor_reduce(rmax[:, q:q + 1], psum[:, q, :], X, ALU.max).then_inc(row_max, 1)
                if not first:
                    dve.wait_ge(alpha_ready, 4 * j + q - 3)
                V.tensor_copy(nprev[:, q:q + 1], nbias[:, q:q + 1]).then_inc(prev_kept, 1)
                dve.wait_ge(prev_kept, u + 1)
                dve.wait_ge(row_max, u + 1)
                V.tensor_scalar(nbias[:, q:q + 1], rmax[:, q:q + 1], -X_SCALE, nbias[:, q:q + 1], ALU.mult,
                                ALU.min).then_inc(bias_ready, 1)

            def row_sums(j):
                dve.wait_ge(alpha_ready, 4 * (j + 1))
                V.tensor_tensor(lsum[:], lsum[:], alpha[:], ALU.mult).then_inc(l_scaled, 1)
                dve.wait_ge(l_scaled, j + 1)
                V.tensor_tensor(lsum[:], lsum[:], rsum[:], ALU.add).then_inc(l_done, 1)

            def v_self(eh, t):
                dve.wait_ge(proj_hi, A_V + 4 * eh + t + 1)
                V.tensor_tensor(vrows(2, t, 1, eh), psum[:, 4 * (1 - eh) + t, :], vrows(2, t, 0, eh).bitcast(F32),
                                ALU.subtract).then_inc(proj_out, 1)

            weight(WV + 2, 0)
            for q in range(NT):
                row_bias(q, q, 0, first=True)
            row_sums(0)
            for t in range(NT):
                v_self(0, t)
                if t == 0:
                    weight(WV + 3, 1)
            weight(K0, 0)
            for t in range(NT):
                v_self(1, t)
            weight(K0 + 1, 1)

            def out_add(j, g):
                dh, q = divmod(g, NT)
                dve.wait_ge(pv_ready, 8 * j + g + 1)
                o = oacc[:, q, dh * HALF:(dh + 1) * HALF]
                V.scalar_tensor_tensor(out=o, in0=o, scalar=alpha_o[:, q:q + 1], in1=psum[:, 6 + g % 2, :],
                                       op0=ALU.mult, op1=ALU.add).then_inc(o_done, 1)

            def turn_lo(e, kt):
                dve.wait_ge(t_hi, e + 1)
                V.tensor_tensor(pT[:, 1, kt, :], psum[:, 4 + kt % 2, :], pT[:, 0, kt, :].bitcast(F32),
                                ALU.subtract).then_inc(t_lo, 1)

            def take_alpha(j, first=False):
                dve.wait_ge(alpha_ready, 4 * (j + 1))
                if not first:
                    dve.wait_ge(o_done, 8 * j)
                V.tensor_copy(alpha_o[:], alpha[:]).then_inc(alpha_taken, 1)

            def block_step(b, n_v, n_k, first=False):
                take_alpha(b, first)
                if n_v is not None:
                    for i in range(2):
                        split_lo(n_v + i, i, slot[:, 2 + i, 1, :], slot[:, 2 + i, 0, :])
                row_bias(4 * (b + 1), 0, b + 1)
                turn_lo(T_P + 4 * b, 0)
                turn_lo(T_P + 4 * b + 1, 1)
                row_bias(4 * (b + 1) + 1, 1, b + 1)
                turn_lo(T_P + 4 * b + 2, 2)
                turn_lo(T_P + 4 * b + 3, 3)
                row_bias(4 * (b + 1) + 2, 2, b + 1)
                row_bias(4 * (b + 1) + 3, 3, b + 1)
                dve.wait_ge(alpha_taken, b + 1)
                for g in range(8):
                    if n_k is not None and g in (1, 3):
                        s = g // 2
                        split_lo(n_k + s, s, slot[:, s, 1, :], slot[:, s, 0, :])
                    if g == 4:
                        row_sums(b + 1)
                    out_add(b, g)

            block_step(0, None, K0 + 2, first=True)
            with dve.Fori(1, NB - 1) as b:
                block_step(b, LOOP0 + 4 * (b - 1), LOOP0 + 4 * (b - 1) + 2)
            block_step(NB - 1, V14, V15)
            take_alpha(NB)
            for kt in range(4):
                turn_lo(T_P + 4 * NB + kt, kt)
            dve.wait_ge(alpha_taken, NB + 1)
            chain.link(V.reciprocal(linv[:], lsum[:]))
            for g in range(8):
                if g == 2:
                    weight(WO, 2)
                    weight(WO + 1, 3)
                out_add(NB, g)
                if g >= 5:
                    natural(T_O + g - 5, oT, g - 5, 0)
            natural(T_O + 3, oT, 3, 0)
            weight(WO + 2, 0)
            weight(WO + 3, 1)
            for e in range(4):
                natural(T_O + 4 + e, oT, e, 1)

            def residual(eh, t):
                dve.wait_ge(proj_ready, A_O + 4 * eh + t + 1)
                r = xres[:, t, eh * HALF:(eh + 1) * HALF]
                V.scalar_tensor_tensor(out=r, in0=psum[:, 4 * eh + t, :], scalar=linv[:, t:t + 1], in1=r,
                                       op0=ALU.mult, op1=ALU.add).then_inc(proj_out, 1)

            for t in range(NT):
                residual(0, t)
            for t in range(NT):
                residual(1, t)
                dve.wait_ge(proj_out, A_O + 4 + t + 1)
                if t == 0:
                    dve.wait_ge(t_full, T_Y)
                stats(xres[:, t, :], NT + t, t)
                normalise(xres[:, t, :], oacc[:, t, :], NT + t, t, xn_ready)
                weight(SV + t, (2 + t) % 4)
                for hf in range(2):
                    natural(T_Y + 2 * t + hf, xT, t, hf, 0)
            dve.wait_ge(tables_full, 48)
            chain.link(V.tensor_reduce(slo[:, 0, :], tables[:, 1, :].rearrange("p (j g) -> p j g", j=SLICE), X,
                                       ALU.add))
            V.tensor_scalar(slo[:, 1, :], slo[:, 0, :], 0.0, None, ALU.is_gt)
            chain.link(V.tensor_scalar(slo[:, 2, :], slo[:, 0, :], 0.0, None, ALU.is_lt))
            chain.link(V.tensor_tensor(slo[:, 1, :], slo[:, 1, :], slo[:, 2, :], ALU.subtract))
            dve.wait_ge(bv_full, 16)

            def values(eh, t):
                dve.wait_ge(proj_ready, A_SV + 4 * eh + t + 1)
                V.tensor_tensor(val[:, t, eh * HALF:(eh + 1) * HALF], psum[:, 4 * (1 - eh) + t, :],
                                bvb[:, eh * HALF:(eh + 1) * HALF], ALU.add).then_inc(proj_out, 1)

            for t in range(NT):
                values(0, t)
            weight(SQ, 2)
            weight(SQ + 1, 3)
            for t in range(NT):
                values(1, t)
            dve.wait_ge(proj_out, A_SQ)
            weight(SQ + 2, 0)

            def biased(j, a, bias):
                dve.wait_ge(proj_ready, a + 1)
                if j >= 2:
                    dve.wait_ge(f_lo_of[j - 2][0], f_lo_of[j - 2][1])
                    if j - 2 < NC:
                        dve.wait_ge(sq_ready, j - 1)
                V.tensor_scalar(qf[:, j % 2, :], psum[:, 6 + j % 2, :], bias, None,
                                ALU.add).then_inc(f_ready, 1)
                dve.wait_ge(f_ready, j + 1)

            f_lo_of = [(fh_ready, j + 1) for j in range(NC)] + [(f_lo, j + 1) for j in range(NC)]

            def q_lo(j):
                biased(j, A_SQ + j, bqc[:, j:j + 1])
                dve.wait_ge(fh_ready, j + 1)
                V.tensor_tensor(qstack[HD:P, 2 * j, :], qf[0:HD, j % 2, :], qstack[0:HD, 2 * j, :].bitcast(F32),
                                ALU.subtract)
                V.tensor_tensor(qstack[0:HD, 2 * j + 1, :], qf[HD:P, j % 2, :],
                                qstack[HD:P, 2 * j + 1, :].bitcast(F32), ALU.subtract).then_inc(proj_out, 1)

            def k_lo(j):
                biased(NC + j, A_SK + j, bkc[:, j:j + 1])
                dve.wait_ge(fh_ready, NC + j + 1)
                V.tensor_tensor(klo[0:HD, j, :], qf[0:HD, j % 2, :], kstack[0:HD, 2 * j, :].bitcast(F32),
                                ALU.subtract)
                V.tensor_tensor(klo[HD:P, j, :], qf[HD:P, j % 2, :], kstack[HD:P, 2 * j + 1, :].bitcast(F32),
                                ALU.subtract).then_inc(proj_out, 1)

            dve.wait_ge(consts_full, 32)
            for j in range(4):
                q_lo(2 * j)
                if j == 0:
                    weight(SQ + 3, 1)
                elif j == 3:
                    weight(SK, 0)
                q_lo(2 * j + 1)

            def top_round(r):
                chain.link(V.max(out=top8[:], in_=norms[:]))
                if (r + 1) * 8 > TOPK:
                    chain.link(V.memset(top8[:, TOPK - 8 * r:8], -1.0))
                chain.link(V.match_replace(out=norms[:], in_to_replace=top8[:], in_values=norms[:], imm_value=-1.0))

            for j in range(NC):
                if j == 0:
                    weight(SK + 1, 1)
                k_lo(j)
                if j == 0:
                    dve.wait_ge(norm_part, NC)
                    chain.link(V.tensor_copy(norms[:], psum[0:HEADS, 2, :]))
                if j in (0, 2):
                    weight(SK + 2 + j // 2, j // 2)
                top_round(j)
            V.memset(norms[:, 0:1], -1.0)
            chain.link(V.memset(norms[:, T - 1:T], -1.0))
            consumed(dve, 26)
            V.tensor_scalar(local, norms[:], -1.0, None, ALU.not_equal).then_inc(local_ready, 1)
            V.tensor_tensor(spread.rearrange("p (t j) -> p t j", t=TILES),
                            ident[0:TILES, 0:TILES].unsqueeze(2).to_broadcast([TILES, TILES, SLICE]),
                            slo[:, 1, :].unsqueeze(1).to_broadcast([TILES, TILES, SLICE]), ALU.mult)
            consumed(dve, 27)
            V.tensor_scalar(ones, ident[0:TILES, :], 0.0, 1.0, ALU.mult, ALU.add).then_inc(spread_ready, 1)

            def head_bias(u):
                dve.wait_ge(hs_ready, u + 1)
                chain.link(V.tensor_reduce(hmax[:, u % 2:u % 2 + 1], psum[:, u % 3, :], X, ALU.max))
                if u >= 4:
                    dve.wait_ge(hp_ready, u - 3)
                V.tensor_scalar(hbias[:, u % 4:u % 4 + 1], hmax[:, u % 2:u % 2 + 1], -S_SCALE, None,
                                ALU.mult).then_inc(hbias_ready, 1)

            def heads_out(i, hf):
                dve.wait_ge(ho_ready, HEADS * i + 8 * hf + 8)
                chain.link(V.reciprocal(hinv[:], hsum[:, i % 2, 8 * hf:8 * hf + 8]))
                tmp = xln[:, 0:HALF]
                if i >= 1:
                    dve.wait_ge(base_ready, i)
                chain.link(V.tensor_tensor(tmp.rearrange("p (h d) -> p h d", h=8),
                                           psum[:, 4 + 2 * (i % 2) + hf, :].rearrange("p (h d) -> p h d", h=8),
                                           hinv[:].unsqueeze(2).to_broadcast([P, 8, HD]), ALU.mult))
                r = xres[:, i, hf * HALF:(hf + 1) * HALF]
                V.tensor_tensor(r, r, tmp, ALU.add).then_inc(ho_taken, 1)
                dve.wait_ge(ho_taken, 2 * i + hf + 1)

            def route(i, step):
                k = 2 * NT + 2 * i
                oh = onehot[:, i, :]
                oh32 = oh.bitcast(F32)
                tiles3 = [P, TILES, SLICE]
                if step == 0:
                    stats(xres[:, i, :], k, 0)
                elif step == 1:
                    normalise(xres[:, i, :], xln, k, 0, xln_ready)
                    dve.wait_ge(xln_ready, i + 1)
                elif step == 2:
                    stats(xln, k + 1, 1)
                elif step == 3:
                    normalise(xln, xff, k + 1, 1, dve_step)
                    chain.n += 1
                    dve.wait_ge(dve_step, chain.n)
                elif step == 4:
                    if i == 0:
                        dve.wait_ge(affine_full, 32)
                    chain.link(V.tensor_tensor(xff, xff, gam, ALU.mult))
                elif step == 5:
                    V.tensor_tensor(xff, xff, bet, ALU.add).then_inc(xf_ready, 1)
                elif step == 6:
                    dve.wait_ge(sign_ready, i + 1)
                    if i == 0:
                        dve.wait_ge(ssign_ready, 1)
                    chain.link(V.tensor_tensor(signs, signs.bitcast(F32), ssign.bitcast(F32), ALU.mult))
                elif step == 7:
                    chain.link(V.tensor_reduce(tsc[:], signs.bitcast(F32).rearrange("p (t j) -> p t j", t=TILES), X,
                                               ALU.add))
                elif step == 8:
                    c1, c2, c3 = (csc[:, CLUSTERS * n:CLUSTERS * (n + 1)] for n in range(3))
                    chain.link(V.tensor_reduce(c1, tsc[:].rearrange("p (c t) -> p c t", c=CLUSTERS), X, ALU.add))
                    chain.link(V.scalar_tensor_tensor(out=c2, in0=c1, scalar=8.0, in1=steps[:, 0:CLUSTERS],
                                                      op0=ALU.mult, op1=ALU.subtract))
                    chain.link(V.tensor_reduce(small[:, 0:1], c2, X, ALU.max))
                    chain.link(V.tensor_scalar(c3, c2, small[:, 0:1], BOOST, ALU.is_equal, ALU.mult))
                    t3 = tsc[:].rearrange("p (c t) -> p c t", c=CLUSTERS)
                    chain.link(V.scalar_tensor_tensor(
                        out=t3, in0=t3, scalar=8.0,
                        in1=steps[:, 0:8].unsqueeze(1).to_broadcast([P, CLUSTERS, 8]), op0=ALU.mult,
                        op1=ALU.subtract))
                    chain.link(V.tensor_tensor(t3, t3, c3.unsqueeze(2).to_broadcast([P, CLUSTERS, 8]), ALU.add))
                    chain.link(V.tensor_reduce(small[:, 1:2], tsc[:], X, ALU.max))
                    chain.link(V.tensor_scalar(oh, tsc[:], small[:, 1:2], None, ALU.is_equal))
                elif step == 9:
                    x3 = xff.rearrange("p (t j) -> p t j", t=TILES)
                    chain.link(V.tensor_tensor(x3, x3, oh32.unsqueeze(2).to_broadcast(tiles3), ALU.mult))
                elif step == 10:
                    chain.link(V.tensor_reduce(xs[:, i, :], xff.rearrange("p (t j) -> p j t", t=TILES), X, ALU.add))
                elif step == 11:
                    V.tensor_reduce(small[:, 2:3], xs[:, i, :], X, ALU.min)
                    V.tensor_reduce(small[:, 3:4], xs[:, i, :], X, ALU.max)
                    if i >= 1:
                        dve.wait_ge(mm_full, i)
                    chain.link(V.tensor_scalar(tsc[:], oh32, -BIG, BIG, ALU.mult, ALU.add))
                    V.scalar_tensor_tensor(out=mmx[:, 0, :], in0=oh32, scalar=small[:, 2:3], in1=tsc[:],
                                           op0=ALU.mult, op1=ALU.add)
                    V.scalar_tensor_tensor(out=mmx[:, 1, :], in0=oh32, scalar=small[:, 3:4], in1=tsc[:],
                                           op0=ALU.mult, op1=ALU.subtract).then_inc(mm_ready, 1)

            def extremes(i):
                dve.wait_ge(mm_full, i + 1)
                bank = psum[0:TILES, 4 + 2 * (i % 2), :]
                V.tensor_reduce(tmm[:, 0, i:i + 1], bank[:, P:2 * P], X, ALU.min)
                V.tensor_reduce(tmm[:, 1, i:i + 1], bank[:, 2 * P:3 * P], X, ALU.max)
                V.tensor_copy(ohT[:, i, :], bank[:, 0:P]).then_inc(mm_taken, 1)

            for u in range(NU):
                i, h = divmod(u, HEADS)
                head_bias(u)
                if h == 11:
                    heads_out(i, 0)
                if i >= 1:
                    if h == 3:
                        heads_out(i - 1, 1)
                    if h >= 4:
                        route(i - 1, h - 4)
                if i >= 2 and h == 0:
                    extremes(i - 2)
            heads_out(NT - 1, 1)
            extremes(NT - 2)
            for step in range(12):
                route(NT - 1, step)
            extremes(NT - 1)
            dve.wait_ge(mm_taken, NT)
            V.tensor_reduce(gath[:, 1:2], tmm[:, 0, :], X, ALU.min)
            V.tensor_reduce(gath[:, 2:3], tmm[:, 1, :], X, ALU.max).then_inc(gath_ready, 1)

            def spline(i):
                dve.wait_ge(picked, i + 1)
                g = pick_f[:, 0:3]
                rec, u, n16, cnt, neg = (ubuf[:, 16 * n:16 * n + 16] for n in range(5))
                chain.link(V.tensor_copy(g, psum[:, 4 + i, 0:3]))
                lo, hi, sc = g[:, 1:2], g[:, 2:3], g[:, 0:1]
                chain.link(V.tensor_scalar(rec[:, 0:1], hi, lo, 1e-8, ALU.subtract, ALU.add))
                chain.link(V.reciprocal(rec[:, 1:2], rec[:, 0:1]))
                chain.link(V.tensor_scalar(u, xs[:, i, :], lo, rec[:, 1:2], ALU.subtract, ALU.mult))
                chain.link(V.tensor_scalar(u, u, 0.0, 1.0 - 1e-6, ALU.max, ALU.min))
                chain.link(V.tensor_scalar(n16, u, float(GRID), None, ALU.mult))
                b3 = [P, SLICE, GRID + 1]
                chain.link(V.tensor_tensor(bins, n16.unsqueeze(2).to_broadcast(b3),
                                           steps[:].unsqueeze(1).to_broadcast(b3), ALU.is_ge))
                V.tensor_reduce(cnt, bins, X, ALU.add)
                cell = wide[:, 0:SLICE * GRID].rearrange("p (j g) -> p j g", j=SLICE)
                chain.link(V.tensor_tensor(cell, bins[:, :, 0:GRID], bins[:, :, 1:GRID + 1], ALU.subtract))
                V.scalar_tensor_tensor(out=neg, in0=cnt, scalar=-1.0, in1=n16, op0=ALU.add, op1=ALU.subtract)
                w = SLICE * GRID
                for s in range(2):
                    ins = V.tensor_tensor(pick[:, s * w:(s + 1) * w], psum[:, i, s * w:(s + 1) * w],
                                          wide[:, 0:w], ALU.mult)
                chain.link(ins)
                both = ubuf[:, 96:128]
                chain.link(V.tensor_reduce(both, pick.rearrange("p (n g) -> p n g", g=GRID), X, ALU.add))
                chain.link(V.tensor_tensor(u, both[:, SLICE:2 * SLICE], neg, ALU.mult))
                chain.link(V.tensor_tensor(u, both[:, 0:SLICE], u, ALU.subtract))
                chain.link(V.tensor_scalar(u, u, sc, None, ALU.mult))
                t3 = [P, TILES, SLICE]
                chain.link(V.tensor_tensor(wide.rearrange("p (t j) -> p t j", t=TILES),
                                           onehot[:, i, :].bitcast(F32).unsqueeze(2).to_broadcast(t3),
                                           u.unsqueeze(1).to_broadcast(t3), ALU.mult))
                if i == 0:
                    dve.wait_ge(base_ready, NT)
                V.tensor_tensor(xres[:, i, :], xres[:, i, :], wide, ALU.add).then_inc(tile_done, 1)

            for i in range(NT):
                spline(i)

        @block.tensor
        def _(pe):
            def mm3(dst, st, mov, first, last):
                for n, (a, c) in enumerate(((0, 0), (0, 1), (1, 0))):
                    ins = nc.tensor.matmul(dst, st(a), mov(c), start=first and n == 0, stop=last and n == 2)
                return ins

            def natural(e, src, t, hf, bank0=4, ready=()):
                if e >= 2:
                    pe.wait_ge(t_lo, e - 1)
                for c in range(4):
                    at = (4 * hf + c) * P
                    ins = nc.tensor.transpose(psum[:, bank0 + e % 2, c * P:(c + 1) * P], src[:, t, at:at + P],
                                              ident[:])
                ins.then_inc(t_full, 1)

            pe.wait_ge(consts_ready, 1)
            for t in range(NT):
                pe.wait_ge(xn_ready, t + 1)
                for hf in range(2):
                    natural(T_X + 2 * t + hf, oacc, t, hf)

            def columns(n, s, a0, free, side=None):
                pe.wait_ge(piece_lo, n + 1)
                w = wcols(s)
                for m in range(2):
                    a = a0 + m
                    if free(a):
                        pe.wait_ge(proj_out, free(a))
                    for c in range(NC):
                        ins = mm3(psum[:, bank_of(a), :], lambda h: w[:, h, c, m * P:(m + 1) * P],
                                  lambda h: xT[:, h, c, :], c == 0, c == NC - 1)
                    ins.then_inc(proj_ready, 1)
                    if side:
                        side(a)

            def rows(n, s, dh, bank0, src, ready):
                pe.wait_ge(piece_lo, n + 1)
                w = wrows(s)
                for t in range(NT):
                    ready(t)
                    for c in range(4):
                        ins = mm3(psum[:, bank0 + t, :], lambda h: src[:, h, 4 * dh + c, t * P:(t + 1) * P],
                                  lambda h: w[:, h, c, :], dh == 0 and c == 0, dh == 1 and c == 3)
                    if dh == 1:
                        ins.then_inc(proj_ready, 1)
                if dh == 0:
                    ins.then_inc(half_used, 1)

            pe.wait_ge(t_lo, 8)
            for j in range(4):
                columns(WQ + j, j % 2, A_Q + 2 * j, lambda a: a - 1 if a >= 2 else 0)
            for j in range(4):
                columns(WK + j, j % 2, A_K + 2 * j, lambda a: a - 1)

            def scores(u, q, s0):
                for c in range(NC):
                    ins = mm3(psum[:, q, :], lambda h: qT[:, h, c, q * P:(q + 1) * P], lambda h: kchunk(s0, c, h),
                              c == 0, c == NC - 1)
                ins.then_inc(s_ready, 1)

            pe.wait_ge(proj_out, A_V)
            for q in range(NT):
                scores(q, q, 2)

            def own_values(t, eh):
                if eh == 1:
                    pe.wait_ge(p_ready, t + 1)

            for eh in range(2):
                for dh in range(2):
                    n = WV + 2 * eh + dh
                    rows(n, n % 2, dh, 4 * (1 - eh), xT, lambda t: own_values(t, eh) if dh == 0 else None)
    
            def turn(e, kt):
                pe.wait_ge(t_lo, e - 1)
                for q in range(NT):
                    ins = nc.tensor.transpose(psum[:, 4 + kt % 2, q * P:(q + 1) * P],
                                              prob[:, q, kt * P:(kt + 1) * P], ident[:])
                ins.then_inc(t_full, 1)

            def with_values(j, g, s0, free):
                dh, q = divmod(g, NT)
                if free is not None:
                    pe.wait_ge(o_done, free)
                for kt in range(4):
                    ins = mm3(psum[:, 6 + g % 2, :], lambda h: pT[:, h, kt, q * P:(q + 1) * P],
                              lambda h: vrows(s0, kt, h, dh), kt == 0, kt == 3)
                ins.then_inc(pv_ready, 1)

            def block_step(b, keys_lo, values_lo, first=False):
                pe.wait_ge(piece_lo, keys_lo)
                for q in range(NT):
                    pe.wait_ge(p_ready, 4 * b + q + 1)
                    if first:
                        pe.wait_ge(proj_out, A_V + 4 + q + 1)
                    scores(4 * (b + 1) + q, q, 0)
                    if q < 2:
                        if q == 0:
                            pe.wait_ge(p_ready, 4 * (b + 1))
                        turn(T_P + 4 * b + 2 * q, 2 * q)
                        turn(T_P + 4 * b + 2 * q + 1, 2 * q + 1)
                pe.wait_ge(t_lo, T_P + 4 * (b + 1))
                if values_lo is not None:
                    pe.wait_ge(piece_lo, values_lo)
                for g in range(8):
                    with_values(b, g, 2, None if first and g < 2 else 8 * b + g - 1)

            block_step(0, K0 + 2, None, first=True)
            with pe.Fori(1, NB - 1) as b:
                block_step(b, LOOP0 + 4 * (b - 1), LOOP0 + 4 * (b - 1) + 2)
            block_step(NB - 1, V14, V14 + 2)
            pe.wait_ge(p_ready, 4 * (NB + 1))
            for kt in range(4):
                turn(T_P + 4 * NB + kt, kt)
            pe.wait_ge(t_lo, T_P + 4 * (NB + 1))
            pe.wait_ge(piece_lo, V15 + 2)
            for g in range(8):
                with_values(NB, g, 0, 8 * NB + g - 1)
                if g >= 4:
                    pe.wait_ge(o_done, 8 * NB + g - 3)
                    natural(T_O + g - 4, oacc, g - 4, 0)

            def wo_ready(t, eh, dh):
                if eh == 0 and dh == 0:
                    if t == 0:
                        pe.wait_ge(t_lo, T_O + 4)
                    if t >= 1:
                        q = t - 1
                        pe.wait_ge(o_done, 8 * NB + 4 + q + 1)
                        natural(T_O + 4 + q, oacc, q, 1)
                if eh == 0 and dh == 1 and t == 0:
                    pe.wait_ge(o_done, 8 * NB + 8)
                    natural(T_O + 7, oacc, 3, 1)
                if eh == 0 and dh == 1:
                    pe.wait_ge(t_lo, T_O + 5 + t)
                if eh == 1 and dh == 0 and t == 0:
                    pe.wait_ge(t_lo, T_Y)
                    pe.wait_ge(o_done, 8 * (NB + 1))
                if eh == 1 and dh == 1 and t >= 2:
                    y_turn(t - 2)

            def y_turn(t):
                pe.wait_ge(xn_ready, NT + t + 1)
                if t == 0:
                    pe.wait_ge(proj_out, A_O + 4)
                for hf in range(2):
                    natural(T_Y + 2 * t + hf, oacc, t, hf, 0)

            for eh in range(2):
                for dh in range(2):
                    i = 2 * eh + dh
                    rows(WO + i, (2 + i) % 4, dh, 4 * eh, oT, lambda t: wo_ready(t, eh, dh))
    
            def sv_ready(t, eh, dh):
                if eh == 0 and dh == 0:
                    if t in (1, 2):
                        y_turn(t + 1)
                    pe.wait_ge(t_lo, T_Y + 2 * t + 2)
                    pe.wait_ge(proj_out, A_O + 4 + t + 1)

            for eh in range(2):
                for dh in range(2):
                    i = 2 * eh + dh
                    rows(SV + i, (2 + i) % 4, dh, 4 * (1 - eh), xT, lambda t: sv_ready(t, eh, dh))
    
            def norm(j):
                pe.wait_ge(sq_ready, j + 1)
                if j == 0:
                    pe.wait_ge(consts_ready, 3)
                    pe.wait_ge(proj_out, A_SV + 7)
                nc.tensor.matmul(psum[0:HEADS, 2, :], heads[:, j, :], sqr[:, j % 2, :], start=(j == 0),
                                 stop=(j == NC - 1)).then_inc(norm_part, 1)

            def beside(a):
                if a - A_SQ >= 1 and a < A_SK:
                    norm(a - A_SQ - 1)
                if a == A_SK:
                    norm(NC - 1)

            for j in range(4):
                columns(SQ + j, (2 + j) % 4, A_SQ + 2 * j, lambda a: A_SV + 4 if a < A_SQ + 2 else a - 1, beside)
            for j in range(4):
                columns(SK + j, j % 2, A_SK + 2 * j, lambda a: a - 1, beside)

            def head_scores(u):
                i, h = divmod(u, HEADS)
                half = slice(0, HD) if h % 2 == 0 else slice(HD, P)
                at = slice(i * P, (i + 1) * P)
                if u == 0:
                    pe.wait_ge(f_lo, NC)
                    pe.wait_ge(proj_out, A_SK + 8)
                if u >= 3:
                    pe.wait_ge(hp_ready, u - 2)
                dst = psum[:, u % 3, :]
                nc.tensor.matmul(dst, qstack[:, h, at], kstack[:, h, :], start=True, stop=False)
                nc.tensor.matmul(dst, qstack[half, h, at], klo[half, h // 2, :], start=False, stop=False)
                pe.wait_ge(flag_ready, u + 1)
                if u == 0:
                    pe.wait_ge(outside_ready, 1)
                first = (NT - 1 - i) * P
                nc.tensor.matmul(dst, flag[0:HEADS, u % 4, :], outside[:, first:first + T], start=False,
                                 stop=True).then_inc(hs_ready, 1)

            def head_turn(u):
                pe.wait_ge(hp_ready, u + 1)
                if u >= 1:
                    pe.wait_ge(ht_out, u)
                for kt in range(4):
                    ins = nc.tensor.transpose(psum[:, 3, kt * P:(kt + 1) * P], hprob[:, u % 2, kt * P:(kt + 1) * P],
                                              ident[:])
                ins.then_inc(ht_full, 1)

            def head_values(u):
                i, h = divmod(u, HEADS)
                pe.wait_ge(ht_out, u + 1)
                if h == 0 and i >= 2:
                    pe.wait_ge(ho_taken, 2 * (i - 1))
                    pe.wait_ge(mm_taken, i - 1)
                if h == 0 and i == 1:
                    pe.wait_ge(ssign_ready, 1)
                for kt in range(4):
                    ins = nc.tensor.matmul(psum[:, 4 + 2 * (i % 2) + h // 8, (h % 8) * HD:(h % 8 + 1) * HD],
                                           hpT[:, u % 2, kt * P:(kt + 1) * P], val[:, kt, h * HD:(h + 1) * HD],
                                           start=(kt == 0), stop=(kt == 3))
                ins.then_inc(ho_ready, 1)

            def mm_turn(i):
                pe.wait_ge(mm_ready, i + 1)
                bank = psum[0:TILES, 4 + 2 * (i % 2), :]
                nc.tensor.transpose(bank[:, 0:P], onehot[:, i, :].bitcast(F32), ident[:])
                nc.tensor.transpose(bank[:, P:2 * P], mmx[:, 0, :], ident[:])
                nc.tensor.transpose(bank[:, 2 * P:3 * P], mmx[:, 1, :], ident[:]).then_inc(mm_full, 1)

            for u in range(NU + 2):
                if u < NU:
                    if u % HEADS == 0 and u >= 2 * HEADS:
                        mm_turn(u // HEADS - 2)
                    head_scores(u)
                if u == 2:
                    pe.wait_ge(spread_ready, 1)
                    for s in range(2):
                        ins = nc.tensor.matmul(psum[:, 6 + s, :], ones, spread[:, s * HALF:(s + 1) * HALF],
                                               start=True, stop=True)
                    ins.then_inc(ssign_full, 1)
                if 1 <= u <= NU:
                    head_turn(u - 1)
                if u >= 2:
                    head_values(u - 2)
            mm_turn(NT - 2)
            mm_turn(NT - 1)
            pe.wait_ge(gath_ready, 1)
            for i in range(NT):
                nc.tensor.matmul(psum[:, i, :], ohT[:, i, :].bitcast(F32), tables[:].rearrange("p a n -> p (a n)"), start=True,
                                 stop=True)
                nc.tensor.matmul(psum[:, 4 + i, 0:3], ohT[:, i, :].bitcast(F32), gath[:, 0:3], start=True,
                                 stop=True).then_inc(picked, 1)


def bank_of(a):
    return 6 + a % 2


def kernel(**inputs):
    import numpy as np
    import concourse.bacc as bacc
    from concourse import mybir as mb
    from concourse.bass_utils import run_bass_kernel_spmd as run

    g = {k: np.asarray(v) for k, v in inputs.items()}

    def columns(w):
        return np.ascontiguousarray(w.reshape(8, 128, 4, 256).transpose(2, 1, 0, 3)).reshape(4, 128, 2048)

    def rows(w):
        return np.ascontiguousarray(w.reshape(2, 4, 128, 2, 512).transpose(3, 0, 2, 1, 4)).reshape(4, 128, 2048)

    c = g["ctx_2048"][0]
    arrays = {
        "x": g["x"][0],
        "keys": np.ascontiguousarray(c.reshape(16, 512, 2, 4, 128).transpose(0, 2, 4, 3, 1)).reshape(16, 2, 128, 2048),
        "values": np.ascontiguousarray(c.reshape(16, 2, 2, 128, 1024).transpose(0, 1, 3, 2, 4)).reshape(16, 2, 128, 2048),
        "wq": columns(g["L0_xattn_wq"].T), "wk": columns(g["L0_xattn_wk"].T),
        "wv": rows(g["L0_xattn_wv"].T), "wo": rows(g["L0_xattn_wo"].T),
        "sv": rows(g["L0_attn_Wv"]), "sq": columns(g["L0_attn_Wq"]), "sk": columns(g["L0_attn_Wk"]),
        "bq": np.ascontiguousarray(g["L0_attn_bq"].reshape(8, 128).T),
        "bk": np.ascontiguousarray(g["L0_attn_bk"].reshape(8, 128).T),
        "bv": g["L0_attn_bv"], "gamma": g["L0_ffn_ln_gamma"], "beta": g["L0_ffn_ln_beta"],
        "bases": g["L0_ffn_spline_bases"].reshape(64, 256), "slopes": g["L0_ffn_spline_slopes"].reshape(64, 256),
        "scale": g["L0_ffn_output_scale"].reshape(64, 1),
    }
    nc = bacc.Bacc("TRN2", target_bir_lowering=False, num_devices=1)
    feed, args = {}, []
    for name, a in arrays.items():
        a = np.ascontiguousarray(a)
        feed[f"in_{name}_dram"] = a
        args.append(nc.dram_tensor(f"in_{name}_dram", a.shape, mb.dt.from_np(a.dtype), kind="ExternalInput").ap())
    args.append(nc.dram_tensor("out_0_dram", (512, 1024), mb.dt.float32, kind="ExternalOutput").ap())
    program(nc, *args)
    r = run(nc, [feed], core_ids=[0])
    return r.results[0]["out_0_dram"].reshape(1, 512, 1024)
```

```python
from contextlib import ExitStack

import concourse.bass as bass
from concourse import mybir

F32 = mybir.dt.float32
F32R = mybir.dt.float32r
ALU = mybir.AluOpType
ACT = mybir.ActivationFunctionType
X = mybir.AxisListType.X

P = 128
T = 512
D = 1024
NT = T // P
NC = D // P
KV = 8192
NB = KV // T
HALF = 512
HEADS = 16
HD = D // HEADS
TOPK = 62
TILES = 64
CLUSTERS = 8
SLICE = D // TILES
GRID = 16
EPS = 1e-5
X_SCALE = 1.0 / 32.0
S_SCALE = 1.0 / 8.0
FAR = float(-(2.0 ** 100))
BIG = 1e30
BOOST = 1024.0
ROUNDER = float(2 ** 23)

WQ, WK, WV = 0, 4, 8
K0 = 12
LOOP0 = 16
V14 = LOOP0 + 4 * (NB - 2)
V15 = V14 + 2
WO = V15 + 2
SV, SQ, SK = WO + 4, WO + 8, WO + 12
T_X = 0
T_P = 8
T_O = T_P + 4 * (NB + 1)
T_Y = T_O + 8
A_Q, A_K, A_V, A_O, A_SV, A_SQ, A_SK = (8 * n for n in range(7))
NU = NT * HEADS
FLAGS = 8
AHEAD = 4
FIRST = 3


class Tally:

    def __init__(self, eng, sem):
        self.eng, self.sem, self.n = eng, sem, 0

    def link(self, ins):
        self.n += 1
        ins.then_inc(self.sem, 1)
        self.eng.wait_ge(self.sem, self.n)


def program(nc, x_in, k_in, v_in, wq, wk, wv, wo, sv, sq, sk, bq, bk, bv, gamma, beta, bases, slopes, scale, out):
    with ExitStack() as ctx:
        def sb(name, shape, dt=F32):
            return ctx.enter_context(nc.sbuf_tensor(name, shape, dt))

        def sem(name):
            return ctx.enter_context(nc.semaphore(name))

        psum = ctx.enter_context(nc.psum_tensor("psum", [P, 8, 512], F32))
        xT = sb("xT", [P, 2, NC, T], F32R)
        qT = sb("qT", [P, 2, NC, T], F32R)
        slot = sb("slot", [P, 4, 2, 2048], F32R)
        klo = sb("klo", [P, NC, T], F32R)
        xres = sb("xres", [P, NT, D])
        oacc = sb("oacc", [P, NT, D])
        raw = sb("raw", [P, 2, 2048])
        prob = sb("prob", [P, 4, T])
        ident = sb("ident", [P, P])
        halves = sb("halves", [P, 2])
        tables = sb("tables", [TILES, 2, SLICE * GRID])
        gath = sb("gath", [TILES, 4])
        spare = sb("spare", [P, T])
        top8 = sb("top8", [HEADS, 8])
        bqc = sb("bqc", [P, NC])
        bkc = sb("bkc", [P, NC])
        steps = sb("steps", [P, GRID])
        stat = sb("stat", [P, NT, 2, 6])
        mv = sb("mv", [P, NT, 2])
        var = sb("var", [P, NT])
        rs0 = sb("rs0", [P, NT])
        rsq = sb("rsq", [P, NT, 3])
        power = sb("power", [P, 1])
        rmax = sb("rmax", [P, NT])
        nbias = sb("nbias", [P, NT])
        nprev = sb("nprev", [P, NT])
        rsum = sb("rsum", [P, NT])
        alpha = sb("alpha", [P, NT])
        alpha_o = sb("alpha_o", [P, NT])
        lsum = sb("lsum", [P, NT])
        linv = sb("linv", [P, NT])
        got = sb("got", [P, NT, 4])
        rec = sb("rec", [P, 2, NT])
        hmax = sb("hmax", [P, 2])
        hbias = sb("hbias", [P, 4])
        hsum = sb("hsum", [P, 2, HEADS])
        hinv = sb("hinv", [P, 8])
        tsc = sb("tsc", [P, TILES])
        csc = sb("csc", [P, 4 * CLUSTERS])
        small = sb("small", [P, 8])
        xs = sb("xs", [P, NT, SLICE])
        tmm = sb("tmm", [TILES, 2, NT])
        slo = sb("slo", [TILES, 3, SLICE])

        pT = xT[:, :, 0:4, :]
        pT_last = xT[:, :, 4:8, :]
        oT = qT
        qa = slot[:, 2:4].rearrange("p s h n -> p (s h n)").rearrange("p (h t) -> p h t", h=HEADS)
        qstack = qT[:].rearrange("p s c t -> p (s c) t")
        kstack = qa
        val = oacc
        qf = prob[:, 0:2]
        sqr = prob[:, 2:4]
        bvb = prob[:].rearrange("p a t -> p (a t)")[:, 0:D]
        norms = spare[0:HEADS, :]
        hprob = [spare, prob[:, 0], prob[:, 1]]
        hpT = prob[:, 2:4]
        outside = slot[:, 0, 0, 0:896]
        flag = slot[:, 0, 1, 0:FLAGS * P].rearrange("p (r q) -> p r q", r=FLAGS)
        local = slot[0:HEADS, 0, 0, 1536:2048]
        spread = slot[0:TILES, 1, 1, D:2 * D]
        ssign = slot[:, 0, 1, D:2 * D]
        signs = slot[:, 1, 0, 0:D]
        ones = slot[0:TILES, 1, 0, D:D + P]
        onehot = slot[:, 1, 1, 0:NT * TILES].rearrange("p (i t) -> p i t", i=NT)
        gam = raw[:, 0, 0:D]
        bet = raw[:, 0, D:2 * D]
        xln = raw[:, 1, 0:D]
        xff = raw[:, 1, D:2 * D]
        vflat = val[:].rearrange("p t e -> p (t e)")
        nval = NT * SLICE
        cell = vflat[:, 1088:1088 + nval * GRID]
        wide = [vflat[:, 2112:2112 + D], raw[:, 0, 0:D], raw[:, 0, D:2 * D], raw[:, 1, 0:D]]
        pick = raw[:, 1, :]
        ubuf = vflat[:, 3200:3200 + 8 * nval].rearrange("p (n i j) -> p n i j", n=8, i=NT)
        mmx = sb("mmx", [P, 2, TILES])
        ohT = slot[0:TILES, 1, 1, 512:512 + NT * P].rearrange("p (i t) -> p i t", i=NT)

        x_full = [sem(f"x_full{t}") for t in range(NT)]
        raw_full = [sem(f"raw_full{s}") for s in range(2)]
        consts_full = sem("consts_full")
        tables_full = sem("tables_full")
        bv_full = sem("bv_full")
        affine_full = sem("affine_full")
        piece_hi, piece_lo = sem("piece_hi"), sem("piece_lo")
        half_used = sem("half_used")
        ln_var, ln_pow, ln_ready, xn_ready = sem("ln_var"), sem("ln_pow"), sem("ln_ready"), sem("xn_ready")
        t_full, t_hi, t_lo = sem("t_full"), sem("t_hi"), sem("t_lo")
        proj_ready, proj_hi, proj_out = sem("proj_ready"), sem("proj_hi"), sem("proj_out")
        s_ready, row_max, bias_ready = sem("s_ready"), sem("row_max"), sem("bias_ready")
        prev_kept, p_ready, alpha_ready = sem("prev_kept"), sem("p_ready"), sem("alpha_ready")
        alpha_taken, l_scaled, l_done = sem("alpha_taken"), sem("l_scaled"), sem("l_done")
        pv_ready, o_done = sem("pv_ready"), sem("o_done")
        state_zero = sem("state_zero")
        consts_ready = sem("consts_ready")
        pool_step = sem("pool_step")
        dve_step = sem("dve_step")
        f_ready, fh_ready, f_lo = sem("f_ready"), sem("fh_ready"), sem("f_lo")
        sq_ready, norm_part = sem("sq_ready"), sem("norm_part")
        norms_kept, norms_turned = sem("norms_kept"), sem("norms_turned")
        local_ready, outside_ready = sem("local_ready"), sem("outside_ready")
        flag_ready = sem("flag_ready")
        hs_ready, hbias_ready, hp_ready = sem("hs_ready"), sem("hbias_ready"), sem("hp_ready")
        ht_full, ht_out, ho_ready, ho_taken = sem("ht_full"), sem("ht_out"), sem("ho_ready"), sem("ho_taken")
        spread_ready, ssign_full, ssign_ready = sem("spread_ready"), sem("ssign_full"), sem("ssign_ready")
        xln_ready, base_ready = sem("xln_ready"), sem("base_ready")
        xff_ready, gamma_done = sem("xff_ready"), sem("gamma_done")
        xf_ready, sign_ready = sem("xf_ready"), sem("sign_ready")
        mm_ready, mm_full, mm_taken = sem("mm_ready"), sem("mm_full"), sem("mm_taken")
        wide_ready = sem("wide_ready")
        gath_ready, rows_picked, picked = sem("gath_ready"), sem("rows_picked"), sem("picked")
        tile_done, stored = [sem(f"tile_done{i}") for i in range(NT)], sem("stored")

        block = ctx.enter_context(nc.Block())

        def wcols(s):
            return slot[:, s].rearrange("p h (c e) -> p h c e", c=NC)

        def wrows(s):
            return slot[:, s].rearrange("p h (c e) -> p h c e", c=4)

        def kchunk(s0, c, h):
            return slot[:, s0 + c // 4, h, (c % 4) * T:(c % 4 + 1) * T]

        def vrows(s0, kt, h, dh):
            at = (kt % 2) * D + dh * HALF
            return slot[:, s0 + kt // 2, h, at:at + HALF]

        def consumed(eng, m):
            kind, i = divmod(m, 4)
            if kind in (0, 1, 5, 6):
                eng.wait_ge(proj_ready, 8 * kind + 2 * (i + 1))
            elif i % 2:
                eng.wait_ge(proj_ready, 8 * kind + 2 * (i + 1))
            else:
                eng.wait_ge(half_used, 2 * (kind - 2) + i // 2 + 1)

        @block.sync
        def _(sp):
            def piece(par, src):
                sp.dma_start(raw[:, par, :], src).then_inc(raw_full[par], 16)

            def weight(n, w, i):
                if n >= 2:
                    sp.wait_ge(piece_lo, n - 1)
                piece(n % 2, w[i])

            for t in range(NT):
                sp.dma_start(xres[:, t, :], x_in[t * P:(t + 1) * P, :]).then_inc(x_full[t], 16)
            for i in range(2):
                weight(WQ + i, wq, i)
            sp.dma_start(bqc[:], bq).then_inc(consts_full, 16)
            sp.dma_start(bkc[:], bk).then_inc(consts_full, 16)
            sp.dma_start(tables[:, 0, :], bases).then_inc(tables_full, 16)
            sp.dma_start(tables[:, 1, :], slopes).then_inc(tables_full, 16)
            sp.dma_start(gath[:, 0:1], scale).then_inc(tables_full, 16)
            for i in range(2, 4):
                weight(WQ + i, wq, i)
            for i in range(4):
                weight(WK + i, wk, i)
            for i in range(4):
                weight(WV + i, wv, i)

            def keys(n_lo, b):
                for i in range(2):
                    sp.wait_ge(piece_lo, n_lo + i)
                    piece(i, k_in[b, i] if isinstance(b, int) else k_in[bass.ds(b, 1), i].rearrange("b p n -> (b p) n"))

            def values(n_lo, b):
                for i in range(2):
                    sp.wait_ge(piece_lo, n_lo + i)
                    piece(i, v_in[b, i] if isinstance(b, int) else v_in[bass.ds(b, 1), i].rearrange("b p n -> (b p) n"))

            keys(K0 - 1, 0)
            keys(K0 + 1, 1)
            with sp.Fori(1, NB - 1) as b:
                values(LOOP0 - 1 + 4 * (b - 1), b - 1)
                keys(LOOP0 + 1 + 4 * (b - 1), b + 1)
            values(V14 - 1, NB - 2)
            values(V15 - 1, NB - 1)
            for i in range(4):
                weight(WO + i, wo, i)
            for i in range(4):
                weight(SV + i, sv, i)
                if i == 0:
                    sp.wait_ge(t_full, T_O)
                    sp.dma_start(bvb, bv.partition_broadcast(P)).then_inc(bv_full, 16)
            for i in range(4):
                weight(SQ + i, sq, i)
            for i in range(4):
                weight(SK + i, sk, i)
            sp.wait_ge(piece_lo, SK + 4)
            sp.dma_start(gam, gamma.partition_broadcast(P)).then_inc(affine_full, 16)
            sp.dma_start(bet, beta.partition_broadcast(P)).then_inc(affine_full, 16)
            for i in (0, 1, 2, 3):
                sp.wait_ge(tile_done[i], 1)
                sp.dma_start(out[i * P:(i + 1) * P, :], xres[:, i, :]).then_inc(stored, 16)
            sp.wait_ge(stored, 16 * NT)

        @block.gpsimd
        def _(pool):
            chain = Tally(pool, pool_step)
            chain.link(nc.gpsimd.memset(ident[:], 0.0))
            nc.gpsimd.affine_select(out=ident[:], in_=ident[:], compare_op=ALU.not_equal, fill=1.0, base=0,
                                    pattern=[[-1, P]], channel_multiplier=1).then_inc(consts_ready, 1)
            nc.gpsimd.memset(power[:], -0.5).then_inc(consts_ready, 1)

            def rsqrt(k, n):
                pool.wait_ge(ln_var, k + 1)
                nc.gpsimd.tensor_tensor(rs0[:, n:n + 1], var[:, n:n + 1], power[:], ALU.pow).then_inc(ln_pow, 1)
                pool.wait_ge(ln_pow, k + 1)

            def shift(k, n):
                rsqrt(k, n)
                a, b, c = (rsq[:, n, m:m + 1] for m in range(3))
                if k >= NT:
                    pool.wait_ge(xn_ready, NT)
                chain.link(nc.gpsimd.tensor_scalar(a, rs0[:, n:n + 1], var[:, n:n + 1], rs0[:, n:n + 1], ALU.mult,
                                                   ALU.mult))
                chain.link(nc.gpsimd.tensor_scalar(b, a, -0.5, 1.5, ALU.mult, ALU.add))
                chain.link(nc.gpsimd.tensor_tensor(c, b, rs0[:, n:n + 1], ALU.mult))
                nc.gpsimd.tensor_scalar(a, mv[:, n, 0:1], c, -1.0, ALU.mult, ALU.mult).then_inc(ln_ready, 1)
                pool.wait_ge(ln_ready, k + 1)

            pool.wait_ge(consts_ready, 2)
            for t in range(NT):
                shift(t, t)
            chain.link(nc.gpsimd.memset(halves[:], 0.0))
            nc.gpsimd.memset(halves[0:HD, 0:1], 1.0)
            nc.gpsimd.memset(halves[HD:P, 1:2], 1.0).then_inc(consts_ready, 1)
            pool.wait_ge(consts_ready, 3)
            for t in range(NT):
                shift(NT + t, t)
            for j in range(NC):
                pool.wait_ge(f_ready, j + 1)
                if j >= 2:
                    pool.wait_ge(norm_part, j - 1)
                nc.gpsimd.tensor_tensor(sqr[:, j % 2], qf[:, j % 2], qf[:, j % 2], ALU.mult).then_inc(sq_ready, 1)
                pool.wait_ge(sq_ready, j + 1)
            for i in range(2, 4):
                pool.wait_ge(piece_hi, SK + i + 1)
                pool.wait_ge(piece_lo, SK + i)
                nc.gpsimd.tensor_tensor(slot[:, i % 2, 1, :], raw[:, i % 2, :], slot[:, i % 2, 0, :].bitcast(F32),
                                        ALU.subtract).then_inc(piece_lo, 1)
                pool.wait_ge(piece_lo, SK + i + 1)
            consumed(pool, 26)
            o32 = outside.bitcast(F32)
            chain.link(nc.gpsimd.memset(flag[:].bitcast(F32), 0.0))
            nc.gpsimd.memset(o32[:, 0:320], FAR)
            nc.gpsimd.memset(o32[:, 320:576], 0.0)
            nc.gpsimd.memset(o32[:, 576:896], FAR).then_inc(outside_ready, 1)
            pool.wait_ge(outside_ready, 1)

            def flags(u):
                i, h = divmod(u, HEADS)
                if u == 0:
                    pool.wait_ge(local_ready, 1)
                if u >= FLAGS:
                    pool.wait_ge(hs_ready, u - FLAGS + 1)
                nc.gpsimd.tensor_scalar(flag[0:HEADS, u % FLAGS, :], local[:, i * P:(i + 1) * P].bitcast(F32),
                                        ident[0:HEADS, h:h + 1], 1.0, ALU.mult, ALU.mult).then_inc(flag_ready, 1)
                pool.wait_ge(flag_ready, u + 1)

            def affine(i):
                if i == 0:
                    pool.wait_ge(affine_full, 32)
                pool.wait_ge(xff_ready, i + 1)
                nc.gpsimd.tensor_tensor(xff, xff, gam, ALU.mult).then_inc(gamma_done, 1)
                pool.wait_ge(gamma_done, i + 1)
                nc.gpsimd.tensor_tensor(xff, xff, bet, ALU.add).then_inc(xf_ready, 1)
                pool.wait_ge(xf_ready, i + 1)

            def base(i):
                pool.wait_ge(xln_ready, i + 1)
                nc.gpsimd.tensor_tensor(xres[:, i, :], xres[:, i, :], xln, ALU.add).then_inc(base_ready, 1)
                pool.wait_ge(base_ready, i + 1)

            for u in range(AHEAD):
                flags(u)
            for i in range(NT):
                for h in range(HEADS):
                    if HEADS * i + h + AHEAD < NU:
                        flags(HEADS * i + h + AHEAD)
                    if i >= 1:
                        if h == 4:
                            rsqrt(2 * NT + 2 * (i - 1), 2 * ((i - 1) % 2))
                        if h == 6:
                            base(i - 1)
                        if h == 7:
                            rsqrt(2 * NT + 2 * (i - 1) + 1, 2 * ((i - 1) % 2) + 1)
                        if h == 8:
                            affine(i - 1)
            rsqrt(4 * NT - 2, 2 * ((NT - 1) % 2))
            base(NT - 1)
            rsqrt(4 * NT - 1, 2 * ((NT - 1) % 2) + 1)
            for i in range(2):
                pool.wait_ge(wide_ready, i + 1)
                nc.gpsimd.tensor_tensor(xres[:, i, :], xres[:, i, :], wide[i], ALU.add).then_inc(tile_done[i], 1)
                pool.wait_ge(tile_done[i], 1)

        @block.scalar
        def _(act):
            def split(par, full, dst):
                act.wait_ge(raw_full[par], full)
                nc.scalar.copy(dst, raw[:, par, :]).then_inc(piece_hi, 1)

            def weight(n, s, used=None):
                if used is not None:
                    consumed(act, used - 1)
                split(n % 2, 16 * (n // 2 + 1), slot[:, s, 0, :])

            def natural(e, dst, t, hf, bank0=4, ring=2):
                act.wait_ge(t_full, e + 1)
                nc.scalar.copy(dst[:, 0, 4 * hf:4 * hf + 4, t * P:(t + 1) * P],
                               psum[:, bank0 + e % ring, :].rearrange("p (c t) -> p c t", c=4)).then_inc(t_hi, 1)

            def normalise(k, t):
                act.wait_ge(ln_ready, k + 1)
                nc.scalar.activation(oacc[:, t, :], xres[:, t, :], ACT.Identity, bias=rsq[:, t, 0:1],
                                     scale=rsq[:, t, 2:3]).then_inc(xn_ready, 1)

            for t in range(NT + 1):
                if t < NT:
                    normalise(t, t)
                if t >= 1:
                    for hf in range(2):
                        natural(T_X + 2 * (t - 1) + hf, xT, t - 1, hf, 0, NC)
            act.wait_ge(piece_lo, 1)
            weight(WQ + 1, 1)

            def hi_of(a, dst):
                act.wait_ge(proj_ready, a + 1)
                nc.scalar.copy(dst, psum[:, bank_of(a), :]).then_inc(proj_hi, 1)

            for j in range(4):
                for m in range(2):
                    hi_of(A_Q + 2 * j + m, qT[:, 0, 2 * j + m, :])
                n = WQ + j + 2
                weight(n, n % 2, n - 1)
            for j in range(4):
                for m in range(2):
                    hi_of(A_K + 2 * j + m, kchunk(2, 2 * j + m, 0))
                n = WK + j + 2
                weight(n, n % 2, n - 1)

            def softmax(u, q, j, first=False):
                act.wait_ge(bias_ready, u + 1)
                if not first:
                    if q == 0:
                        act.wait_ge(t_full, T_P + 4 * j)
                        act.wait_ge(l_done, j)
                nc.scalar.activation(prob[:, q, :], psum[:, q, :], ACT.Exp, bias=nbias[:, q:q + 1], scale=X_SCALE,
                                     accum_out=rsum[:, q:q + 1]).then_inc(p_ready, 1)
                if not first and q == 0:
                    act.wait_ge(alpha_taken, j)
                nc.scalar.activation(alpha[:, q:q + 1], nprev[:, q:q + 1], ACT.Exp, bias=nbias[:, q:q + 1],
                                     scale=-1.0).then_inc(alpha_ready, 1)

            def v_self(eh, t):
                act.wait_ge(proj_ready, A_V + 4 * eh + t + 1)
                nc.scalar.copy(vrows(2, t, 0, eh), psum[:, 4 * (1 - eh) + t, :]).then_inc(proj_hi, 1)

            def turn(e, kt, dst=pT):
                act.wait_ge(t_full, e + 1)
                nc.scalar.copy(dst[:, 0, kt, :], psum[:, 4 + kt % 2, :]).then_inc(t_hi, 1)

            for q in range(NT):
                softmax(q, q, 0, first=True)
            weight(WV + 2, 0, WV + 1)
            for t in range(NT):
                v_self(0, t)
            weight(WV + 3, 1, WV + 2)
            weight(K0, 0, WV + 3)
            for t in range(NT):
                v_self(1, t)
                turn(T_P + t, t)
            weight(K0 + 1, 1, WV + 4)

            def block_step(b, v_pieces, k_next, pair, turned=False):
                if v_pieces:
                    act.wait_ge(pv_ready, 8 * b)
                    for i in range(2):
                        split(i, 16 * (pair + 1), slot[:, 2 + i, 0, :])
                if not turned:
                    for kt in range(4):
                        turn(T_P + 4 * b + kt, kt)
                for q in range(NT):
                    softmax(4 * (b + 1) + q, q, b + 1)
                if k_next:
                    act.wait_ge(s_ready, 4 * (b + 2))
                    for i in range(2):
                        split(i, 16 * (pair + (2 if v_pieces else 1)), slot[:, i, 0, :])

            block_step(0, False, True, LOOP0 // 2 - 1, turned=True)
            with act.Fori(1, NB - 1) as b:
                block_step(b, True, True, LOOP0 // 2 + 2 * (b - 1))
            block_step(NB - 1, True, False, V14 // 2)
            act.wait_ge(s_ready, 4 * (NB + 1))
            for i in range(2):
                split(i, 16 * (V15 // 2 + 1), slot[:, i, 0, :])
                for kt in range(2 * i, 2 * i + 2):
                    turn(T_P + 4 * NB + kt, kt, pT_last)
            act.wait_ge(pv_ready, 8 * NB)
            weight(WO, 2)
            weight(WO + 1, 3)
            for e in range(4):
                natural(T_O + e, oT, e, 0)
            act.wait_ge(pv_ready, 8 * (NB + 1))
            natural(T_O + 4, oT, 0, 1)
            weight(WO + 2, 0)
            natural(T_O + 5, oT, 1, 1)
            natural(T_O + 6, oT, 2, 1)
            weight(WO + 3, 1)
            natural(T_O + 7, oT, 3, 1)
            for i in range(2):
                weight(SV + i, (2 + i) % 4, 12 + i + 1)
            for t in range(NT + 1):
                if t < NT:
                    normalise(NT + t, t)
                if t >= 1:
                    for hf in range(2):
                        natural(T_Y + 2 * (t - 1) + hf, xT, t - 1, hf, 0)
            for i in range(2, 4):
                weight(SV + i, (2 + i) % 4, 12 + i + 1)

            def q_hi(j):
                act.wait_ge(f_ready, j + 1)
                nc.scalar.copy(qstack[0:HD, 2 * j, :], qf[0:HD, j % 2, :])
                nc.scalar.copy(qstack[HD:P, 2 * j + 1, :], qf[HD:P, j % 2, :]).then_inc(fh_ready, 1)

            def k_hi(j):
                act.wait_ge(f_ready, NC + j + 1)
                nc.scalar.copy(kstack[0:HD, 2 * j, :], qf[0:HD, j % 2, :])
                nc.scalar.copy(kstack[HD:P, 2 * j + 1, :], qf[HD:P, j % 2, :]).then_inc(fh_ready, 1)
                nc.scalar.copy(kstack[HD:P, 2 * j, :], qf[0:HD, j % 2, :])
                nc.scalar.copy(kstack[0:HD, 2 * j + 1, :], qf[HD:P, j % 2, :]).then_inc(f_lo, 1)

            for i in range(4):
                weight(SQ + i, (2 + i) % 4, 16 + i + 1)
            for j in range(NC):
                q_hi(j)
                if j in (5, 7):
                    weight(SK + (j - 5) // 2, (j - 5) // 2, 23 + (j - 5) // 2)
            for j in range(NC - 1):
                k_hi(j)
                if j in (1, 3):
                    weight(SK + 2 + j // 2, j // 2, 25 + j // 2)

            def head_exp(u):
                act.wait_ge(hbias_ready, u + 1)
                if u == 0:
                    act.wait_ge(local_ready, 1)
                if u in (1, 2):
                    act.wait_ge(f_lo, NC - 2 + u)
                    act.wait_ge(proj_out, A_SK + NC - 2 + u)
                if u >= 3:
                    act.wait_ge(ht_full, u - 2)
                if u % HEADS == 0 and u >= 2 * HEADS:
                    act.wait_ge(ho_taken, 2 * (u // HEADS - 1))
                nc.scalar.activation(hprob[u % 3][:], psum[:, u % 3, :], ACT.Exp, bias=hbias[:, u % 4:u % 4 + 1],
                                     scale=S_SCALE, accum_out=hsum[:, (u // HEADS) % 2, u % HEADS:u % HEADS + 1]
                                     ).then_inc(hp_ready, 1)

            def head_turn(u):
                act.wait_ge(ht_full, u + 1)
                if u >= 2:
                    act.wait_ge(ho_ready, u - 1)
                nc.scalar.copy(hpT[:, u % 2, :], psum[:, 3, :]).then_inc(ht_out, 1)

            def sign(i):
                act.wait_ge(xf_ready, i + 1)
                nc.scalar.activation(signs, xff, ACT.Sign).then_inc(sign_ready, 1)

            for u in range(NU + 2):
                if u >= HEADS and u < NU and u % HEADS == 12:
                    sign(u // HEADS - 1)
                if u == 2:
                    k_hi(NC - 1)
                if u >= 2:
                    head_turn(u - 2)
                if u < NU:
                    head_exp(u)
                if u == 9:
                    act.wait_ge(ssign_full, 1)
                    nc.scalar.copy(ssign, psum[:, 6:8, :].rearrange("p a t -> p (a t)")).then_inc(ssign_ready, 1)
            sign(NT - 1)

        @block.vector
        def _(dve):
            chain = Tally(dve, dve_step)
            V = nc.vector

            def split_lo(n, par, dst, hi):
                dve.wait_ge(piece_hi, n + 1)
                V.tensor_tensor(dst, raw[:, par, :], hi.bitcast(F32), ALU.subtract).then_inc(piece_lo, 1)

            def weight(n, s):
                split_lo(n, n % 2, slot[:, s, 1, :], slot[:, s, 0, :])

            def half_stats(src, n, g):
                V.bn_stats(stat[:, n, g, :], src[:, g * HALF:(g + 1) * HALF]).then_inc(dve_step, 1)
                chain.n += 1

            def variance(n):
                dve.wait_ge(dve_step, chain.n)
                chain.link(V.bn_aggr(mv[:, n, :], stat[:, n].rearrange("p g s -> p (g s)")))
                V.tensor_scalar(var[:, n:n + 1], mv[:, n, 1:2], EPS, None, ALU.add).then_inc(ln_var, 1)

            def stats(src, n):
                for g in range(2):
                    half_stats(src, n, g)
                variance(n)

            def root(k, n):
                dve.wait_ge(ln_pow, k + 1)
                a, b, c = (rsq[:, n, m:m + 1] for m in range(3))
                chain.link(V.scalar_tensor_tensor(out=a, in0=rs0[:, n:n + 1], scalar=var[:, n:n + 1],
                                                  in1=rs0[:, n:n + 1], op0=ALU.mult, op1=ALU.mult))
                chain.link(V.tensor_scalar(b, a, -0.5, 1.5, ALU.mult, ALU.add))
                chain.link(V.tensor_tensor(c, b, rs0[:, n:n + 1], ALU.mult))
                return c

            def normalise(src, dst, k, n, done):
                c = root(k, n)
                V.tensor_scalar(dst, src, mv[:, n, 0:1], c, ALU.subtract, ALU.mult).then_inc(done, 1)

            def natural(e, dst, t, hf, bank0=4, ring=2):
                dve.wait_ge(t_hi, e + 1)
                at = (4 * hf, 4 * hf + 4)
                V.tensor_tensor(dst[:, 1, at[0]:at[1], t * P:(t + 1) * P],
                                psum[:, bank0 + e % ring, :].rearrange("p (c t) -> p c t", c=4),
                                dst[:, 0, at[0]:at[1], t * P:(t + 1) * P].bitcast(F32),
                                ALU.subtract).then_inc(t_lo, 1)

            V.memset(nbias[:], BIG)
            V.memset(lsum[:], 0.0)
            for g in range(GRID):
                V.memset(steps[:, g:g + 1], float(g))
            V.memset(oacc[:, :, :].rearrange("p a b -> p (a b)")[:, 0:1], 0.0).then_inc(state_zero, 1)
            dve.wait_ge(state_zero, 1)
            for t in range(NT):
                dve.wait_ge(x_full[t], 16)
                stats(xres[:, t, :], t)
            dve.wait_ge(raw_full[0], 16)
            V.tensor_copy(slot[:, 0, 0, :], raw[:, 0, :]).then_inc(piece_hi, 1)
            weight(WQ, 0)
            for t in range(NT):
                for hf in range(2):
                    natural(T_X + 2 * t + hf, xT, t, hf, 0, NC)
            weight(WQ + 1, 1)

            def lo_of(a, dst, hi):
                dve.wait_ge(proj_hi, a + 1)
                V.tensor_tensor(dst, psum[:, bank_of(a), :], hi.bitcast(F32), ALU.subtract).then_inc(proj_out, 1)

            for j in range(4):
                for m in range(2):
                    lo_of(A_Q + 2 * j + m, qT[:, 1, 2 * j + m, :], qT[:, 0, 2 * j + m, :])
                weight(WQ + j + 2, j % 2)
            dve.wait_ge(t_full, T_X + 8)
            V.memset(oacc[:], 0.0).then_inc(state_zero, 1)
            for j in range(4):
                for m in range(2):
                    lo_of(A_K + 2 * j + m, kchunk(2, 2 * j + m, 1), kchunk(2, 2 * j + m, 0))
                weight(WK + j + 2, j % 2)

            def row_bias(u, q, j, first=False):
                dve.wait_ge(s_ready, u + 1)
                V.tensor_reduce(rmax[:, q:q + 1], psum[:, q, :], X, ALU.max).then_inc(row_max, 1)
                if not first:
                    dve.wait_ge(alpha_ready, 4 * j + q - 3)
                V.tensor_copy(nprev[:, q:q + 1], nbias[:, q:q + 1]).then_inc(prev_kept, 1)
                dve.wait_ge(prev_kept, u + 1)
                dve.wait_ge(row_max, u + 1)
                V.tensor_scalar(nbias[:, q:q + 1], rmax[:, q:q + 1], -X_SCALE, nbias[:, q:q + 1], ALU.mult,
                                ALU.min).then_inc(bias_ready, 1)

            def row_sums(j):
                dve.wait_ge(alpha_ready, 4 * (j + 1))
                V.tensor_tensor(lsum[:], lsum[:], alpha[:], ALU.mult).then_inc(l_scaled, 1)
                dve.wait_ge(l_scaled, j + 1)
                V.tensor_tensor(lsum[:], lsum[:], rsum[:], ALU.add).then_inc(l_done, 1)

            def v_self(eh, t):
                dve.wait_ge(proj_hi, A_V + 4 * eh + t + 1)
                V.tensor_tensor(vrows(2, t, 1, eh), psum[:, 4 * (1 - eh) + t, :], vrows(2, t, 0, eh).bitcast(F32),
                                ALU.subtract).then_inc(proj_out, 1)

            def out_add(j, g):
                dh, q = divmod(g, NT)
                dve.wait_ge(pv_ready, 8 * j + g + 1)
                o = oacc[:, q, dh * HALF:(dh + 1) * HALF]
                V.scalar_tensor_tensor(out=o, in0=o, scalar=alpha_o[:, q:q + 1], in1=psum[:, 6 + g % 2, :],
                                       op0=ALU.mult, op1=ALU.add).then_inc(o_done, 1)

            def turn_lo(e, kt, dst=pT):
                dve.wait_ge(t_hi, e + 1)
                V.tensor_tensor(dst[:, 1, kt, :], psum[:, 4 + kt % 2, :], dst[:, 0, kt, :].bitcast(F32),
                                ALU.subtract).then_inc(t_lo, 1)

            def take_alpha(j, first=False):
                dve.wait_ge(alpha_ready, 4 * (j + 1))
                if not first:
                    dve.wait_ge(o_done, 8 * j)
                V.tensor_copy(alpha_o[:], alpha[:]).then_inc(alpha_taken, 1)

            def split_keys(n, s):
                split_lo(n, s, slot[:, s, 1, :], slot[:, s, 0, :])

            for q in range(NT):
                row_bias(q, q, 0, first=True)
            weight(WV + 2, 0)
            row_sums(0)
            for t in range(NT):
                v_self(0, t)
            weight(WV + 3, 1)
            weight(K0, 0)
            for t in range(NT):
                v_self(1, t)
                turn_lo(T_P + t, t)
            take_alpha(0, first=True)
            dve.wait_ge(alpha_taken, 1)
            out_add(0, 0)
            weight(K0 + 1, 1)
            for g in range(1, 4):
                out_add(0, g)
            for q in range(NT):
                row_bias(4 + q, q, 1)
            for g in range(4, 8):
                if g >= 6:
                    split_keys(K0 + 2 + g - 6, g - 6)
                if g == 5:
                    row_sums(1)
                out_add(0, g)

            def block_scores(b, n_v):
                take_alpha(b)
                for i in range(2):
                    split_lo(n_v + i, i, slot[:, 2 + i, 1, :], slot[:, 2 + i, 0, :])
                row_bias(4 * (b + 1), 0, b + 1)
                turn_lo(T_P + 4 * b, 0)
                turn_lo(T_P + 4 * b + 1, 1)
                row_bias(4 * (b + 1) + 1, 1, b + 1)
                turn_lo(T_P + 4 * b + 2, 2)
                turn_lo(T_P + 4 * b + 3, 3)
                row_bias(4 * (b + 1) + 2, 2, b + 1)
                row_bias(4 * (b + 1) + 3, 3, b + 1)
                dve.wait_ge(alpha_taken, b + 1)

            with dve.Fori(1, NB - 1) as b:
                block_scores(b, LOOP0 + 4 * (b - 1))
                for g in range(8):
                    if g in (1, 3):
                        split_keys(LOOP0 + 4 * (b - 1) + 2 + g // 2, g // 2)
                    if g == 4:
                        row_sums(b + 1)
                    out_add(b, g)
            block_scores(NB - 1, V14)
            for g in range(8):
                out_add(NB - 1, g)
                if g in (0, 2):
                    split_keys(V15 + g // 2, g // 2)
                if g % 2 == 0:
                    turn_lo(T_P + 4 * NB + g // 2, g // 2, pT_last)
                if g == 5:
                    row_sums(NB)
            take_alpha(NB)
            dve.wait_ge(alpha_taken, NB + 1)
            dve.wait_ge(l_done, NB + 1)
            chain.link(V.reciprocal(linv[:], lsum[:]))
            for g in range(8):
                out_add(NB, g)
                if g in (0, 2):
                    weight(WO + g // 2, 2 + g // 2)
                if g >= 5:
                    natural(T_O + g - 5, oT, g - 5, 0)
            natural(T_O + 3, oT, 3, 0)
            natural(T_O + 4, oT, 0, 1)
            weight(WO + 2, 0)
            natural(T_O + 5, oT, 1, 1)
            natural(T_O + 6, oT, 2, 1)
            weight(WO + 3, 1)
            natural(T_O + 7, oT, 3, 1)

            def residual(eh, t):
                dve.wait_ge(proj_ready, A_O + 4 * eh + t + 1)
                r = xres[:, t, eh * HALF:(eh + 1) * HALF]
                V.scalar_tensor_tensor(out=r, in0=psum[:, 4 * eh + t, :], scalar=linv[:, t:t + 1], in1=r,
                                       op0=ALU.mult, op1=ALU.add).then_inc(proj_out, 1)

            for t in range(NT):
                residual(0, t)
            dve.wait_ge(proj_out, A_O + NT)
            for t in range(NT):
                half_stats(xres[:, t, :], t, 0)
            for i in range(2):
                weight(SV + i, (2 + i) % 4)
            dve.wait_ge(t_full, T_Y)
            for t in range(NT + 2):
                if t < NT:
                    residual(1, t)
                    dve.wait_ge(proj_out, A_O + 4 + t + 1)
                    half_stats(xres[:, t, :], t, 1)
                    variance(t)
                if t >= 2:
                    for hf in range(2):
                        natural(T_Y + 2 * (t - 2) + hf, xT, t - 2, hf, 0)
            for i in range(2, 4):
                weight(SV + i, (2 + i) % 4)
            dve.wait_ge(tables_full, 48)
            chain.link(V.tensor_reduce(slo[:, 0, :], tables[:, 1, :].rearrange("p (j g) -> p j g", j=SLICE), X,
                                       ALU.add))
            V.tensor_scalar(slo[:, 1, :], slo[:, 0, :], 0.0, None, ALU.is_gt)
            chain.link(V.tensor_scalar(slo[:, 2, :], slo[:, 0, :], 0.0, None, ALU.is_lt))
            chain.link(V.tensor_tensor(slo[:, 1, :], slo[:, 1, :], slo[:, 2, :], ALU.subtract))
            dve.wait_ge(bv_full, 16)

            def values(eh, t):
                dve.wait_ge(proj_ready, A_SV + 4 * eh + t + 1)
                V.tensor_tensor(val[:, t, eh * HALF:(eh + 1) * HALF], psum[:, 4 * (1 - eh) + t, :],
                                bvb[:, eh * HALF:(eh + 1) * HALF], ALU.add).then_inc(proj_out, 1)

            for t in range(NT):
                values(0, t)
            for i in range(3):
                weight(SQ + i, (2 + i) % 4)
            for t in range(NT):
                values(1, t)
            dve.wait_ge(proj_out, A_SQ)
            weight(SQ + 3, 1)

            def biased(j, a, bias):
                dve.wait_ge(proj_ready, a + 1)
                if j >= 2:
                    dve.wait_ge(f_lo_of[j - 2][0], f_lo_of[j - 2][1])
                    if j - 2 < NC:
                        dve.wait_ge(sq_ready, j - 1)
                V.tensor_scalar(qf[:, j % 2, :], psum[:, 6 + j % 2, :], bias, None,
                                ALU.add).then_inc(f_ready, 1)
                dve.wait_ge(f_ready, j + 1)

            f_lo_of = [(fh_ready, j + 1) for j in range(NC)] + [(f_lo, j + 1) for j in range(NC)]

            def q_lo(j):
                biased(j, A_SQ + j, bqc[:, j:j + 1])
                dve.wait_ge(fh_ready, j + 1)
                V.tensor_tensor(qstack[HD:P, 2 * j, :], qf[0:HD, j % 2, :], qstack[0:HD, 2 * j, :].bitcast(F32),
                                ALU.subtract)
                V.tensor_tensor(qstack[0:HD, 2 * j + 1, :], qf[HD:P, j % 2, :],
                                qstack[HD:P, 2 * j + 1, :].bitcast(F32), ALU.subtract).then_inc(proj_out, 1)

            def k_bias(j):
                biased(NC + j, A_SK + j, bkc[:, j:j + 1])

            def k_lo(j):
                dve.wait_ge(fh_ready, NC + j + 1)
                V.tensor_tensor(klo[0:HD, j, :], qf[0:HD, j % 2, :], kstack[0:HD, 2 * j, :].bitcast(F32),
                                ALU.subtract)
                V.tensor_tensor(klo[HD:P, j, :], qf[HD:P, j % 2, :], kstack[HD:P, 2 * j + 1, :].bitcast(F32),
                                ALU.subtract).then_inc(proj_out, 1)

            dve.wait_ge(consts_full, 32)
            for j in range(NC):
                q_lo(j)
                if j in (5, 7):
                    weight(SK + (j - 5) // 2, (j - 5) // 2)

            def top_round(r):
                chain.link(V.max(out=top8[:], in_=norms))
                if (r + 1) * 8 > TOPK:
                    chain.link(V.memset(top8[:, TOPK - 8 * r:8], -1.0))
                chain.link(V.match_replace(out=norms, in_to_replace=top8[:], in_values=norms, imm_value=-1.0))

            rounds = {2: ((1,), (2,)), 3: ((3,), (4,)), 4: ((5,), (6,)), 5: ((7,), ())}
            for j in range(NC - 1):
                k_bias(j)
                if j == 0:
                    dve.wait_ge(norm_part, NC)
                    V.tensor_copy(tsc[:], psum[:, 2, 0:NT * HEADS]).then_inc(norms_kept, 1)
                for r in rounds.get(j, ((), ()))[0]:
                    top_round(r)
                if j == 5:
                    V.memset(norms[:, 0:1], -1.0)
                    chain.link(V.memset(norms[:, T - 1:T], -1.0))
                    consumed(dve, 26)
                    V.tensor_scalar(local, norms, -1.0, None, ALU.not_equal).then_inc(local_ready, 1)
                k_lo(j)
                if j == 1:
                    dve.wait_ge(norms_turned, 1)
                    chain.link(V.tensor_copy(norms, psum[0:HEADS, 3, :]))
                    top_round(0)
                for r in rounds.get(j, ((), ()))[1]:
                    top_round(r)

            def slope_signs():
                consumed(dve, 27)
                V.tensor_tensor(spread.rearrange("p (t j) -> p t j", t=TILES),
                                ident[0:TILES, 0:TILES].unsqueeze(2).to_broadcast([TILES, TILES, SLICE]),
                                slo[:, 1, :].unsqueeze(1).to_broadcast([TILES, TILES, SLICE]), ALU.mult)
                V.tensor_scalar(ones, ident[0:TILES, :], 0.0, 1.0, ALU.mult, ALU.add).then_inc(spread_ready, 1)

            def head_bias(u):
                dve.wait_ge(hs_ready, u + 1)
                chain.link(V.tensor_reduce(hmax[:, u % 2:u % 2 + 1], psum[:, u % 3, :], X, ALU.max))
                if u >= 4:
                    dve.wait_ge(hp_ready, u - 3)
                V.tensor_scalar(hbias[:, u % 4:u % 4 + 1], hmax[:, u % 2:u % 2 + 1], -S_SCALE, None,
                                ALU.mult).then_inc(hbias_ready, 1)

            def heads_out(i, hf):
                dve.wait_ge(ho_ready, HEADS * i + 8 * hf + 8)
                chain.link(V.reciprocal(hinv[:], hsum[:, i % 2, 8 * hf:8 * hf + 8]))
                tmp = xln[:, 0:HALF]
                if hf == 0 and i >= 1:
                    dve.wait_ge(base_ready, i)
                chain.link(V.tensor_tensor(tmp.rearrange("p (h d) -> p h d", h=8),
                                           psum[:, 4 + 2 * (i % 2) + hf, :].rearrange("p (h d) -> p h d", h=8),
                                           hinv[:].unsqueeze(2).to_broadcast([P, 8, HD]), ALU.mult))
                r = xres[:, i, hf * HALF:(hf + 1) * HALF]
                V.tensor_tensor(r, r, tmp, ALU.add).then_inc(ho_taken, 1)
                dve.wait_ge(ho_taken, 2 * i + hf + 1)

            def route(i, step):
                k = 2 * NT + 2 * i
                oh = onehot[:, i, :]
                oh32 = oh.bitcast(F32)
                tiles3 = [P, TILES, SLICE]
                n = 2 * (i % 2)
                if step == 0:
                    half_stats(xres[:, i, :], n, 0)
                elif step == 1:
                    half_stats(xres[:, i, :], n, 1)
                    variance(n)
                elif step == 2:
                    normalise(xres[:, i, :], xln, k, n, xln_ready)
                elif step == 3:
                    dve.wait_ge(xln_ready, i + 1)
                    stats(xln, n + 1)
                elif step == 4:
                    normalise(xln, xff, k + 1, n + 1, xff_ready)
                elif step == 5:
                    dve.wait_ge(affine_full, 32)
                    c = root(k + 1, n + 1)
                    chain.link(V.scalar_tensor_tensor(out=xff, in0=xln, scalar=mv[:, n + 1, 0:1], in1=gam,
                                                      op0=ALU.subtract, op1=ALU.mult))
                    V.scalar_tensor_tensor(out=xff, in0=xff, scalar=c, in1=bet, op0=ALU.mult,
                                           op1=ALU.add).then_inc(xf_ready, 1)
                elif step == 6:
                    dve.wait_ge(sign_ready, i + 1)
                    if i == 0:
                        dve.wait_ge(ssign_ready, 1)
                    chain.link(V.tensor_tensor(signs, signs.bitcast(F32), ssign.bitcast(F32), ALU.mult))
                elif step == 7:
                    chain.link(V.tensor_reduce(tsc[:], signs.bitcast(F32).rearrange("p (t j) -> p t j", t=TILES), X,
                                               ALU.add))
                elif step == 8:
                    c1, c2, c3 = (csc[:, CLUSTERS * n:CLUSTERS * (n + 1)] for n in range(3))
                    chain.link(V.tensor_reduce(c1, tsc[:].rearrange("p (c t) -> p c t", c=CLUSTERS), X, ALU.add))
                    chain.link(V.scalar_tensor_tensor(out=c2, in0=c1, scalar=8.0, in1=steps[:, 0:CLUSTERS],
                                                      op0=ALU.mult, op1=ALU.subtract))
                    chain.link(V.tensor_reduce(small[:, 0:1], c2, X, ALU.max))
                    chain.link(V.tensor_scalar(c3, c2, small[:, 0:1], BOOST, ALU.is_equal, ALU.mult))
                elif step == 9:
                    c3 = csc[:, 2 * CLUSTERS:3 * CLUSTERS]
                    t3 = tsc[:].rearrange("p (c t) -> p c t", c=CLUSTERS)
                    chain.link(V.scalar_tensor_tensor(
                        out=t3, in0=t3, scalar=8.0,
                        in1=steps[:, 0:8].unsqueeze(1).to_broadcast([P, CLUSTERS, 8]), op0=ALU.mult,
                        op1=ALU.subtract))
                    chain.link(V.tensor_tensor(t3, t3, c3.unsqueeze(2).to_broadcast([P, CLUSTERS, 8]), ALU.add))
                    chain.link(V.tensor_reduce(small[:, 1:2], tsc[:], X, ALU.max))
                    chain.link(V.tensor_scalar(oh, tsc[:], small[:, 1:2], None, ALU.is_equal))
                elif step == 10:
                    x3 = xff.rearrange("p (t j) -> p t j", t=TILES)
                    chain.link(V.tensor_tensor(x3, x3, oh32.unsqueeze(2).to_broadcast(tiles3), ALU.mult))
                elif step == 11:
                    chain.link(V.tensor_reduce(xs[:, i, :], xff.rearrange("p (t j) -> p j t", t=TILES), X, ALU.add))
                elif step == 12:
                    V.tensor_reduce(small[:, 2:3], xs[:, i, :], X, ALU.min)
                    V.tensor_reduce(small[:, 3:4], xs[:, i, :], X, ALU.max)
                    if i >= 1:
                        dve.wait_ge(mm_full, i)
                    chain.link(V.tensor_scalar(tsc[:], oh32, -BIG, BIG, ALU.mult, ALU.add))
                    V.scalar_tensor_tensor(out=mmx[:, 0, :], in0=oh32, scalar=small[:, 2:3], in1=tsc[:],
                                           op0=ALU.mult, op1=ALU.add)
                    V.scalar_tensor_tensor(out=mmx[:, 1, :], in0=oh32, scalar=small[:, 3:4], in1=tsc[:],
                                           op0=ALU.mult, op1=ALU.subtract).then_inc(mm_ready, 1)

            def extremes(i):
                dve.wait_ge(mm_full, i + 1)
                bank = psum[0:TILES, turn_bank(i), :]
                V.tensor_reduce(tmm[:, 0, i:i + 1], bank[:, P:2 * P], X, ALU.min)
                V.tensor_reduce(tmm[:, 1, i:i + 1], bank[:, 2 * P:3 * P], X, ALU.max)
                V.tensor_copy(ohT[:, i, :], bank[:, 0:P]).then_inc(mm_taken, 1)

            beside = {4: (1,), 5: (2,), 6: (3,), 7: (4,), 13: (6,), 14: (7,), 15: (8,)}
            beside_later = {0: (9,), 1: (10,), 2: (11,), 3: (12,)}
            for u in range(NU):
                i, h = divmod(u, HEADS)
                if u == 2:
                    k_bias(NC - 1)
                    k_lo(NC - 1)
                head_bias(u)
                if u == 3:
                    slope_signs()
                if h == 11:
                    heads_out(i, 0)
                if h == 12:
                    dve.wait_ge(ho_taken, 2 * i + 1)
                    route(i, 0)
                if i >= 1:
                    if h == 3:
                        heads_out(i - 1, 1)
                    for step in beside.get(h, ()):
                        route(i - 1, step)
                if i >= 2:
                    for step in beside_later.get(h, ()):
                        route(i - 2, step)
                    if h == 8:
                        extremes(i - 2)
            route(NT - 2, 9)
            route(NT - 2, 10)
            heads_out(NT - 1, 1)
            for tile, step in ((-1, 1), (-2, 11), (-1, 2), (-1, 3), (-2, 12), (-1, 5)):
                route(NT + tile, step)
            extremes(NT - 2)
            for step in range(6, 13):
                route(NT - 1, step)
            extremes(NT - 1)
            dve.wait_ge(mm_taken, NT)
            V.tensor_reduce(gath[:, 1:2], tmm[:, 0, :], X, ALU.min)
            V.tensor_reduce(gath[:, 2:3], tmm[:, 1, :], X, ALU.max).then_inc(gath_ready, 1)

            dve.wait_ge(picked, NT)
            chain.link(V.tensor_copy(got[:, :, 0:3], psum[:, 4, 0:4 * NT].rearrange("p (i n) -> p i n", n=4)[:, :, 0:3]))
            sc, lo, hi = (got[:, :, n] for n in range(3))
            u, n16, neg = ubuf[:, 0], ubuf[:, 1], ubuf[:, 2]
            cnt = ubuf[:, 3]
            wide_in = [P, NT, SLICE]
            chain.link(V.tensor_tensor(rec[:, 0, :], hi, lo, ALU.subtract))
            chain.link(V.tensor_scalar(rec[:, 0, :], rec[:, 0, :], 1e-8, None, ALU.add))
            chain.link(V.reciprocal(rec[:, 1, :], rec[:, 0, :]))
            chain.link(V.tensor_tensor(u, xs[:], lo.unsqueeze(2).to_broadcast(wide_in), ALU.subtract))
            chain.link(V.tensor_tensor(u, u, rec[:, 1, :].unsqueeze(2).to_broadcast(wide_in), ALU.mult))
            chain.link(V.tensor_scalar(u, u, 0.0, 1.0 - 1e-6, ALU.max, ALU.min))
            chain.link(V.tensor_scalar(n16, u, float(GRID), None, ALU.mult))
            chain.link(V.tensor_scalar(cnt, n16, ROUNDER, None, ALU.add))
            chain.link(V.tensor_scalar(cnt, cnt, -ROUNDER, None, ALU.add))
            chain.link(V.tensor_tensor(neg, cnt, n16, ALU.is_gt))
            chain.link(V.tensor_tensor(cnt, cnt, neg, ALU.subtract))
            b3 = [P, nval, GRID]
            chain.link(V.tensor_tensor(cell.rearrange("p (n g) -> p n g", n=nval),
                                       cnt.rearrange("p i j -> p (i j)").unsqueeze(2).to_broadcast(b3),
                                       steps[:, 0:GRID].unsqueeze(1).to_broadcast(b3), ALU.is_equal))
            w = SLICE * GRID
            dve.wait_ge(rows_picked, NT)
            dve.wait_ge(base_ready, NT)
            chain.link(V.tensor_tensor(pick.rearrange("p (i s n) -> p i s n", i=NT, s=2),
                                       psum[:, 0:NT, :].rearrange("p i (s n) -> p i s n", s=2),
                                       cell.rearrange("p (i n) -> p i n", i=NT).unsqueeze(2).to_broadcast(
                                           [P, NT, 2, w]), ALU.mult))
            chain.link(V.tensor_tensor(neg, cnt, n16, ALU.subtract))
            both = ubuf[:, 4:6].rearrange("p n i j -> p (n i j)")
            chain.link(V.tensor_reduce(both, pick.rearrange("p (n g) -> p n g", g=GRID), X, ALU.add))
            both4 = both.rearrange("p (i s j) -> p i s j", i=NT, s=2)
            chain.link(V.tensor_tensor(u, both4[:, :, 1, :], neg, ALU.mult))
            chain.link(V.tensor_tensor(u, both4[:, :, 0, :], u, ALU.subtract))
            chain.link(V.tensor_tensor(u, u, sc.unsqueeze(2).to_broadcast(wide_in), ALU.mult))

            for i in range(NT):
                t3 = [P, TILES, SLICE]
                V.tensor_tensor(wide[i].rearrange("p (t j) -> p t j", t=TILES),
                                onehot[:, i, :].bitcast(F32).unsqueeze(2).to_broadcast(t3),
                                u[:, i, :].unsqueeze(1).to_broadcast(t3), ALU.mult).then_inc(wide_ready, 1)
                if i >= 2:
                    dve.wait_ge(wide_ready, i + 1)
                    V.tensor_tensor(xres[:, i, :], xres[:, i, :], wide[i], ALU.add).then_inc(tile_done[i], 1)

        @block.tensor
        def _(pe):
            def mm3(dst, st, mov, first, last):
                for n, (a, c) in enumerate(((0, 0), (0, 1), (1, 0))):
                    ins = nc.tensor.matmul(dst, st(a), mov(c), start=first and n == 0, stop=last and n == 2)
                return ins

            def natural(e, src, t, hf, bank0=4, ring=2):
                if ring == 2:
                    pe.wait_ge(t_lo, e - 1)
                for c in range(4):
                    at = (4 * hf + c) * P
                    ins = nc.tensor.transpose(psum[:, bank0 + e % ring, c * P:(c + 1) * P], src[:, t, at:at + P],
                                              ident[:])
                ins.then_inc(t_full, 1)

            pe.wait_ge(consts_ready, 1)
            for t in range(NT):
                pe.wait_ge(xn_ready, t + 1)
                for hf in range(2):
                    natural(T_X + 2 * t + hf, oacc, t, hf, 0, NC)

            def columns(n, s, a0, free, side=None, amid=None):
                pe.wait_ge(piece_lo, n + 1)
                w = wcols(s)
                for m in range(2):
                    a = a0 + m
                    free(a)
                    for c in range(NC):
                        if amid and c == NC // 2:
                            amid(a)
                        ins = mm3(psum[:, bank_of(a), :], lambda h: w[:, h, c, m * P:(m + 1) * P],
                                  lambda h: xT[:, h, c, :], c == 0, c == NC - 1)
                    ins.then_inc(proj_ready, 1)
                    if side:
                        side(a)

            def rows(n, s, dh, bank0, src, ready):
                pe.wait_ge(piece_lo, n + 1)
                w = wrows(s)
                for t in range(NT):
                    ready(t)
                    for c in range(4):
                        if n == WO + 3 and t == NT - 1 and c == 3:
                            y_turn(0)
                        ins = mm3(psum[:, bank0 + t, :], lambda h: src[:, h, 4 * dh + c, t * P:(t + 1) * P],
                                  lambda h: w[:, h, c, :], dh == 0 and c == 0, dh == 1 and c == 3)
                    if dh == 1:
                        ins.then_inc(proj_ready, 1)
                if dh == 0:
                    ins.then_inc(half_used, 1)

            pe.wait_ge(t_lo, 8)
            for j in range(4):
                columns(WQ + j, j % 2, A_Q + 2 * j, lambda a: pe.wait_ge(proj_out, a - 1) if a >= 2 else None)
            for j in range(4):
                columns(WK + j, j % 2, A_K + 2 * j, lambda a: pe.wait_ge(proj_out, a - 1))

            def scores(u, q, s0):
                for c in range(NC):
                    ins = mm3(psum[:, q, :], lambda h: qT[:, h, c, q * P:(q + 1) * P], lambda h: kchunk(s0, c, h),
                              c == 0, c == NC - 1)
                ins.then_inc(s_ready, 1)

            def own_values(t, eh, dh):
                if eh == 0 and dh == 0 and t == 2:
                    pe.wait_ge(proj_out, A_V)
                if eh == 1 and dh == 0:
                    pe.wait_ge(p_ready, t + 1)
                if eh == 1 and dh == 1 and t >= 1:
                    turn(T_P + t - 1, t - 1)

            def turn(e, kt):
                pe.wait_ge(t_lo, e - 1)
                for q in range(NT):
                    ins = nc.tensor.transpose(psum[:, 4 + kt % 2, q * P:(q + 1) * P],
                                              prob[:, q, kt * P:(kt + 1) * P], ident[:])
                ins.then_inc(t_full, 1)

            rows(WV, 0, 0, 4, xT, lambda t: own_values(t, 0, 0))
            pe.wait_ge(proj_out, A_V)
            for q in range(NT):
                scores(q, q, 2)
            rows(WV + 1, 1, 1, 4, xT, lambda t: None)
            rows(WV + 2, 0, 0, 0, xT, lambda t: own_values(t, 1, 0))
            pe.wait_ge(proj_out, A_V + 4)
            rows(WV + 3, 1, 1, 0, xT, lambda t: own_values(t, 1, 1))
            turn(T_P + 3, 3)

            def with_values(j, g, s0, free, src=pT):
                dh, q = divmod(g, NT)
                if free is not None:
                    pe.wait_ge(o_done, free)
                for kt in range(4):
                    ins = mm3(psum[:, 6 + g % 2, :], lambda h: src[:, h, kt, q * P:(q + 1) * P],
                              lambda h: vrows(s0, kt, h, dh), kt == 0, kt == 3)
                ins.then_inc(pv_ready, 1)

            pe.wait_ge(t_lo, T_P + 4)
            for g in range(4):
                with_values(0, g, 2, g - 1 if g >= 2 else None)
            for q in range(NT):
                pe.wait_ge(piece_lo, K0 + 2)
                pe.wait_ge(proj_out, A_V + 4 + q + 1)
                scores(4 + q, q, 0)
            for g in range(4, 8):
                with_values(0, g, 2, g - 1)

            def block_scores(b, keys_lo):
                pe.wait_ge(piece_lo, keys_lo)
                for q in range(NT):
                    pe.wait_ge(p_ready, 4 * b + q + 1)
                    scores(4 * (b + 1) + q, q, 0)
                    if q < 2:
                        if q == 0:
                            pe.wait_ge(p_ready, 4 * (b + 1))
                        turn(T_P + 4 * b + 2 * q, 2 * q)
                        turn(T_P + 4 * b + 2 * q + 1, 2 * q + 1)
                pe.wait_ge(t_lo, T_P + 4 * (b + 1))

            with pe.Fori(1, NB - 1) as b:
                block_scores(b, LOOP0 + 4 * (b - 1))
                pe.wait_ge(piece_lo, LOOP0 + 4 * (b - 1) + 2)
                for g in range(8):
                    with_values(b, g, 2, 8 * b + g - 1)
            block_scores(NB - 1, V14)
            pe.wait_ge(piece_lo, V14 + 2)
            for g in range(8):
                with_values(NB - 1, g, 2, 8 * (NB - 1) + g - 1)
                if g % 2 == 0:
                    if g == 0:
                        pe.wait_ge(p_ready, 4 * (NB + 1))
                    turn(T_P + 4 * NB + g // 2, g // 2)
            pe.wait_ge(t_lo, T_P + 4 * (NB + 1))
            pe.wait_ge(piece_lo, V15 + 2)
            for g in range(8):
                with_values(NB, g, 0, 8 * NB + g - 1, pT_last)
                if g >= 4:
                    pe.wait_ge(o_done, 8 * NB + g - 3)
                    natural(T_O + g - 4, oacc, g - 4, 0)

            def wo_ready(t, eh, dh):
                if eh == 0 and dh == 0:
                    if t == 0:
                        pe.wait_ge(t_lo, T_O + 4)
                    if t >= 1:
                        q = t - 1
                        pe.wait_ge(o_done, 8 * NB + 4 + q + 1)
                        natural(T_O + 4 + q, oacc, q, 1)
                if eh == 0 and dh == 1 and t == 0:
                    pe.wait_ge(o_done, 8 * NB + 8)
                    natural(T_O + 7, oacc, 3, 1)
                if eh == 0 and dh == 1:
                    pe.wait_ge(t_lo, T_O + 5 + t)
                if eh == 1 and dh == 0 and t == 0:
                    pe.wait_ge(t_lo, T_Y)
                    pe.wait_ge(o_done, 8 * (NB + 1))

            def y_turn(t):
                pe.wait_ge(xn_ready, NT + t + 1)
                if t == 0:
                    pe.wait_ge(proj_out, A_O + 4)
                for hf in range(2):
                    natural(T_Y + 2 * t + hf, oacc, t, hf, 0)

            for eh in range(2):
                for dh in range(2):
                    i = 2 * eh + dh
                    rows(WO + i, (2 + i) % 4, dh, 4 * eh, oT, lambda t: wo_ready(t, eh, dh))
    
            def sv_ready(t, eh, dh):
                if eh == 0 and dh == 0:
                    if t < 3:
                        y_turn(t + 1)
                    pe.wait_ge(t_lo, T_Y + 2 * t + 2)
                    pe.wait_ge(proj_out, A_O + 4 + t + 1)

            for eh in range(2):
                for dh in range(2):
                    i = 2 * eh + dh
                    rows(SV + i, (2 + i) % 4, dh, 4 * (1 - eh), xT, lambda t: sv_ready(t, eh, dh))
    
            def norm(j):
                pe.wait_ge(sq_ready, j + 1)
                if j == 0:
                    pe.wait_ge(consts_ready, 3)
                    pe.wait_ge(proj_out, A_SV + 8)
                for t in range(NT):
                    at = t * HEADS + 2 * j
                    ins = nc.tensor.matmul(psum[:, 2, at:at + 2], sqr[:, j % 2, t * P:(t + 1) * P], halves[:],
                                           start=True, stop=True)
                ins.then_inc(norm_part, 1)

            def beside(a):
                if a - A_SQ >= 1 and a < A_SK:
                    norm(a - A_SQ - 1)
                if a == A_SK:
                    norm(NC - 1)
                if a == A_SK + 1:
                    pe.wait_ge(norms_kept, 1)
                    for t in range(NT):
                        ins = nc.tensor.transpose(psum[0:HEADS, 3, t * P:(t + 1) * P],
                                                  tsc[:, t * HEADS:(t + 1) * HEADS], ident[:])
                    ins.then_inc(norms_turned, 1)

            def head_bank_free(a):
                if a < A_SQ + 2:
                    pe.wait_ge(proj_out, A_SV + 4)
                else:
                    pe.wait_ge(f_ready, a - A_SQ - 1)

            def head_scores(u):
                i, h = divmod(u, HEADS)
                half = slice(0, HD) if h % 2 == 0 else slice(HD, P)
                at = slice(i * P, (i + 1) * P)
                if i == 0:
                    pe.wait_ge(f_lo, h // 2 + 1)
                    pe.wait_ge(proj_out, A_SK + h // 2 + 1)
                if u >= 3:
                    pe.wait_ge(hp_ready, u - 2)
                dst = psum[:, u % 3, :]
                nc.tensor.matmul(dst, qstack[:, h, at], kstack[:, h, :], start=True, stop=False)
                nc.tensor.matmul(dst, qstack[half, h, at], klo[half, h // 2, :], start=False, stop=False)
                pe.wait_ge(flag_ready, u + 1)
                if u == 0:
                    pe.wait_ge(outside_ready, 1)
                first = (NT - 1 - i) * P
                nc.tensor.matmul(dst, flag[:, u % FLAGS, :], outside[:, first:first + T], start=False,
                                 stop=True).then_inc(hs_ready, 1)

            def first_scores(a):
                if a == A_SK + NC - 1:
                    for u in range(FIRST):
                        head_scores(u)

            for j in range(4):
                columns(SQ + j, (2 + j) % 4, A_SQ + 2 * j, head_bank_free, beside)
            for j in range(4):
                columns(SK + j, j % 2, A_SK + 2 * j, head_bank_free, beside, first_scores)

            def head_turn(u):
                pe.wait_ge(hp_ready, u + 1)
                if u >= 1:
                    pe.wait_ge(ht_out, u)
                for kt in range(4):
                    ins = nc.tensor.transpose(psum[:, 3, kt * P:(kt + 1) * P], hprob[u % 3][:, kt * P:(kt + 1) * P],
                                              ident[:])
                ins.then_inc(ht_full, 1)

            def head_values(u):
                i, h = divmod(u, HEADS)
                pe.wait_ge(ht_out, u + 1)
                if h == 0 and i >= 2:
                    pe.wait_ge(ho_taken, 2 * (i - 1))
                if h == 0 and i >= 3:
                    pe.wait_ge(mm_taken, i - 2)
                if h == 0 and i == 1:
                    pe.wait_ge(ssign_ready, 1)
                for kt in range(4):
                    ins = nc.tensor.matmul(psum[:, 4 + 2 * (i % 2) + h // 8, (h % 8) * HD:(h % 8 + 1) * HD],
                                           hpT[:, u % 2, kt * P:(kt + 1) * P], val[:, kt, h * HD:(h + 1) * HD],
                                           start=(kt == 0), stop=(kt == 3))
                ins.then_inc(ho_ready, 1)

            def mm_turn(i):
                pe.wait_ge(mm_ready, i + 1)
                pe.wait_ge(ho_taken, 2 * (i + 2) if i + 1 < NT else 2 * i)
                if i >= 2:
                    pe.wait_ge(mm_taken, i - 1)
                bank = psum[0:TILES, turn_bank(i), :]
                nc.tensor.transpose(bank[:, 0:P], onehot[:, i, :].bitcast(F32), ident[:])
                nc.tensor.transpose(bank[:, P:2 * P], mmx[:, 0, :], ident[:])
                nc.tensor.transpose(bank[:, 2 * P:3 * P], mmx[:, 1, :], ident[:]).then_inc(mm_full, 1)

            for u in range(NU + 3):
                if FIRST <= u < NU:
                    if u % HEADS == 6 and u >= 2 * HEADS:
                        mm_turn(u // HEADS - 2)
                    head_scores(u)
                if u == 6:
                    pe.wait_ge(spread_ready, 1)
                    for s in range(2):
                        ins = nc.tensor.matmul(psum[:, 6 + s, :], ones, spread[:, s * HALF:(s + 1) * HALF],
                                               start=True, stop=True)
                    ins.then_inc(ssign_full, 1)
                if 2 <= u <= NU + 1:
                    head_turn(u - 2)
                if u >= 3:
                    head_values(u - 3)
            pe.wait_ge(hp_ready, NU)
            pe.wait_ge(tables_full, 48)

            def pick_tables(i):
                pe.wait_ge(mm_taken, i + 1)
                nc.tensor.matmul(psum[:, i, :], ohT[:, i, :].bitcast(F32), tables[:].rearrange("p a n -> p (a n)"),
                                 start=True, stop=True).then_inc(rows_picked, 1)

            mm_turn(NT - 2)
            for i in range(NT - 1):
                pick_tables(i)
            mm_turn(NT - 1)
            pe.wait_ge(gath_ready, 1)
            for i in range(NT):
                nc.tensor.matmul(psum[:, 4, 4 * i:4 * i + 3], ohT[:, i, :].bitcast(F32), gath[:, 0:3], start=True,
                                 stop=True).then_inc(picked, 1)
            pe.wait_ge(ht_out, NU)
            pick_tables(NT - 1)


def bank_of(a):
    return 6 + a % 2


def turn_bank(i):
    return 4 + 2 * ((i + 1) % 2)


def kernel(**inputs):
    import numpy as np
    import concourse.bacc as bacc
    from concourse import mybir as mb
    from concourse.bass_utils import run_bass_kernel_spmd as run

    g = {k: np.asarray(v) for k, v in inputs.items()}

    def columns(w):
        return np.ascontiguousarray(w.reshape(8, 128, 4, 256).transpose(2, 1, 0, 3)).reshape(4, 128, 2048)

    def rows(w):
        return np.ascontiguousarray(w.reshape(2, 4, 128, 2, 512).transpose(3, 0, 2, 1, 4)).reshape(4, 128, 2048)

    c = g["ctx_2048"][0]
    arrays = {
        "x": g["x"][0],
        "keys": np.ascontiguousarray(c.reshape(16, 512, 2, 4, 128).transpose(0, 2, 4, 3, 1)).reshape(16, 2, 128, 2048),
        "values": np.ascontiguousarray(c.reshape(16, 2, 2, 128, 1024).transpose(0, 1, 3, 2, 4)).reshape(16, 2, 128, 2048),
        "wq": columns(g["L0_xattn_wq"].T), "wk": columns(g["L0_xattn_wk"].T),
        "wv": rows(g["L0_xattn_wv"].T), "wo": rows(g["L0_xattn_wo"].T),
        "sv": rows(g["L0_attn_Wv"]), "sq": columns(g["L0_attn_Wq"]), "sk": columns(g["L0_attn_Wk"]),
        "bq": np.ascontiguousarray(g["L0_attn_bq"].reshape(8, 128).T),
        "bk": np.ascontiguousarray(g["L0_attn_bk"].reshape(8, 128).T),
        "bv": g["L0_attn_bv"], "gamma": g["L0_ffn_ln_gamma"], "beta": g["L0_ffn_ln_beta"],
        "bases": g["L0_ffn_spline_bases"].reshape(64, 256), "slopes": g["L0_ffn_spline_slopes"].reshape(64, 256),
        "scale": g["L0_ffn_output_scale"].reshape(64, 1),
    }
    nc = bacc.Bacc("TRN2", target_bir_lowering=False, num_devices=1)
    feed, args = {}, []
    for name, a in arrays.items():
        a = np.ascontiguousarray(a)
        feed[f"in_{name}_dram"] = a
        args.append(nc.dram_tensor(f"in_{name}_dram", a.shape, mb.dt.from_np(a.dtype), kind="ExternalInput").ap())
    args.append(nc.dram_tensor("out_0_dram", (512, 1024), mb.dt.float32, kind="ExternalOutput").ap())
    program(nc, *args)
    r = run(nc, [feed], core_ids=[0])
    return r.results[0]["out_0_dram"].reshape(1, 512, 1024)
```

```python
from contextlib import ExitStack

import concourse.bass as bass
from concourse import mybir

F32 = mybir.dt.float32
F32R = mybir.dt.float32r
ALU = mybir.AluOpType
ACT = mybir.ActivationFunctionType
X = mybir.AxisListType.X

P = 128
T = 512
D = 1024
NT = T // P
NC = D // P
KV = 8192
NB = KV // T
HALF = 512
HEADS = 16
HD = D // HEADS
TOPK = 62
TILES = 64
CLUSTERS = 8
SLICE = D // TILES
GRID = 16
EPS = 1e-5
X_SCALE = 1.0 / 32.0
S_SCALE = 1.0 / 8.0
FAR = float(-(2.0 ** 100))
BIG = 1e30
BOOST = 1024.0

WQ, WK, WV = 0, 4, 8
K0 = 12
LOOP0 = 16
V14 = LOOP0 + 4 * (NB - 2)
V15 = V14 + 2
WO = V15 + 2
SV, SQ, SK = WO + 4, WO + 8, WO + 12
T_X = 0
T_P = 8
T_O = T_P + 4 * (NB + 1)
T_Y = T_O + 8
A_Q, A_K, A_V, A_O, A_SV, A_SQ, A_SK = (8 * n for n in range(7))
NU = NT * HEADS
FLAGS = 8
AHEAD = 4
LAST_TURNS = (0, 2, 4, 5)
FIRST = 3


class Tally:

    def __init__(self, eng, sem):
        self.eng, self.sem, self.n = eng, sem, 0

    def link(self, ins):
        self.n += 1
        ins.then_inc(self.sem, 1)
        self.eng.wait_ge(self.sem, self.n)


def program(nc, x_in, k_in, v_in, wq, wk, wv, wo, sv, sq, sk, bq, bk, bv, gamma, beta, bases, slopes, scale, out):
    with ExitStack() as ctx:
        def sb(name, shape, dt=F32):
            return ctx.enter_context(nc.sbuf_tensor(name, shape, dt))

        def sem(name):
            return ctx.enter_context(nc.semaphore(name))

        psum = ctx.enter_context(nc.psum_tensor("psum", [P, 8, 512], F32))
        xT = sb("xT", [P, 2, NC, T], F32R)
        qT = sb("qT", [P, 2, NC, T], F32R)
        slot = sb("slot", [P, 4, 2, 2048], F32R)
        klo = sb("klo", [P, NC, T], F32R)
        xres = sb("xres", [P, NT, D])
        oacc = sb("oacc", [P, NT, D])
        raw = sb("raw", [P, 2, 2048])
        prob = sb("prob", [P, 4, T])
        ident = sb("ident", [P, P])
        halves = sb("halves", [P, 2])
        tables = sb("tables", [TILES, 2, SLICE * GRID])
        gath = sb("gath", [TILES, 4])
        spare = sb("spare", [P, T])
        top8 = sb("top8", [HEADS, 8])
        bqc = sb("bqc", [P, NC])
        bkc = sb("bkc", [P, NC])
        steps = sb("steps", [P, GRID])
        stat = sb("stat", [P, NT, 2, 6])
        mv = sb("mv", [P, NT, 2])
        var = sb("var", [P, NT])
        rs0 = sb("rs0", [P, NT])
        rsq = sb("rsq", [P, NT, 3])
        power = sb("power", [P, 1])
        rmax = sb("rmax", [P, NT])
        nbias = sb("nbias", [P, NT])
        nprev = sb("nprev", [P, NT])
        rsum = sb("rsum", [P, NT])
        alpha = sb("alpha", [P, NT])
        alpha_o = sb("alpha_o", [P, NT])
        lsum = sb("lsum", [P, NT])
        linv = sb("linv", [P, NT])
        got = sb("got", [P, NT, 4])
        rec = sb("rec", [P, 2, NT])
        hmax = sb("hmax", [P, 2])
        hbias = sb("hbias", [P, 4])
        hsum = sb("hsum", [P, 2, HEADS])
        hinv = sb("hinv", [P, 8])
        tsc = sb("tsc", [P, TILES])
        csc = sb("csc", [P, 4 * CLUSTERS])
        small = sb("small", [P, 8])
        xs = sb("xs", [P, NT, SLICE])
        tmm = sb("tmm", [TILES, 2, NT])
        slo = sb("slo", [TILES, 3, SLICE])
        mmx = sb("mmx", [P, 2, TILES])

        pT = xT[:, :, 0:4, :]
        pT_last = xT[:, :, 4:8, :]
        oT = qT
        qstack = qT[:].rearrange("p s c t -> p (s c) t")
        kstack = slot[:, 2:4].rearrange("p s h n -> p (s h n)").rearrange("p (h t) -> p h t", h=HEADS)
        val = oacc
        qf = prob[:, 0:2]
        sqr = prob[:, 2:4]
        bvb = prob[:].rearrange("p a t -> p (a t)")[:, 0:D]
        norms = spare[0:HEADS, :]
        hprob = [spare, prob[:, 0], prob[:, 1]]
        hpT = prob[:, 2:4]
        far = slot[:, 0, 0, 0:T]
        flag = slot[:, 0, 1, 0:FLAGS * P].rearrange("p (r q) -> p r q", r=FLAGS)
        local = slot[0:HEADS, 0, 0, 3 * T:4 * T]
        spread = slot[0:TILES, 1, 1, D:2 * D]
        ssign = slot[:, 0, 1, D:2 * D]
        signs = slot[:, 1, 0, 0:D]
        ones = slot[0:TILES, 1, 0, D:D + P]
        onehot = slot[:, 1, 1, 0:NT * TILES].rearrange("p (i t) -> p i t", i=NT)
        gam = raw[:, 0, 0:D]
        bet = raw[:, 0, D:2 * D]
        xln = raw[:, 1, 0:D]
        xff = raw[:, 1, D:2 * D]
        over = xln[:, 0:HALF]
        vflat = val[:].rearrange("p t e -> p (t e)")
        nval = NT * SLICE
        wide = [vflat[:, D:2 * D], raw[:, 0, 0:D], raw[:, 0, D:2 * D], raw[:, 1, 0:D]]
        ubuf = vflat[:, 0:3 * nval].rearrange("p (n i j) -> p n i j", n=3, i=NT)
        ohT = slot[0:TILES, 1, 1, HALF:HALF + NT * P].rearrange("p (i t) -> p i t", i=NT)

        x_full = [sem(f"x_full{t}") for t in range(NT)]
        raw_full = [sem(f"raw_full{s}") for s in range(2)]
        consts_full = sem("consts_full")
        tables_full = sem("tables_full")
        bv_full = sem("bv_full")
        affine_full = sem("affine_full")
        piece_hi, piece_lo = sem("piece_hi"), sem("piece_lo")
        half_used, half_ready = sem("half_used"), sem("half_ready")
        ln_var, ln_pow, ln_ready, xn_ready = sem("ln_var"), sem("ln_pow"), sem("ln_ready"), sem("xn_ready")
        t_full, t_hi, t_lo = sem("t_full"), sem("t_hi"), sem("t_lo")
        proj_ready, proj_hi, proj_out = sem("proj_ready"), sem("proj_hi"), sem("proj_out")
        s_ready, row_max, bias_ready = sem("s_ready"), sem("row_max"), sem("bias_ready")
        prev_kept, p_ready, alpha_ready = sem("prev_kept"), sem("p_ready"), sem("alpha_ready")
        alpha_taken, l_scaled, l_done = sem("alpha_taken"), sem("l_scaled"), sem("l_done")
        pv_ready, o_done = sem("pv_ready"), sem("o_done")
        state_zero = sem("state_zero")
        consts_ready = sem("consts_ready")
        pool_step = sem("pool_step")
        dve_step = sem("dve_step")
        f_ready, fh_ready, k_stacked = sem("f_ready"), sem("fh_ready"), sem("k_stacked")
        sq_ready, norm_part = sem("sq_ready"), sem("norm_part")
        norms_kept, norms_turned = sem("norms_kept"), sem("norms_turned")
        local_ready, far_ready = sem("local_ready"), sem("far_ready")
        flag_ready = sem("flag_ready")
        hs_ready, hbias_ready, hp_ready = sem("hs_ready"), sem("hbias_ready"), sem("hp_ready")
        ht_full, ht_out, ho_ready, ho_taken = sem("ht_full"), sem("ht_out"), sem("ho_ready"), sem("ho_taken")
        spread_ready, ssign_full, ssign_ready = sem("spread_ready"), sem("ssign_full"), sem("ssign_ready")
        xln_ready, base_ready = sem("xln_ready"), sem("base_ready")
        xff_ready, gamma_done = sem("xff_ready"), sem("gamma_done")
        xf_ready, sign_ready = sem("xf_ready"), sem("sign_ready")
        mm_ready, mm_full, mm_taken = sem("mm_ready"), sem("mm_full"), sem("mm_taken")
        delta_ready, wide_ready, wide_last = sem("delta_ready"), sem("wide_ready"), sem("wide_last")
        gath_ready, rows_picked, picked = sem("gath_ready"), sem("rows_picked"), sem("picked")
        tile_done, stored = [sem(f"tile_done{i}") for i in range(NT)], sem("stored")

        block = ctx.enter_context(nc.Block())

        def wcols(s):
            return slot[:, s].rearrange("p h (c e) -> p h c e", c=NC)

        raw_cols = raw[:, 0, :].rearrange("p (c e) -> p c e", c=NC)

        def wrows(s):
            return slot[:, s].rearrange("p h (c e) -> p h c e", c=4)

        def kchunk(s0, c, h):
            return slot[:, s0 + c // 4, h, (c % 4) * T:(c % 4 + 1) * T]

        def vrows(s0, kt, h, dh):
            at = (kt % 2) * D + dh * HALF
            return slot[:, s0 + kt // 2, h, at:at + HALF]

        def k_rows(j):
            return qf[:, j % 2, :] if j < NC - 1 else raw[:, 1, D:D + T]

        def consumed(eng, m):
            kind, i = divmod(m, 4)
            if kind in (0, 1, 5, 6):
                eng.wait_ge(proj_ready, 8 * kind + 2 * (i + 1))
            elif i % 2:
                eng.wait_ge(proj_ready, 8 * kind + 2 * (i + 1))
            else:
                eng.wait_ge(half_used, 2 * (kind - 2) + i // 2 + 1)

        @block.sync
        def _(sp):
            def piece(par, src):
                sp.dma_start(raw[:, par, :], src).then_inc(raw_full[par], 16)

            def weight(n, w, i):
                if n >= 2:
                    sp.wait_ge(piece_lo, n - 1)
                if n == 2:
                    sp.wait_ge(half_ready, 1)
                piece(n % 2, w[i])

            for t in range(NT):
                sp.dma_start(xres[:, t, :], x_in[t * P:(t + 1) * P, :]).then_inc(x_full[t], 16)
            for i in range(2):
                weight(WQ + i, wq, i)
            sp.dma_start(bqc[:], bq).then_inc(consts_full, 16)
            sp.dma_start(bkc[:], bk).then_inc(consts_full, 16)
            sp.dma_start(tables[:, 0, :], bases).then_inc(tables_full, 16)
            sp.dma_start(tables[:, 1, :], slopes).then_inc(tables_full, 16)
            sp.dma_start(gath[:, 0:1], scale).then_inc(tables_full, 16)
            for i in range(2, 4):
                weight(WQ + i, wq, i)
            for i in range(4):
                weight(WK + i, wk, i)
            for i in range(4):
                weight(WV + i, wv, i)

            def keys(n_lo, b):
                for i in range(2):
                    sp.wait_ge(piece_lo, n_lo + i)
                    piece(i, k_in[b, i] if isinstance(b, int) else k_in[bass.ds(b, 1), i].rearrange("b p n -> (b p) n"))

            def values(n_lo, b):
                for i in range(2):
                    sp.wait_ge(piece_lo, n_lo + i)
                    piece(i, v_in[b, i] if isinstance(b, int) else v_in[bass.ds(b, 1), i].rearrange("b p n -> (b p) n"))

            keys(K0 - 1, 0)
            keys(K0 + 1, 1)
            with sp.Fori(1, NB - 1) as b:
                values(LOOP0 - 1 + 4 * (b - 1), b - 1)
                keys(LOOP0 + 1 + 4 * (b - 1), b + 1)
            values(V14 - 1, NB - 2)
            values(V15 - 1, NB - 1)
            for i in range(4):
                weight(WO + i, wo, i)
            for i in range(4):
                weight(SV + i, sv, i)
                if i == 0:
                    sp.wait_ge(t_full, T_O)
                    sp.dma_start(bvb, bv.partition_broadcast(P)).then_inc(bv_full, 16)
            for i in range(4):
                weight(SQ + i, sq, i)
            for i in range(4):
                weight(SK + i, sk, i)
            sp.wait_ge(piece_lo, SK + 4)
            sp.dma_start(gam, gamma.partition_broadcast(P)).then_inc(affine_full, 16)
            sp.dma_start(bet, beta.partition_broadcast(P)).then_inc(affine_full, 16)
            for i, hf in ((0, 0), (0, 1), (2, 0), (1, 0), (2, 1), (3, 0), (1, 1), (3, 1)):
                sp.wait_ge(tile_done[i], hf + 1)
                cols = slice(hf * HALF, (hf + 1) * HALF)
                sp.dma_start(out[i * P:(i + 1) * P, cols], xres[:, i, cols]).then_inc(stored, 16)
            sp.wait_ge(stored, 16 * 2 * NT)

        @block.gpsimd
        def _(pool):
            chain = Tally(pool, pool_step)
            chain.link(nc.gpsimd.memset(ident[:], 0.0))
            nc.gpsimd.affine_select(out=ident[:], in_=ident[:], compare_op=ALU.not_equal, fill=1.0, base=0,
                                    pattern=[[-1, P]], channel_multiplier=1).then_inc(consts_ready, 1)
            nc.gpsimd.memset(power[:], -0.5).then_inc(consts_ready, 1)

            def rsqrt(k, n):
                pool.wait_ge(ln_var, k + 1)
                nc.gpsimd.tensor_tensor(rs0[:, n:n + 1], var[:, n:n + 1], power[:], ALU.pow).then_inc(ln_pow, 1)
                pool.wait_ge(ln_pow, k + 1)

            def shift(k, n):
                rsqrt(k, n)
                a, b, c = (rsq[:, n, m:m + 1] for m in range(3))
                if k >= NT:
                    pool.wait_ge(xn_ready, NT)
                chain.link(nc.gpsimd.tensor_scalar(a, rs0[:, n:n + 1], var[:, n:n + 1], rs0[:, n:n + 1], ALU.mult,
                                                   ALU.mult))
                chain.link(nc.gpsimd.tensor_scalar(b, a, -0.5, 1.5, ALU.mult, ALU.add))
                chain.link(nc.gpsimd.tensor_tensor(c, b, rs0[:, n:n + 1], ALU.mult))
                nc.gpsimd.tensor_scalar(a, mv[:, n, 0:1], c, -1.0, ALU.mult, ALU.mult).then_inc(ln_ready, 1)
                pool.wait_ge(ln_ready, k + 1)

            pool.wait_ge(consts_ready, 2)
            for t in range(NT):
                shift(t, t)
            pool.wait_ge(piece_hi, 1)
            half = slice(P, 2 * P)
            nc.gpsimd.tensor_tensor(wcols(0)[:, 1, :, half], raw_cols[:, :, half], wcols(0)[:, 0, :, half].bitcast(F32),
                                    ALU.subtract).then_inc(half_ready, 1)
            pool.wait_ge(half_ready, 1)
            chain.link(nc.gpsimd.memset(halves[:], 0.0))
            nc.gpsimd.memset(halves[0:HD, 0:1], 1.0)
            nc.gpsimd.memset(halves[HD:P, 1:2], 1.0).then_inc(consts_ready, 1)
            pool.wait_ge(consts_ready, 3)
            for t in range(NT):
                shift(NT + t, t)
            for j in range(NC):
                pool.wait_ge(f_ready, j + 1)
                if j >= 2:
                    pool.wait_ge(norm_part, j - 1)
                nc.gpsimd.tensor_tensor(sqr[:, j % 2], qf[:, j % 2], qf[:, j % 2], ALU.mult).then_inc(sq_ready, 1)
                pool.wait_ge(sq_ready, j + 1)
            for i in range(2, 4):
                pool.wait_ge(piece_hi, SK + i + 1)
                pool.wait_ge(piece_lo, SK + i)
                nc.gpsimd.tensor_tensor(slot[:, i % 2, 1, :], raw[:, i % 2, :], slot[:, i % 2, 0, :].bitcast(F32),
                                        ALU.subtract).then_inc(piece_lo, 1)
                pool.wait_ge(piece_lo, SK + i + 1)
            consumed(pool, 26)
            chain.link(nc.gpsimd.memset(flag[:].bitcast(F32), 0.0))
            nc.gpsimd.memset(far.bitcast(F32), FAR).then_inc(far_ready, 1)
            pool.wait_ge(far_ready, 1)

            def flags(u):
                i, h = divmod(u, HEADS)
                if u == 0:
                    pool.wait_ge(local_ready, 1)
                if u >= FLAGS:
                    pool.wait_ge(hs_ready, u - FLAGS + 1)
                nc.gpsimd.tensor_scalar(flag[0:HEADS, u % FLAGS, :], local[:, i * P:(i + 1) * P].bitcast(F32),
                                        ident[0:HEADS, h:h + 1], 1.0, ALU.mult, ALU.mult).then_inc(flag_ready, 1)
                pool.wait_ge(flag_ready, u + 1)

            def affine(i):
                if i == 0:
                    pool.wait_ge(affine_full, 32)
                pool.wait_ge(xff_ready, i + 1)
                nc.gpsimd.tensor_tensor(xff, xff, gam, ALU.mult).then_inc(gamma_done, 1)
                pool.wait_ge(gamma_done, i + 1)
                nc.gpsimd.tensor_tensor(xff, xff, bet, ALU.add).then_inc(xf_ready, 1)
                pool.wait_ge(xf_ready, i + 1)

            def base(i):
                pool.wait_ge(xln_ready, i + 1)
                nc.gpsimd.tensor_tensor(xres[:, i, :], xres[:, i, :], xln, ALU.add).then_inc(base_ready, 1)
                pool.wait_ge(base_ready, i + 1)

            for u in range(AHEAD):
                flags(u)
            for i in range(NT):
                for h in range(HEADS):
                    if HEADS * i + h + AHEAD < NU:
                        flags(HEADS * i + h + AHEAD)
                    if i >= 1:
                        if h == 6:
                            rsqrt(2 * NT + 2 * (i - 1), 2 * ((i - 1) % 2))
                        if h == 7:
                            base(i - 1)
                        if h == 8:
                            rsqrt(2 * NT + 2 * (i - 1) + 1, 2 * ((i - 1) % 2) + 1)
                        if h == 9:
                            affine(i - 1)
            rsqrt(4 * NT - 2, 2 * ((NT - 1) % 2))
            base(NT - 1)
            rsqrt(4 * NT - 1, 2 * ((NT - 1) % 2) + 1)
            for i in range(2):
                pool.wait_ge(wide_ready, i + 1)
                for hf in range(2):
                    r = xres[:, i, hf * HALF:(hf + 1) * HALF]
                    nc.gpsimd.tensor_tensor(r, r, wide[i][:, hf * HALF:(hf + 1) * HALF],
                                            ALU.add).then_inc(tile_done[i], 1)
                    pool.wait_ge(tile_done[i], hf + 1)

        @block.scalar
        def _(act):
            def split(par, full, dst):
                act.wait_ge(raw_full[par], full)
                nc.scalar.copy(dst, raw[:, par, :]).then_inc(piece_hi, 1)

            def weight(n, s, used=None):
                if used is not None:
                    consumed(act, used - 1)
                split(n % 2, 16 * (n // 2 + 1), slot[:, s, 0, :])

            def natural(e, dst, t, hf, bank0=4, ring=2):
                act.wait_ge(t_full, e + 1)
                nc.scalar.copy(dst[:, 0, 4 * hf:4 * hf + 4, t * P:(t + 1) * P],
                               psum[:, (bank0 + e % ring) % 8, :].rearrange("p (c t) -> p c t", c=4)).then_inc(t_hi, 1)

            def normalise(k, t):
                act.wait_ge(ln_ready, k + 1)
                nc.scalar.activation(oacc[:, t, :], xres[:, t, :], ACT.Identity, bias=rsq[:, t, 0:1],
                                     scale=rsq[:, t, 2:3]).then_inc(xn_ready, 1)

            for t in range(NT + 1):
                if t < NT:
                    normalise(t, t)
                if t >= 1:
                    for hf in range(2):
                        natural(T_X + 2 * (t - 1) + hf, xT, t - 1, hf, 6, 8)
            act.wait_ge(piece_lo, 1)
            weight(WQ + 1, 1)

            def hi_of(a, dst):
                act.wait_ge(proj_ready, a + 1)
                nc.scalar.copy(dst, psum[:, bank_of(a), :]).then_inc(proj_hi, 1)

            for j in range(4):
                for m in range(2):
                    hi_of(A_Q + 2 * j + m, qT[:, 0, 2 * j + m, :])
                n = WQ + j + 2
                weight(n, n % 2, n - 1)
            for j in range(4):
                for m in range(2):
                    hi_of(A_K + 2 * j + m, kchunk(2, 2 * j + m, 0))
                n = WK + j + 2
                weight(n, n % 2, n - 1)

            def softmax(u, q, j, first=False):
                act.wait_ge(bias_ready, u + 1)
                if not first:
                    if q == 0:
                        act.wait_ge(t_full, T_P + 4 * j)
                        act.wait_ge(l_done, j)
                nc.scalar.activation(prob[:, q, :], psum[:, q, :], ACT.Exp, bias=nbias[:, q:q + 1], scale=X_SCALE,
                                     accum_out=rsum[:, q:q + 1]).then_inc(p_ready, 1)
                if not first and q == 0:
                    act.wait_ge(alpha_taken, j)
                nc.scalar.activation(alpha[:, q:q + 1], nprev[:, q:q + 1], ACT.Exp, bias=nbias[:, q:q + 1],
                                     scale=-1.0).then_inc(alpha_ready, 1)

            def v_self(eh, t):
                act.wait_ge(proj_ready, A_V + 4 * eh + t + 1)
                nc.scalar.copy(vrows(2, t, 0, eh), psum[:, 4 * (1 - eh) + t, :]).then_inc(proj_hi, 1)

            def turn(e, kt, dst=pT):
                act.wait_ge(t_full, e + 1)
                nc.scalar.copy(dst[:, 0, kt, :], psum[:, 4 + kt % 2, :]).then_inc(t_hi, 1)

            for q in range(NT):
                softmax(q, q, 0, first=True)
            weight(WV + 2, 0, WV + 1)
            for t in range(NT):
                v_self(0, t)
            weight(WV + 3, 1, WV + 2)
            weight(K0, 0, WV + 3)
            for t in range(NT):
                turn(T_P + t, t)
                v_self(1, t)
            weight(K0 + 1, 1, WV + 4)

            def block_step(b, v_pieces, k_next, pair, turned=False):
                if v_pieces:
                    act.wait_ge(pv_ready, 8 * b)
                    for i in range(2):
                        split(i, 16 * (pair + 1), slot[:, 2 + i, 0, :])
                if not turned:
                    for kt in range(4):
                        turn(T_P + 4 * b + kt, kt)
                for q in range(NT):
                    softmax(4 * (b + 1) + q, q, b + 1)
                if k_next:
                    act.wait_ge(s_ready, 4 * (b + 2))
                    for i in range(2):
                        split(i, 16 * (pair + (2 if v_pieces else 1)), slot[:, i, 0, :])

            block_step(0, False, True, LOOP0 // 2 - 1, turned=True)
            with act.Fori(1, NB - 1) as b:
                block_step(b, True, True, LOOP0 // 2 + 2 * (b - 1))
            block_step(NB - 1, True, False, V14 // 2)
            act.wait_ge(s_ready, 4 * (NB + 1))
            for i in range(2):
                split(i, 16 * (V15 // 2 + 1), slot[:, i, 0, :])
                for kt in range(2 * i, 2 * i + 2):
                    turn(T_P + 4 * NB + kt, kt, pT_last)
            act.wait_ge(pv_ready, 8 * NB)
            weight(WO, 2)
            weight(WO + 1, 3)
            for e in range(4):
                natural(T_O + e, oT, e, 0)
            act.wait_ge(pv_ready, 8 * (NB + 1))
            natural(T_O + 4, oT, 0, 1)
            weight(WO + 2, 0)
            natural(T_O + 5, oT, 1, 1)
            natural(T_O + 6, oT, 2, 1)
            weight(WO + 3, 1)
            natural(T_O + 7, oT, 3, 1)
            for i in range(2):
                weight(SV + i, (2 + i) % 4, 12 + i + 1)
            for t in range(NT + 1):
                if t < NT:
                    normalise(NT + t, t)
                if t >= 1:
                    for hf in range(2):
                        natural(T_Y + 2 * (t - 1) + hf, xT, t - 1, hf, 0)
            for i in range(2, 4):
                weight(SV + i, (2 + i) % 4, 12 + i + 1)

            def q_hi(j):
                act.wait_ge(f_ready, j + 1)
                nc.scalar.copy(qstack[0:HD, 2 * j, :], qf[0:HD, j % 2, :])
                nc.scalar.copy(qstack[HD:P, 2 * j + 1, :], qf[HD:P, j % 2, :]).then_inc(fh_ready, 1)

            def k_copy(j, n):
                act.wait_ge(f_ready, NC + j + 1)
                src = k_rows(j)
                if n == 0:
                    nc.scalar.copy(kstack[0:HD, 2 * j, :], src[0:HD])
                elif n == 1:
                    nc.scalar.copy(kstack[HD:P, 2 * j + 1, :], src[HD:P]).then_inc(fh_ready, 1)
                elif n == 2:
                    nc.scalar.copy(kstack[HD:P, 2 * j, :], src[0:HD])
                else:
                    nc.scalar.copy(kstack[0:HD, 2 * j + 1, :], src[HD:P]).then_inc(k_stacked, 1)

            for i in range(4):
                weight(SQ + i, (2 + i) % 4, 16 + i + 1)
            for j in range(NC):
                q_hi(j)
                if j in (5, 7):
                    weight(SK + (j - 5) // 2, (j - 5) // 2, 23 + (j - 5) // 2)
            for j in range(NC - 1):
                for n in range(4):
                    k_copy(j, n)
                if j in (1, 3):
                    weight(SK + 2 + j // 2, j // 2, 25 + j // 2)

            def head_exp(u):
                act.wait_ge(hbias_ready, u + 1)
                if u == 0:
                    act.wait_ge(local_ready, 1)
                if u in (1, 2):
                    act.wait_ge(k_stacked, NC - u)
                    act.wait_ge(proj_out, A_SK + NC - u)
                if u >= 3:
                    act.wait_ge(ht_full, u - 2)
                if u % HEADS == 0 and u >= 2 * HEADS:
                    act.wait_ge(ho_taken, 2 * (u // HEADS - 1))
                nc.scalar.activation(hprob[u % 3][:], psum[:, u % 3, :], ACT.Exp, bias=hbias[:, u % 4:u % 4 + 1],
                                     scale=S_SCALE, accum_out=hsum[:, (u // HEADS) % 2, u % HEADS:u % HEADS + 1]
                                     ).then_inc(hp_ready, 1)

            def head_turn(u):
                act.wait_ge(ht_full, u + 1)
                if u >= 2:
                    act.wait_ge(ho_ready, u - 1)
                nc.scalar.copy(hpT[:, u % 2, :], psum[:, 3, :]).then_inc(ht_out, 1)

            def sign(i):
                act.wait_ge(xf_ready, i + 1)
                nc.scalar.activation(signs, xff, ACT.Sign).then_inc(sign_ready, 1)

            def place_last():
                act.wait_ge(delta_ready, 1)
                w3 = wide[NT - 1].rearrange("p (t j) -> p t j", t=TILES)
                for j in range(SLICE):
                    ins = nc.scalar.activation(w3[:, :, j], onehot[:, NT - 1, :].bitcast(F32), ACT.Identity,
                                               scale=ubuf[:, 0, NT - 1, j:j + 1])
                ins.then_inc(wide_last, 1)

            for u in range(NU + 2):
                if u >= HEADS and u < NU and u % HEADS == 13:
                    sign(u // HEADS - 1)
                if 4 <= u < 8:
                    k_copy(NC - 1, u - 4)
                if u >= 2:
                    head_turn(u - 2)
                if u < NU:
                    head_exp(u)
                if u == 9:
                    act.wait_ge(ssign_full, 1)
                    nc.scalar.copy(ssign, psum[:, 6:8, :].rearrange("p a t -> p (a t)")).then_inc(ssign_ready, 1)
            for hf in range(2):
                cols = slice(hf * HALF, (hf + 1) * HALF)
                act.wait_ge(xf_ready, NT + hf)
                nc.scalar.activation(signs[:, cols], xff[:, cols], ACT.Sign).then_inc(sign_ready, 1)
            place_last()

        @block.vector
        def _(dve):
            chain = Tally(dve, dve_step)
            V = nc.vector

            def split_lo(n, par, dst, hi):
                dve.wait_ge(piece_hi, n + 1)
                V.tensor_tensor(dst, raw[:, par, :], hi.bitcast(F32), ALU.subtract).then_inc(piece_lo, 1)

            def weight(n, s):
                split_lo(n, n % 2, slot[:, s, 1, :], slot[:, s, 0, :])

            def half_stats(src, n, g):
                V.bn_stats(stat[:, n, g, :], src[:, g * HALF:(g + 1) * HALF]).then_inc(dve_step, 1)
                chain.n += 1

            def variance(n):
                dve.wait_ge(dve_step, chain.n)
                chain.link(V.bn_aggr(mv[:, n, :], stat[:, n].rearrange("p g s -> p (g s)")))
                V.tensor_scalar(var[:, n:n + 1], mv[:, n, 1:2], EPS, None, ALU.add).then_inc(ln_var, 1)

            def stats(src, n):
                for g in range(2):
                    half_stats(src, n, g)
                variance(n)

            def root(k, n):
                dve.wait_ge(ln_pow, k + 1)
                a, b, c = (rsq[:, n, m:m + 1] for m in range(3))
                chain.link(V.scalar_tensor_tensor(out=a, in0=rs0[:, n:n + 1], scalar=var[:, n:n + 1],
                                                  in1=rs0[:, n:n + 1], op0=ALU.mult, op1=ALU.mult))
                chain.link(V.tensor_scalar(b, a, -0.5, 1.5, ALU.mult, ALU.add))
                chain.link(V.tensor_tensor(c, b, rs0[:, n:n + 1], ALU.mult))
                return c

            def normalise(src, dst, k, n, done):
                c = root(k, n)
                V.tensor_scalar(dst, src, mv[:, n, 0:1], c, ALU.subtract, ALU.mult).then_inc(done, 1)

            def natural(e, dst, t, hf, bank0=4, ring=2):
                dve.wait_ge(t_hi, e + 1)
                at = (4 * hf, 4 * hf + 4)
                V.tensor_tensor(dst[:, 1, at[0]:at[1], t * P:(t + 1) * P],
                                psum[:, (bank0 + e % ring) % 8, :].rearrange("p (c t) -> p c t", c=4),
                                dst[:, 0, at[0]:at[1], t * P:(t + 1) * P].bitcast(F32),
                                ALU.subtract).then_inc(t_lo, 1)

            V.memset(nbias[:], BIG)
            V.memset(lsum[:], 0.0)
            for g in range(GRID):
                V.memset(steps[:, g:g + 1], float(g))
            V.memset(oacc[:, :, :].rearrange("p a b -> p (a b)")[:, 0:1], 0.0).then_inc(state_zero, 1)
            dve.wait_ge(state_zero, 1)
            for t in range(NT):
                dve.wait_ge(x_full[t], 16)
                stats(xres[:, t, :], t)
            dve.wait_ge(raw_full[0], 16)
            V.tensor_copy(slot[:, 0, 0, :], raw[:, 0, :]).then_inc(piece_hi, 1)
            dve.wait_ge(piece_hi, 1)
            half = slice(0, P)
            V.tensor_tensor(wcols(0)[:, 1, :, half], raw_cols[:, :, half], wcols(0)[:, 0, :, half].bitcast(F32),
                            ALU.subtract).then_inc(piece_lo, 1)
            for t in range(NT):
                for hf in range(2):
                    natural(T_X + 2 * t + hf, xT, t, hf, 6, 8)
            weight(WQ + 1, 1)

            def lo_of(a, dst, hi):
                dve.wait_ge(proj_hi, a + 1)
                V.tensor_tensor(dst, psum[:, bank_of(a), :], hi.bitcast(F32), ALU.subtract).then_inc(proj_out, 1)

            for j in range(4):
                for m in range(2):
                    lo_of(A_Q + 2 * j + m, qT[:, 1, 2 * j + m, :], qT[:, 0, 2 * j + m, :])
                weight(WQ + j + 2, j % 2)
            dve.wait_ge(t_full, T_X + 8)
            V.memset(oacc[:], 0.0).then_inc(state_zero, 1)
            for j in range(4):
                for m in range(2):
                    lo_of(A_K + 2 * j + m, kchunk(2, 2 * j + m, 1), kchunk(2, 2 * j + m, 0))
                weight(WK + j + 2, j % 2)

            def row_bias(u, q, j, first=False):
                dve.wait_ge(s_ready, u + 1)
                V.tensor_reduce(rmax[:, q:q + 1], psum[:, q, :], X, ALU.max).then_inc(row_max, 1)
                if not first:
                    dve.wait_ge(alpha_ready, 4 * j + q - 3)
                V.tensor_copy(nprev[:, q:q + 1], nbias[:, q:q + 1]).then_inc(prev_kept, 1)
                dve.wait_ge(prev_kept, u + 1)
                dve.wait_ge(row_max, u + 1)
                V.tensor_scalar(nbias[:, q:q + 1], rmax[:, q:q + 1], -X_SCALE, nbias[:, q:q + 1], ALU.mult,
                                ALU.min).then_inc(bias_ready, 1)

            def row_sums(j):
                dve.wait_ge(alpha_ready, 4 * (j + 1))
                V.tensor_tensor(lsum[:], lsum[:], alpha[:], ALU.mult).then_inc(l_scaled, 1)
                dve.wait_ge(l_scaled, j + 1)
                V.tensor_tensor(lsum[:], lsum[:], rsum[:], ALU.add).then_inc(l_done, 1)

            def v_self(eh, t):
                dve.wait_ge(proj_hi, A_V + 4 * eh + t + 1)
                V.tensor_tensor(vrows(2, t, 1, eh), psum[:, 4 * (1 - eh) + t, :], vrows(2, t, 0, eh).bitcast(F32),
                                ALU.subtract).then_inc(proj_out, 1)

            def out_add(j, g):
                dh, q = divmod(g, NT)
                dve.wait_ge(pv_ready, 8 * j + g + 1)
                o = oacc[:, q, dh * HALF:(dh + 1) * HALF]
                V.scalar_tensor_tensor(out=o, in0=o, scalar=alpha_o[:, q:q + 1], in1=psum[:, 6 + g % 2, :],
                                       op0=ALU.mult, op1=ALU.add).then_inc(o_done, 1)

            def turn_lo(e, kt, dst=pT):
                dve.wait_ge(t_hi, e + 1)
                V.tensor_tensor(dst[:, 1, kt, :], psum[:, 4 + kt % 2, :], dst[:, 0, kt, :].bitcast(F32),
                                ALU.subtract).then_inc(t_lo, 1)

            def take_alpha(j, first=False):
                dve.wait_ge(alpha_ready, 4 * (j + 1))
                if not first:
                    dve.wait_ge(o_done, 8 * j)
                V.tensor_copy(alpha_o[:], alpha[:]).then_inc(alpha_taken, 1)

            def split_keys(n, s):
                split_lo(n, s, slot[:, s, 1, :], slot[:, s, 0, :])

            for q in range(NT):
                row_bias(q, q, 0, first=True)
            weight(WV + 2, 0)
            row_sums(0)
            for t in range(NT):
                v_self(0, t)
            weight(WV + 3, 1)
            weight(K0, 0)
            for t in range(NT):
                turn_lo(T_P + t, t)
                v_self(1, t)
            take_alpha(0, first=True)
            dve.wait_ge(alpha_taken, 1)
            out_add(0, 0)
            weight(K0 + 1, 1)
            for g in range(1, 4):
                out_add(0, g)
            for q in range(NT):
                row_bias(4 + q, q, 1)
            for g in range(4, 8):
                if g == 5:
                    row_sums(1)
                if g in (5, 6):
                    split_keys(K0 + 2 + g - 5, g - 5)
                out_add(0, g)

            def block_scores(b, n_v):
                take_alpha(b)
                for i in range(2):
                    split_lo(n_v + i, i, slot[:, 2 + i, 1, :], slot[:, 2 + i, 0, :])
                row_bias(4 * (b + 1), 0, b + 1)
                turn_lo(T_P + 4 * b, 0)
                turn_lo(T_P + 4 * b + 1, 1)
                row_bias(4 * (b + 1) + 1, 1, b + 1)
                turn_lo(T_P + 4 * b + 2, 2)
                turn_lo(T_P + 4 * b + 3, 3)
                row_bias(4 * (b + 1) + 2, 2, b + 1)
                row_bias(4 * (b + 1) + 3, 3, b + 1)
                dve.wait_ge(alpha_taken, b + 1)

            with dve.Fori(1, NB - 1) as b:
                block_scores(b, LOOP0 + 4 * (b - 1))
                for g in range(8):
                    if g in (1, 3):
                        split_keys(LOOP0 + 4 * (b - 1) + 2 + g // 2, g // 2)
                    if g == 4:
                        row_sums(b + 1)
                    out_add(b, g)
            block_scores(NB - 1, V14)
            for g in range(8):
                out_add(NB - 1, g)
                if g in (0, 2):
                    split_keys(V15 + g // 2, g // 2)
                if g in LAST_TURNS:
                    kt = LAST_TURNS.index(g)
                    turn_lo(T_P + 4 * NB + kt, kt, pT_last)
                if g == 5:
                    row_sums(NB)
            take_alpha(NB)
            dve.wait_ge(alpha_taken, NB + 1)
            dve.wait_ge(l_done, NB + 1)
            chain.link(V.reciprocal(linv[:], lsum[:]))
            for g in range(8):
                out_add(NB, g)
                if g in (0, 2):
                    weight(WO + g // 2, 2 + g // 2)
                if g >= 5:
                    natural(T_O + g - 5, oT, g - 5, 0)
            natural(T_O + 3, oT, 3, 0)
            natural(T_O + 4, oT, 0, 1)
            weight(WO + 2, 0)
            natural(T_O + 5, oT, 1, 1)
            natural(T_O + 6, oT, 2, 1)
            weight(WO + 3, 1)
            natural(T_O + 7, oT, 3, 1)

            def residual(eh, t):
                dve.wait_ge(proj_ready, A_O + 4 * eh + t + 1)
                r = xres[:, t, eh * HALF:(eh + 1) * HALF]
                V.scalar_tensor_tensor(out=r, in0=psum[:, 4 * eh + t, :], scalar=linv[:, t:t + 1], in1=r,
                                       op0=ALU.mult, op1=ALU.add).then_inc(proj_out, 1)

            for t in range(NT):
                residual(0, t)
            dve.wait_ge(proj_out, A_O + NT)
            for t in range(NT):
                half_stats(xres[:, t, :], t, 0)
            for i in range(2):
                weight(SV + i, (2 + i) % 4)
            dve.wait_ge(t_full, T_Y)
            for t in range(NT + 2):
                if t < NT:
                    residual(1, t)
                    dve.wait_ge(proj_out, A_O + 4 + t + 1)
                    half_stats(xres[:, t, :], t, 1)
                    variance(t)
                if t >= 2:
                    for hf in range(2):
                        natural(T_Y + 2 * (t - 2) + hf, xT, t - 2, hf, 0)
            for i in range(2, 4):
                weight(SV + i, (2 + i) % 4)
            dve.wait_ge(tables_full, 48)
            chain.link(V.tensor_reduce(slo[:, 0, :], tables[:, 1, :].rearrange("p (j g) -> p j g", j=SLICE), X,
                                       ALU.add))
            V.tensor_scalar(slo[:, 1, :], slo[:, 0, :], 0.0, None, ALU.is_gt)
            chain.link(V.tensor_scalar(slo[:, 2, :], slo[:, 0, :], 0.0, None, ALU.is_lt))
            chain.link(V.tensor_tensor(slo[:, 1, :], slo[:, 1, :], slo[:, 2, :], ALU.subtract))
            dve.wait_ge(bv_full, 16)

            def values(eh, t):
                dve.wait_ge(proj_ready, A_SV + 4 * eh + t + 1)
                V.tensor_tensor(val[:, t, eh * HALF:(eh + 1) * HALF], psum[:, 4 * (1 - eh) + t, :],
                                bvb[:, eh * HALF:(eh + 1) * HALF], ALU.add).then_inc(proj_out, 1)

            for t in range(NT):
                values(0, t)
            for i in range(3):
                weight(SQ + i, (2 + i) % 4)
            for t in range(NT):
                values(1, t)
            dve.wait_ge(proj_out, A_SQ)
            weight(SQ + 3, 1)

            def biased(j, a, bias, dst):
                dve.wait_ge(proj_ready, a + 1)
                if 2 <= j < NC + 2:
                    dve.wait_ge(fh_ready, j - 1)
                    dve.wait_ge(sq_ready, j - 1)
                elif j >= NC + 2:
                    dve.wait_ge(k_stacked, j - NC - 1)
                V.tensor_scalar(dst, psum[:, 6 + j % 2, :], bias, None,
                                ALU.add).then_inc(f_ready, 1)
                dve.wait_ge(f_ready, j + 1)

            def q_lo(j):
                biased(j, A_SQ + j, bqc[:, j:j + 1], qf[:, j % 2, :])
                dve.wait_ge(fh_ready, j + 1)
                V.tensor_tensor(qstack[HD:P, 2 * j, :], qf[0:HD, j % 2, :], qstack[0:HD, 2 * j, :].bitcast(F32),
                                ALU.subtract)
                V.tensor_tensor(qstack[0:HD, 2 * j + 1, :], qf[HD:P, j % 2, :],
                                qstack[HD:P, 2 * j + 1, :].bitcast(F32), ALU.subtract).then_inc(proj_out, 1)

            def k_bias(j):
                if j == NC - 1:
                    dve.wait_ge(piece_lo, SK + 4)
                biased(NC + j, A_SK + j, bkc[:, j:j + 1], k_rows(j))

            def k_rest(j, n):
                dve.wait_ge(fh_ready, NC + j + 1)
                rows = slice(n * HD, (n + 1) * HD)
                ins = V.tensor_tensor(klo[rows, j, :], k_rows(j)[rows], kstack[rows, 2 * j + n, :].bitcast(F32),
                                      ALU.subtract)
                if n == 1:
                    ins.then_inc(proj_out, 1)

            dve.wait_ge(consts_full, 32)
            for j in range(NC):
                q_lo(j)
                if j in (5, 7):
                    weight(SK + (j - 5) // 2, (j - 5) // 2)

            def top_round(r):
                chain.link(V.max(out=top8[:], in_=norms))
                if (r + 1) * 8 > TOPK:
                    chain.link(V.memset(top8[:, TOPK - 8 * r:8], -1.0))
                chain.link(V.match_replace(out=norms, in_to_replace=top8[:], in_values=norms, imm_value=-1.0))

            rounds = {2: ((1,), (2,)), 3: ((3,), (4,)), 4: ((5,), (6,)), 5: ((7,), ())}
            for j in range(NC - 1):
                k_bias(j)
                if j == 0:
                    dve.wait_ge(norm_part, NC)
                    V.tensor_copy(tsc[:], psum[:, 2, 0:NT * HEADS]).then_inc(norms_kept, 1)
                for r in rounds.get(j, ((), ()))[0]:
                    top_round(r)
                if j == 5:
                    V.memset(norms[:, 0:1], -1.0)
                    chain.link(V.memset(norms[:, T - 1:T], -1.0))
                    consumed(dve, 26)
                    V.tensor_scalar(local, norms, -1.0, None, ALU.not_equal).then_inc(local_ready, 1)
                for n in range(2):
                    k_rest(j, n)
                if j == 1:
                    dve.wait_ge(norms_turned, 1)
                    chain.link(V.tensor_copy(norms, psum[0:HEADS, 3, :]))
                    top_round(0)
                for r in rounds.get(j, ((), ()))[1]:
                    top_round(r)

            def slope_signs():
                consumed(dve, 27)
                V.tensor_tensor(spread.rearrange("p (t j) -> p t j", t=TILES),
                                ident[0:TILES, 0:TILES].unsqueeze(2).to_broadcast([TILES, TILES, SLICE]),
                                slo[:, 1, :].unsqueeze(1).to_broadcast([TILES, TILES, SLICE]), ALU.mult)
                V.tensor_scalar(ones, ident[0:TILES, :], 0.0, 1.0, ALU.mult, ALU.add).then_inc(spread_ready, 1)

            def head_bias(u):
                dve.wait_ge(hs_ready, u + 1)
                chain.link(V.tensor_reduce(hmax[:, u % 2:u % 2 + 1], psum[:, u % 3, :], X, ALU.max))
                if u >= 4:
                    dve.wait_ge(hp_ready, u - 3)
                V.tensor_scalar(hbias[:, u % 4:u % 4 + 1], hmax[:, u % 2:u % 2 + 1], -S_SCALE, None,
                                ALU.mult).then_inc(hbias_ready, 1)

            def heads_over(i, hf):
                dve.wait_ge(ho_ready, HEADS * i + 8 * hf + 8)
                chain.link(V.reciprocal(hinv[:], hsum[:, i % 2, 8 * hf:8 * hf + 8]))
                if hf == 0 and i >= 1:
                    dve.wait_ge(base_ready, i)
                V.tensor_tensor(over.rearrange("p (h d) -> p h d", h=8),
                                psum[:, 4 + 2 * (i % 2) + hf, :].rearrange("p (h d) -> p h d", h=8),
                                hinv[:].unsqueeze(2).to_broadcast([P, 8, HD]), ALU.mult).then_inc(ho_taken, 1)

            def heads_add(i, hf):
                dve.wait_ge(ho_taken, 2 * i + hf + 1)
                r = xres[:, i, hf * HALF:(hf + 1) * HALF]
                chain.link(V.tensor_tensor(r, r, over, ALU.add))

            def route(i, step):
                k = 2 * NT + 2 * i
                oh = onehot[:, i, :]
                oh32 = oh.bitcast(F32)
                tiles3 = [P, TILES, SLICE]
                n = 2 * (i % 2)
                if step == 0:
                    half_stats(xres[:, i, :], n, 0)
                elif step == 1:
                    half_stats(xres[:, i, :], n, 1)
                    variance(n)
                elif step == 2:
                    normalise(xres[:, i, :], xln, k, n, xln_ready)
                elif step == 3:
                    dve.wait_ge(xln_ready, i + 1)
                    stats(xln, n + 1)
                elif step == 4:
                    normalise(xln, xff, k + 1, n + 1, xff_ready)
                elif step == 5:
                    dve.wait_ge(affine_full, 32)
                    c = root(k + 1, n + 1)
                    done = chain.n
                    for hf in range(2):
                        cols = slice(hf * HALF, (hf + 1) * HALF)
                        V.scalar_tensor_tensor(out=xff[:, cols], in0=xln[:, cols], scalar=mv[:, n + 1, 0:1],
                                               in1=gam[:, cols], op0=ALU.subtract, op1=ALU.mult).then_inc(dve_step, 1)
                        chain.n += 1
                    for hf in range(2):
                        cols = slice(hf * HALF, (hf + 1) * HALF)
                        dve.wait_ge(dve_step, done + hf + 1)
                        V.scalar_tensor_tensor(out=xff[:, cols], in0=xff[:, cols], scalar=c, in1=bet[:, cols],
                                               op0=ALU.mult, op1=ALU.add).then_inc(xf_ready, 1)
                elif step == 6:
                    if i == NT - 1:
                        for hf in range(2):
                            cols = slice(hf * HALF, (hf + 1) * HALF)
                            dve.wait_ge(sign_ready, NT + hf)
                            V.tensor_tensor(signs[:, cols], signs[:, cols].bitcast(F32), ssign[:, cols].bitcast(F32),
                                            ALU.mult).then_inc(dve_step, 1)
                            chain.n += 1
                        dve.wait_ge(dve_step, chain.n)
                        return
                    dve.wait_ge(sign_ready, i + 1)
                    if i == 0:
                        dve.wait_ge(ssign_ready, 1)
                    chain.link(V.tensor_tensor(signs, signs.bitcast(F32), ssign.bitcast(F32), ALU.mult))
                elif step == 7:
                    chain.link(V.tensor_reduce(tsc[:], signs.bitcast(F32).rearrange("p (t j) -> p t j", t=TILES), X,
                                               ALU.add))
                elif step == 8:
                    c1, c2, c3 = (csc[:, CLUSTERS * n:CLUSTERS * (n + 1)] for n in range(3))
                    chain.link(V.tensor_reduce(c1, tsc[:].rearrange("p (c t) -> p c t", c=CLUSTERS), X, ALU.add))
                    chain.link(V.scalar_tensor_tensor(out=c2, in0=c1, scalar=8.0, in1=steps[:, 0:CLUSTERS],
                                                      op0=ALU.mult, op1=ALU.subtract))
                    chain.link(V.tensor_reduce(small[:, 0:1], c2, X, ALU.max))
                    chain.link(V.tensor_scalar(c3, c2, small[:, 0:1], BOOST, ALU.is_equal, ALU.mult))
                elif step == 9:
                    c3 = csc[:, 2 * CLUSTERS:3 * CLUSTERS]
                    t3 = tsc[:].rearrange("p (c t) -> p c t", c=CLUSTERS)
                    chain.link(V.scalar_tensor_tensor(
                        out=t3, in0=t3, scalar=8.0,
                        in1=steps[:, 0:8].unsqueeze(1).to_broadcast([P, CLUSTERS, 8]), op0=ALU.mult,
                        op1=ALU.subtract))
                    chain.link(V.tensor_tensor(t3, t3, c3.unsqueeze(2).to_broadcast([P, CLUSTERS, 8]), ALU.add))
                    chain.link(V.tensor_reduce(small[:, 1:2], tsc[:], X, ALU.max))
                    chain.link(V.tensor_scalar(oh, tsc[:], small[:, 1:2], None, ALU.is_equal))
                elif step == 10:
                    x3 = xff.rearrange("p (t j) -> p t j", t=TILES)
                    chain.link(V.tensor_tensor(x3, x3, oh32.unsqueeze(2).to_broadcast(tiles3), ALU.mult))
                elif step == 11:
                    chain.link(V.tensor_reduce(xs[:, i, :], xff.rearrange("p (t j) -> p j t", t=TILES), X, ALU.add))
                elif step == 12:
                    V.tensor_reduce(small[:, 2:3], xs[:, i, :], X, ALU.min)
                    V.tensor_reduce(small[:, 3:4], xs[:, i, :], X, ALU.max)
                    if i >= 1:
                        dve.wait_ge(mm_full, i)
                    chain.link(V.tensor_scalar(tsc[:], oh32, -BIG, BIG, ALU.mult, ALU.add))
                    V.scalar_tensor_tensor(out=mmx[:, 0, :], in0=oh32, scalar=small[:, 2:3], in1=tsc[:],
                                           op0=ALU.mult, op1=ALU.add)
                    V.scalar_tensor_tensor(out=mmx[:, 1, :], in0=oh32, scalar=small[:, 3:4], in1=tsc[:],
                                           op0=ALU.mult, op1=ALU.subtract).then_inc(mm_ready, 1)

            def extremes(i):
                dve.wait_ge(mm_full, i + 1)
                bank = psum[0:TILES, turn_bank(i), :]
                V.tensor_reduce(tmm[:, 0, i:i + 1], bank[:, P:2 * P], X, ALU.min)
                V.tensor_reduce(tmm[:, 1, i:i + 1], bank[:, 2 * P:3 * P], X, ALU.max)
                V.tensor_copy(ohT[:, i, :], bank[:, 0:P]).then_inc(mm_taken, 1)

            beside = {6: (1,), 7: (2,), 8: (3,), 9: (4,), 14: (6,), 15: (7,)}
            beside_later = {0: (8, 9), 1: (10,), 2: (11,), 3: (12,)}
            for u in range(NU):
                i, h = divmod(u, HEADS)
                head_bias(u)
                if u == 2:
                    k_bias(NC - 1)
                if u in (8, 9):
                    k_rest(NC - 1, u - 8)
                if u == 3:
                    slope_signs()
                if h == 11:
                    heads_over(i, 0)
                if h == 12:
                    heads_add(i, 0)
                if h == 13:
                    route(i, 0)
                if i >= 1:
                    if h == 4:
                        heads_over(i - 1, 1)
                    if h == 5:
                        heads_add(i - 1, 1)
                    for step in beside.get(h, ()):
                        route(i - 1, step)
                if i >= 2:
                    for step in beside_later.get(h, ()):
                        route(i - 2, step)
                    if h == 8:
                        extremes(i - 2)
            for step in (8, 9, 10):
                route(NT - 2, step)
            heads_over(NT - 1, 1)
            heads_add(NT - 1, 1)
            for tile, step in ((-1, 1), (-2, 11), (-1, 2), (-1, 3), (-2, 12), (-1, 5)):
                route(NT + tile, step)
            extremes(NT - 2)
            for step in range(6, 13):
                route(NT - 1, step)
            extremes(NT - 1)
            dve.wait_ge(mm_taken, NT)
            V.tensor_reduce(gath[:, 1:2], tmm[:, 0, :], X, ALU.min)
            V.tensor_reduce(gath[:, 2:3], tmm[:, 1, :], X, ALU.max).then_inc(gath_ready, 1)

            dve.wait_ge(picked, NT)
            chain.link(V.tensor_copy(got[:, :, 0:3], psum[:, 4, 0:4 * NT].rearrange("p (i n) -> p i n", n=4)[:, :, 0:3]))
            sc, lo, hi = (got[:, :, n] for n in range(3))
            u, n16 = ubuf[:, 0], ubuf[:, 1]
            wide_in = [P, NT, SLICE]
            chain.link(V.tensor_tensor(rec[:, 0, :], hi, lo, ALU.subtract))
            chain.link(V.tensor_scalar(rec[:, 0, :], rec[:, 0, :], 1e-8, None, ALU.add))
            chain.link(V.reciprocal(rec[:, 1, :], rec[:, 0, :]))
            chain.link(V.tensor_tensor(u, xs[:], lo.unsqueeze(2).to_broadcast(wide_in), ALU.subtract))
            chain.link(V.tensor_tensor(u, u, rec[:, 1, :].unsqueeze(2).to_broadcast(wide_in), ALU.mult))
            chain.link(V.tensor_scalar(u, u, 0.0, 1.0 - 1e-6, ALU.max, ALU.min))
            chain.link(V.tensor_scalar(n16, u, float(GRID), None, ALU.mult))
            dve.wait_ge(rows_picked, NT)
            entries = psum[:, 0:NT, :].rearrange("p i (s j g) -> p s i j g", s=2, g=GRID)
            width = GRID // 2
            while width:
                bit = ubuf[:, 2]
                chain.link(V.tensor_scalar(bit, n16, float(width), None, ALU.is_ge))
                mask = bit.bitcast(mybir.dt.uint32).unsqueeze(3).to_broadcast([P, NT, SLICE, width])
                for table in range(2):
                    V.copy_predicated(entries[:, table, :, :, 0:width], mask,
                                      entries[:, table, :, :, width:2 * width]).then_inc(dve_step, 1)
                    chain.n += 1
                chain.link(V.scalar_tensor_tensor(out=n16, in0=bit, scalar=-float(width), in1=n16, op0=ALU.mult,
                                                  op1=ALU.add))
                width //= 2
            chain.link(V.tensor_tensor(u, entries[:, 1, :, :, 0], n16, ALU.mult))
            chain.link(V.tensor_tensor(u, entries[:, 0, :, :, 0], u, ALU.add))
            V.tensor_tensor(u, u, sc.unsqueeze(2).to_broadcast(wide_in), ALU.mult).then_inc(delta_ready, 1)
            dve.wait_ge(delta_ready, 1)

            for i in range(NT - 1):
                t3 = [P, TILES, SLICE]
                V.tensor_tensor(wide[i].rearrange("p (t j) -> p t j", t=TILES),
                                onehot[:, i, :].bitcast(F32).unsqueeze(2).to_broadcast(t3),
                                u[:, i, :].unsqueeze(1).to_broadcast(t3), ALU.mult).then_inc(wide_ready, 1)
            for i in (NT - 2, NT - 1):
                if i == NT - 1:
                    dve.wait_ge(wide_last, 1)
                else:
                    dve.wait_ge(wide_ready, NT - 1)
                for hf in range(2):
                    r = xres[:, i, hf * HALF:(hf + 1) * HALF]
                    V.tensor_tensor(r, r, wide[i][:, hf * HALF:(hf + 1) * HALF], ALU.add).then_inc(tile_done[i], 1)

        @block.tensor
        def _(pe):
            def mm3(dst, st, mov, first, last):
                for n, (a, c) in enumerate(((0, 0), (0, 1), (1, 0))):
                    ins = nc.tensor.matmul(dst, st(a), mov(c), start=first and n == 0, stop=last and n == 2)
                return ins

            def natural(e, src, t, hf, bank0=4, ring=2):
                if ring == 2:
                    pe.wait_ge(t_lo, e - 1)
                for c in range(4):
                    at = (4 * hf + c) * P
                    ins = nc.tensor.transpose(psum[:, (bank0 + e % ring) % 8, c * P:(c + 1) * P], src[:, t, at:at + P],
                                              ident[:])
                ins.then_inc(t_full, 1)

            pe.wait_ge(consts_ready, 1)
            for t in range(NT):
                pe.wait_ge(xn_ready, t + 1)
                for hf in range(2):
                    natural(T_X + 2 * t + hf, oacc, t, hf, 6, 8)

            def columns(n, s, a0, free, side=None, amid=None):
                pe.wait_ge(piece_lo, n + 1)
                w = wcols(s)
                for m in range(2):
                    a = a0 + m
                    free(a)
                    if a == A_Q + 1:
                        pe.wait_ge(half_ready, 1)
                    if a == A_Q:
                        pe.wait_ge(t_lo, T_X + 2)
                        for c in range(NC):
                            for h in range(2):
                                nc.tensor.matmul(psum[:, bank_of(a), :], w[:, h, c, 0:P], xT[:, 0, c, :],
                                                 start=(c == 0 and h == 0), stop=False)
                        pe.wait_ge(t_lo, T_X + 8)
                        for c in range(NC):
                            ins = nc.tensor.matmul(psum[:, bank_of(a), :], w[:, 0, c, 0:P], xT[:, 1, c, :],
                                                   start=False, stop=(c == NC - 1))
                        ins.then_inc(proj_ready, 1)
                        continue
                    for c in range(NC):
                        if amid and c == NC // 2:
                            amid(a)
                        ins = mm3(psum[:, bank_of(a), :], lambda h: w[:, h, c, m * P:(m + 1) * P],
                                  lambda h: xT[:, h, c, :], c == 0, c == NC - 1)
                    ins.then_inc(proj_ready, 1)
                    if side:
                        side(a)

            def rows(n, s, dh, bank0, src, ready):
                pe.wait_ge(piece_lo, n + 1)
                w = wrows(s)
                for t in range(NT):
                    ready(t)
                    for c in range(4):
                        if n == WO + 3 and t == NT - 1 and c == 3:
                            y_turn(0)
                        ins = mm3(psum[:, bank0 + t, :], lambda h: src[:, h, 4 * dh + c, t * P:(t + 1) * P],
                                  lambda h: w[:, h, c, :], dh == 0 and c == 0, dh == 1 and c == 3)
                    if dh == 1:
                        ins.then_inc(proj_ready, 1)
                if dh == 0:
                    ins.then_inc(half_used, 1)

            pe.wait_ge(t_hi, T_X + 8)
            for j in range(4):
                columns(WQ + j, j % 2, A_Q + 2 * j, lambda a: pe.wait_ge(proj_out, a - 1) if a >= 2 else None)
            for j in range(4):
                columns(WK + j, j % 2, A_K + 2 * j, lambda a: pe.wait_ge(proj_out, a - 1))

            def scores(u, q, s0):
                for c in range(NC):
                    ins = mm3(psum[:, q, :], lambda h: qT[:, h, c, q * P:(q + 1) * P], lambda h: kchunk(s0, c, h),
                              c == 0, c == NC - 1)
                ins.then_inc(s_ready, 1)

            def own_values(t, eh, dh):
                if eh == 0 and dh == 0 and t == 2:
                    pe.wait_ge(proj_out, A_V)
                if eh == 1 and dh == 0:
                    pe.wait_ge(p_ready, t + 1)
                if eh == 1 and dh == 1:
                    turn(T_P + t, t)

            def turn(e, kt):
                pe.wait_ge(t_lo, e - 1)
                for q in range(NT):
                    ins = nc.tensor.transpose(psum[:, 4 + kt % 2, q * P:(q + 1) * P],
                                              prob[:, q, kt * P:(kt + 1) * P], ident[:])
                ins.then_inc(t_full, 1)

            rows(WV, 0, 0, 4, xT, lambda t: own_values(t, 0, 0))
            pe.wait_ge(proj_out, A_V)
            for q in range(NT):
                scores(q, q, 2)
            rows(WV + 1, 1, 1, 4, xT, lambda t: None)
            rows(WV + 2, 0, 0, 0, xT, lambda t: own_values(t, 1, 0))
            pe.wait_ge(proj_out, A_V + 4)
            rows(WV + 3, 1, 1, 0, xT, lambda t: own_values(t, 1, 1))

            def with_values(j, g, s0, free, src=pT):
                dh, q = divmod(g, NT)
                if free is not None:
                    pe.wait_ge(o_done, free)
                for kt in range(4):
                    ins = mm3(psum[:, 6 + g % 2, :], lambda h: src[:, h, kt, q * P:(q + 1) * P],
                              lambda h: vrows(s0, kt, h, dh), kt == 0, kt == 3)
                ins.then_inc(pv_ready, 1)

            pe.wait_ge(t_lo, T_P + 4)
            for g in range(4):
                with_values(0, g, 2, g - 1 if g >= 2 else None)
            for q in range(NT):
                pe.wait_ge(piece_lo, K0 + 2)
                pe.wait_ge(proj_out, A_V + 4 + q + 1)
                scores(4 + q, q, 0)
            for g in range(4, 8):
                with_values(0, g, 2, g - 1)

            def block_scores(b, keys_lo):
                pe.wait_ge(piece_lo, keys_lo)
                for q in range(NT):
                    pe.wait_ge(p_ready, 4 * b + q + 1)
                    scores(4 * (b + 1) + q, q, 0)
                    if q < 2:
                        if q == 0:
                            pe.wait_ge(p_ready, 4 * (b + 1))
                        turn(T_P + 4 * b + 2 * q, 2 * q)
                        turn(T_P + 4 * b + 2 * q + 1, 2 * q + 1)
                pe.wait_ge(t_lo, T_P + 4 * (b + 1))

            with pe.Fori(1, NB - 1) as b:
                block_scores(b, LOOP0 + 4 * (b - 1))
                pe.wait_ge(piece_lo, LOOP0 + 4 * (b - 1) + 2)
                for g in range(8):
                    with_values(b, g, 2, 8 * b + g - 1)
            block_scores(NB - 1, V14)
            pe.wait_ge(piece_lo, V14 + 2)
            for g in range(8):
                with_values(NB - 1, g, 2, 8 * (NB - 1) + g - 1)
                if g in LAST_TURNS:
                    kt = LAST_TURNS.index(g)
                    if kt == 0:
                        pe.wait_ge(p_ready, 4 * (NB + 1))
                    turn(T_P + 4 * NB + kt, kt)
            pe.wait_ge(t_lo, T_P + 4 * (NB + 1))
            pe.wait_ge(piece_lo, V15 + 2)
            for g in range(8):
                with_values(NB, g, 0, 8 * NB + g - 1, pT_last)
                if g >= 4:
                    pe.wait_ge(o_done, 8 * NB + g - 3)
                    natural(T_O + g - 4, oacc, g - 4, 0)

            def wo_ready(t, eh, dh):
                if eh == 0 and dh == 0:
                    pe.wait_ge(t_lo, T_O + t + 1)
                    if t >= 1:
                        q = t - 1
                        pe.wait_ge(o_done, 8 * NB + 4 + q + 1)
                        natural(T_O + 4 + q, oacc, q, 1)
                if eh == 0 and dh == 1 and t == 0:
                    pe.wait_ge(o_done, 8 * NB + 8)
                    natural(T_O + 7, oacc, 3, 1)
                if eh == 0 and dh == 1:
                    pe.wait_ge(t_lo, T_O + 5 + t)
                if eh == 1 and dh == 0 and t == 0:
                    pe.wait_ge(t_lo, T_Y)
                    pe.wait_ge(o_done, 8 * (NB + 1))

            def y_turn(t):
                pe.wait_ge(xn_ready, NT + t + 1)
                if t == 0:
                    pe.wait_ge(proj_out, A_O + 4)
                for hf in range(2):
                    natural(T_Y + 2 * t + hf, oacc, t, hf, 0)

            for eh in range(2):
                for dh in range(2):
                    i = 2 * eh + dh
                    rows(WO + i, (2 + i) % 4, dh, 4 * eh, oT, lambda t: wo_ready(t, eh, dh))

            def sv_ready(t, eh, dh):
                if eh == 0 and dh == 0:
                    if t < 3:
                        y_turn(t + 1)
                    pe.wait_ge(t_lo, T_Y + 2 * t + 2)
                    pe.wait_ge(proj_out, A_O + 4 + t + 1)

            for eh in range(2):
                for dh in range(2):
                    i = 2 * eh + dh
                    rows(SV + i, (2 + i) % 4, dh, 4 * (1 - eh), xT, lambda t: sv_ready(t, eh, dh))

            def norm(j):
                pe.wait_ge(sq_ready, j + 1)
                if j == 0:
                    pe.wait_ge(consts_ready, 3)
                    pe.wait_ge(proj_out, A_SV + 8)
                for t in range(NT):
                    at = t * HEADS + 2 * j
                    ins = nc.tensor.matmul(psum[:, 2, at:at + 2], sqr[:, j % 2, t * P:(t + 1) * P], halves[:],
                                           start=True, stop=True)
                ins.then_inc(norm_part, 1)

            def beside(a):
                if a - A_SQ >= 1 and a < A_SK:
                    norm(a - A_SQ - 1)
                if a == A_SK:
                    norm(NC - 1)
                if a == A_SK + 1:
                    pe.wait_ge(norms_kept, 1)
                    for t in range(NT):
                        ins = nc.tensor.transpose(psum[0:HEADS, 3, t * P:(t + 1) * P],
                                                  tsc[:, t * HEADS:(t + 1) * HEADS], ident[:])
                    ins.then_inc(norms_turned, 1)

            def head_bank_free(a):
                if a < A_SQ + 2:
                    pe.wait_ge(proj_out, A_SV + 4)
                else:
                    pe.wait_ge(f_ready, a - A_SQ - 1)

            def head_scores(u):
                i, h = divmod(u, HEADS)
                half = slice(0, HD) if h % 2 == 0 else slice(HD, P)
                at = slice(i * P, (i + 1) * P)
                if i == 0:
                    pe.wait_ge(k_stacked, h // 2 + 1)
                    pe.wait_ge(proj_out, A_SK + h // 2 + 1)
                if u >= 3:
                    pe.wait_ge(hp_ready, u - 2)
                dst = psum[:, u % 3, :]
                nc.tensor.matmul(dst, qstack[:, h, at], kstack[:, h, :], start=True, stop=False)
                pe.wait_ge(flag_ready, u + 1)
                if u == 0:
                    pe.wait_ge(far_ready, 1)
                for lo, hi in ((0, i * P - P // 2), ((i + 1) * P + P // 2, T)):
                    if hi > lo:
                        nc.tensor.matmul(dst[:, lo:hi], flag[:, u % FLAGS, :], far[:, lo:hi], start=False, stop=False)
                nc.tensor.matmul(dst, qstack[half, h, at], klo[half, h // 2, :], start=False,
                                 stop=True).then_inc(hs_ready, 1)

            def first_scores(a):
                if a == A_SK + NC - 1:
                    for u in range(FIRST):
                        head_scores(u)

            for j in range(4):
                columns(SQ + j, (2 + j) % 4, A_SQ + 2 * j, head_bank_free, beside)
            for j in range(4):
                columns(SK + j, j % 2, A_SK + 2 * j, head_bank_free, beside, first_scores)

            def head_turn(u):
                pe.wait_ge(hp_ready, u + 1)
                if u >= 1:
                    pe.wait_ge(ht_out, u)
                for kt in range(4):
                    ins = nc.tensor.transpose(psum[:, 3, kt * P:(kt + 1) * P], hprob[u % 3][:, kt * P:(kt + 1) * P],
                                              ident[:])
                ins.then_inc(ht_full, 1)

            def head_values(u):
                i, h = divmod(u, HEADS)
                pe.wait_ge(ht_out, u + 1)
                if h == 0 and i >= 2:
                    pe.wait_ge(ho_taken, 2 * (i - 1))
                if h == 0 and i >= 3:
                    pe.wait_ge(mm_taken, i - 2)
                if h == 0 and i == 1:
                    pe.wait_ge(ssign_ready, 1)
                for kt in range(4):
                    ins = nc.tensor.matmul(psum[:, 4 + 2 * (i % 2) + h // 8, (h % 8) * HD:(h % 8 + 1) * HD],
                                           hpT[:, u % 2, kt * P:(kt + 1) * P], val[:, kt, h * HD:(h + 1) * HD],
                                           start=(kt == 0), stop=(kt == 3))
                ins.then_inc(ho_ready, 1)

            def mm_turn(i):
                pe.wait_ge(mm_ready, i + 1)
                pe.wait_ge(ho_taken, 2 * (i + 2) if i + 1 < NT else 2 * i)
                if i >= 2:
                    pe.wait_ge(mm_taken, i - 1)
                bank = psum[0:TILES, turn_bank(i), :]
                nc.tensor.transpose(bank[:, 0:P], onehot[:, i, :].bitcast(F32), ident[:])
                nc.tensor.transpose(bank[:, P:2 * P], mmx[:, 0, :], ident[:])
                nc.tensor.transpose(bank[:, 2 * P:3 * P], mmx[:, 1, :], ident[:]).then_inc(mm_full, 1)

            for u in range(NU + 3):
                if FIRST <= u < NU:
                    if u % HEADS == 6 and u >= 2 * HEADS:
                        mm_turn(u // HEADS - 2)
                    head_scores(u)
                if u == 6:
                    pe.wait_ge(spread_ready, 1)
                    pe.wait_ge(f_ready, 2 * NC)
                    for s in range(2):
                        ins = nc.tensor.matmul(psum[:, 6 + s, :], ones, spread[:, s * HALF:(s + 1) * HALF],
                                               start=True, stop=True)
                    ins.then_inc(ssign_full, 1)
                if 2 <= u <= NU + 1:
                    head_turn(u - 2)
                if u >= 3:
                    head_values(u - 3)
            pe.wait_ge(hp_ready, NU)
            pe.wait_ge(tables_full, 48)

            def pick_tables(i):
                pe.wait_ge(mm_taken, i + 1)
                nc.tensor.matmul(psum[:, i, :], ohT[:, i, :].bitcast(F32), tables[:].rearrange("p a n -> p (a n)"),
                                 start=True, stop=True).then_inc(rows_picked, 1)

            mm_turn(NT - 2)
            for i in range(NT - 1):
                pick_tables(i)
            mm_turn(NT - 1)
            pe.wait_ge(gath_ready, 1)
            for i in range(NT):
                nc.tensor.matmul(psum[:, 4, 4 * i:4 * i + 3], ohT[:, i, :].bitcast(F32), gath[:, 0:3], start=True,
                                 stop=True).then_inc(picked, 1)
            pe.wait_ge(ht_out, NU)
            pick_tables(NT - 1)


def bank_of(a):
    return 6 + a % 2


def turn_bank(i):
    return 4 + 2 * ((i + 1) % 2)


def kernel(**inputs):
    import numpy as np
    import concourse.bacc as bacc
    from concourse import mybir as mb
    from concourse.bass_utils import run_bass_kernel_spmd as run

    g = {k: np.asarray(v) for k, v in inputs.items()}

    def columns(w):
        return np.ascontiguousarray(w.reshape(8, 128, 4, 256).transpose(2, 1, 0, 3)).reshape(4, 128, 2048)

    def rows(w):
        return np.ascontiguousarray(w.reshape(2, 4, 128, 2, 512).transpose(3, 0, 2, 1, 4)).reshape(4, 128, 2048)

    c = g["ctx_2048"][0]
    arrays = {
        "x": g["x"][0],
        "keys": np.ascontiguousarray(c.reshape(16, 512, 2, 4, 128).transpose(0, 2, 4, 3, 1)).reshape(16, 2, 128, 2048),
        "values": np.ascontiguousarray(c.reshape(16, 2, 2, 128, 1024).transpose(0, 1, 3, 2, 4)).reshape(16, 2, 128, 2048),
        "wq": columns(g["L0_xattn_wq"].T), "wk": columns(g["L0_xattn_wk"].T),
        "wv": rows(g["L0_xattn_wv"].T), "wo": rows(g["L0_xattn_wo"].T),
        "sv": rows(g["L0_attn_Wv"]), "sq": columns(g["L0_attn_Wq"]), "sk": columns(g["L0_attn_Wk"]),
        "bq": np.ascontiguousarray(g["L0_attn_bq"].reshape(8, 128).T),
        "bk": np.ascontiguousarray(g["L0_attn_bk"].reshape(8, 128).T),
        "bv": g["L0_attn_bv"], "gamma": g["L0_ffn_ln_gamma"], "beta": g["L0_ffn_ln_beta"],
        "bases": g["L0_ffn_spline_bases"].reshape(64, 256), "slopes": g["L0_ffn_spline_slopes"].reshape(64, 256),
        "scale": g["L0_ffn_output_scale"].reshape(64, 1),
    }
    nc = bacc.Bacc("TRN2", target_bir_lowering=False, num_devices=1)
    feed, args = {}, []
    for name, a in arrays.items():
        a = np.ascontiguousarray(a)
        feed[f"in_{name}_dram"] = a
        args.append(nc.dram_tensor(f"in_{name}_dram", a.shape, mb.dt.from_np(a.dtype), kind="ExternalInput").ap())
    args.append(nc.dram_tensor("out_0_dram", (512, 1024), mb.dt.float32, kind="ExternalOutput").ap())
    program(nc, *args)
    r = run(nc, [feed], core_ids=[0])
    return r.results[0]["out_0_dram"].reshape(1, 512, 1024)
```
